# Optimizing a Trainium2 kernel written in Bass

```python
import numpy as np
import jax
import jax.numpy as jnp

def _softmax(x, axis=-1):
    return jax.nn.softmax(x, axis=axis)
def _gelu(x):
    return jax.nn.gelu(x, approximate=True)
def _silu(x):
    return jax.nn.silu(x)
def _sigmoid(x):
    return jax.nn.sigmoid(x)
def _layernorm(x, axis=-1, eps=1e-5):
    m = jnp.mean(x, axis=axis, keepdims=True)
    v = jnp.var(x, axis=axis, keepdims=True)
    return (x - m) / jnp.sqrt(v + eps)
def _scatter_add(tgt, idx, src, axis=0):
    return tgt.at[idx].add(src)
def _segment_sum(src, seg, n):
    return jax.ops.segment_sum(src, seg, n)

kernel_name = 'mk_conv_seq_d2_conv_nhwc512_17ea09'

def setup_inputs(seed: int = 0):
    np.random.seed(seed)
    _w = jnp.asarray
    def _rec_inputs():
        import jax
        import jax.numpy as jnp
        _gk = jax.random.key(seed)
        x = -0.0002928 + 1 * jax.random.normal(jax.random.fold_in(_gk, 1), (8, 32, 32, 512), jnp.float32)
        return x
    x = _rec_inputs()
    def _L0_conv_setup():
        import jax, jax.numpy as jnp
        import numpy as np
        import math
        B, H, W, C = (8, 32, 32, 512)
        NUM_HEAD_CHANNELS = 64
        NUM_HEADS = C // NUM_HEAD_CHANNELS
        HEAD_DIM = C // NUM_HEADS
        NUM_GROUPS = max(1, C // 16)
        EPS = 1e-06

        def _group_norm(x, scale, bias):
            b, h, w, c = x.shape
            xg = x.reshape(b, h * w, NUM_GROUPS, c // NUM_GROUPS)
            mu = jnp.mean(xg, axis=(1, 3), keepdims=True)
            var = jnp.var(xg, axis=(1, 3), keepdims=True)
            xn = (xg - mu) * jax.lax.rsqrt(var + EPS)
            return xn.reshape(b, h, w, c) * scale + bias
        key = jax.random.key(seed)
        ks = jax.random.split(key, 7)
        s = lambda fan: 1.0 / math.sqrt(fan)
        return {'x': jax.random.normal(ks[0], (B, H, W, C), jnp.float32), 'gn_scale': jnp.ones((C,), jnp.float32), 'gn_bias': jnp.zeros((C,), jnp.float32), 'w_qkv': jax.random.normal(ks[1], (C, 3 * C), jnp.float32) * s(C), 'b_qkv': jnp.zeros((3 * C,), jnp.float32), 'w_out': jax.random.normal(ks[2], (C, C), jnp.float32) * s(C), 'b_out': jnp.zeros((C,), jnp.float32)}
    _L0_conv_all = _L0_conv_setup()
    _L0_conv_in = {k: v for k, v in _L0_conv_all.items() if k in ('gn_scale', 'gn_bias', 'w_qkv', 'b_qkv', 'w_out', 'b_out', )}
    del _L0_conv_all

    def _L1_conv_setup():
        import jax, jax.numpy as jnp
        import numpy as np
        B, H, W, C = (4, 64, 64, 512)
        R, NH, KS = (2, 8, 7)
        S = 1.0

        def layernorm(t, g, b):
            m = t.mean(-1, keepdims=True)
            v = ((t - m) ** 2).mean(-1, keepdims=True)
            return (t - m) / jnp.sqrt(v + 1e-05) * g + b

        def grid_sample_bilinear_zeros(img, grid):
            b, c, h, w = img.shape
            gh, gw = (grid.shape[1], grid.shape[2])
            x = (grid[..., 0] + 1.0) * 0.5 * (w - 1)
            y = (grid[..., 1] + 1.0) * 0.5 * (h - 1)
            x0 = jnp.floor(x)
            y0 = jnp.floor(y)
            wx1 = x - x0
            wy1 = y - y0
            x0i = x0.astype(jnp.int32)
            y0i = y0.astype(jnp.int32)
            flat = img.reshape(b, c, h * w)

            def corner(xi, yi, wt):
                valid = ((xi >= 0) & (xi < w) & (yi >= 0) & (yi < h)).astype(img.dtype)
                idx = jnp.clip(yi, 0, h - 1) * w + jnp.clip(xi, 0, w - 1)
                vals = jnp.take_along_axis(flat, idx.reshape(b, 1, gh * gw), axis=2)
                return vals * (valid * wt).reshape(b, 1, gh * gw)
            out = corner(x0i, y0i, (1 - wx1) * (1 - wy1)) + corner(x0i + 1, y0i, wx1 * (1 - wy1)) + corner(x0i, y0i + 1, (1 - wx1) * wy1) + corner(x0i + 1, y0i + 1, wx1 * wy1)
            return out.reshape(b, c, gh, gw)
        key = jax.random.key(seed)
        ks = jax.random.split(key, 12)
        sd = 0.02
        f32 = jnp.float32
        return {'x': jax.random.normal(ks[0], (B, H, W, C), f32), 'ln_g': jnp.ones((C,), f32), 'ln_b': jnp.zeros((C,), f32), 'wq': jax.random.normal(ks[1], (C, C), f32) * sd, 'bq': jnp.zeros((C,), f32), 'wv': jax.random.normal(ks[2], (C, C), f32) * sd, 'bv': jnp.zeros((C,), f32), 'dw_w': jax.random.normal(ks[3], (C, 1, KS, KS), f32) * sd, 'dw_b': jnp.zeros((C,), f32), 'pw_w': jax.random.normal(ks[4], (2, C, 1, 1), f32) * sd, 'mq_w': jax.random.normal(ks[5], (C, C), f32) * sd, 'mq_b': jnp.zeros((C,), f32), 'mk_w': jax.random.normal(ks[6], (C, C), f32) * sd, 'mk_b': jnp.zeros((C,), f32), 'mv_w': jax.random.normal(ks[7], (C, C), f32) * sd, 'mv_b': jnp.zeros((C,), f32), 'mo_w': jax.random.normal(ks[8], (C, C), f32) * sd, 'mo_b': jnp.zeros((C,), f32), 'mlp_w': jax.random.normal(ks[9], (C, C), f32) * sd, 'mlp_b': jnp.zeros((C,), f32)}
    _L1_conv_all = _L1_conv_setup()
    _L1_conv_in = {k: v for k, v in _L1_conv_all.items() if k in ('ln_g', 'ln_b', 'wq', 'bq', 'wv', 'bv', 'dw_w', 'dw_b', 'pw_w', 'mq_w', 'mq_b', 'mk_w', 'mk_b', 'mv_w', 'mv_b', 'mo_w', 'mo_b', 'mlp_w', 'mlp_b', )}
    del _L1_conv_all

    return {
        "x": x,
        "L0_conv_gn_scale": _L0_conv_in["gn_scale"],
        "L0_conv_gn_bias": _L0_conv_in["gn_bias"],
        "L0_conv_w_qkv": _L0_conv_in["w_qkv"],
        "L0_conv_b_qkv": _L0_conv_in["b_qkv"],
        "L0_conv_w_out": _L0_conv_in["w_out"],
        "L0_conv_b_out": _L0_conv_in["b_out"],
        "L1_conv_ln_g": _L1_conv_in["ln_g"],
        "L1_conv_ln_b": _L1_conv_in["ln_b"],
        "L1_conv_wq": _L1_conv_in["wq"],
        "L1_conv_bq": _L1_conv_in["bq"],
        "L1_conv_wv": _L1_conv_in["wv"],
        "L1_conv_bv": _L1_conv_in["bv"],
        "L1_conv_dw_w": _L1_conv_in["dw_w"],
        "L1_conv_dw_b": _L1_conv_in["dw_b"],
        "L1_conv_pw_w": _L1_conv_in["pw_w"],
        "L1_conv_mq_w": _L1_conv_in["mq_w"],
        "L1_conv_mq_b": _L1_conv_in["mq_b"],
        "L1_conv_mk_w": _L1_conv_in["mk_w"],
        "L1_conv_mk_b": _L1_conv_in["mk_b"],
        "L1_conv_mv_w": _L1_conv_in["mv_w"],
        "L1_conv_mv_b": _L1_conv_in["mv_b"],
        "L1_conv_mo_w": _L1_conv_in["mo_w"],
        "L1_conv_mo_b": _L1_conv_in["mo_b"],
        "L1_conv_mlp_w": _L1_conv_in["mlp_w"],
        "L1_conv_mlp_b": _L1_conv_in["mlp_b"],
    }

def reference(x, L0_conv_gn_scale, L0_conv_gn_bias, L0_conv_w_qkv, L0_conv_b_qkv, L0_conv_w_out, L0_conv_b_out, L1_conv_ln_g, L1_conv_ln_b, L1_conv_wq, L1_conv_bq, L1_conv_wv, L1_conv_bv, L1_conv_dw_w, L1_conv_dw_b, L1_conv_pw_w, L1_conv_mq_w, L1_conv_mq_b, L1_conv_mk_w, L1_conv_mk_b, L1_conv_mv_w, L1_conv_mv_b, L1_conv_mo_w, L1_conv_mo_b, L1_conv_mlp_w, L1_conv_mlp_b):
    import jax
    import jax.numpy as jnp
    def _L0_conv_ref(x, gn_scale, gn_bias, w_qkv, b_qkv, w_out, b_out):
        import jax, jax.numpy as jnp
        import numpy as np
        import math
        B, H, W, C = (8, 32, 32, 512)
        NUM_HEAD_CHANNELS = 64
        NUM_HEADS = C // NUM_HEAD_CHANNELS
        HEAD_DIM = C // NUM_HEADS
        NUM_GROUPS = max(1, C // 16)
        EPS = 1e-06

        def _group_norm(x, scale, bias):
            b, h, w, c = x.shape
            xg = x.reshape(b, h * w, NUM_GROUPS, c // NUM_GROUPS)
            mu = jnp.mean(xg, axis=(1, 3), keepdims=True)
            var = jnp.var(xg, axis=(1, 3), keepdims=True)
            xn = (xg - mu) * jax.lax.rsqrt(var + EPS)
            return xn.reshape(b, h, w, c) * scale + bias
        b, h, w, c = x.shape
        seq = h * w
        x_flat = x.reshape(b, seq, c)
        x_norm = _group_norm(x, gn_scale, gn_bias).reshape(b, seq, c)
        qkv = x_norm @ w_qkv + b_qkv
        q, k, v = jnp.split(qkv, 3, axis=-1)
        scale = 1.0 / math.sqrt(HEAD_DIM)

        def to_heads(t):
            return t.reshape(b, seq, NUM_HEADS, HEAD_DIM).transpose(0, 2, 1, 3)
        q, k, v = (to_heads(q), to_heads(k), to_heads(v))
        weight = jnp.einsum('bhld,bhsd->bhls', q * scale, k * scale)
        weight = jax.nn.softmax(weight, axis=-1)
        out = jnp.einsum('bhls,bhsd->bhld', weight, v)
        out = out.transpose(0, 2, 1, 3).reshape(b, seq, c)
        out = out @ w_out + b_out
        return (x_flat + out).reshape(b, h, w, c)

    def _L1_conv_ref(x, ln_g, ln_b, wq, bq, wv, bv, dw_w, dw_b, pw_w, mq_w, mq_b, mk_w, mk_b, mv_w, mv_b, mo_w, mo_b, mlp_w, mlp_b):
        import jax, jax.numpy as jnp
        import numpy as np
        B, H, W, C = (4, 64, 64, 512)
        R, NH, KS = (2, 8, 7)
        S = 1.0

        def layernorm(t, g, b):
            m = t.mean(-1, keepdims=True)
            v = ((t - m) ** 2).mean(-1, keepdims=True)
            return (t - m) / jnp.sqrt(v + 1e-05) * g + b

        def grid_sample_bilinear_zeros(img, grid):
            b, c, h, w = img.shape
            gh, gw = (grid.shape[1], grid.shape[2])
            x = (grid[..., 0] + 1.0) * 0.5 * (w - 1)
            y = (grid[..., 1] + 1.0) * 0.5 * (h - 1)
            x0 = jnp.floor(x)
            y0 = jnp.floor(y)
            wx1 = x - x0
            wy1 = y - y0
            x0i = x0.astype(jnp.int32)
            y0i = y0.astype(jnp.int32)
            flat = img.reshape(b, c, h * w)

            def corner(xi, yi, wt):
                valid = ((xi >= 0) & (xi < w) & (yi >= 0) & (yi < h)).astype(img.dtype)
                idx = jnp.clip(yi, 0, h - 1) * w + jnp.clip(xi, 0, w - 1)
                vals = jnp.take_along_axis(flat, idx.reshape(b, 1, gh * gw), axis=2)
                return vals * (valid * wt).reshape(b, 1, gh * gw)
            out = corner(x0i, y0i, (1 - wx1) * (1 - wy1)) + corner(x0i + 1, y0i, wx1 * (1 - wy1)) + corner(x0i, y0i + 1, (1 - wx1) * wy1) + corner(x0i + 1, y0i + 1, wx1 * wy1)
            return out.reshape(b, c, gh, gw)
        b, h, w, c = x.shape
        x_ln = layernorm(x, ln_g, ln_b).transpose(0, 3, 1, 2)
        x_flat = x_ln.reshape(b, h * w, c)
        q = x_flat @ wq + bq
        q_img = q.reshape(b, c, h, w)
        o = jax.lax.conv_general_dilated(q_img, dw_w, (R, R), [(KS // 2, KS // 2)] * 2, dimension_numbers=('NCHW', 'OIHW', 'NCHW'), feature_group_count=c)
        o = jax.nn.gelu(o + dw_b[None, :, None, None], approximate=False)
        offsets = jax.lax.conv_general_dilated(o, pw_w, (1, 1), [(0, 0), (0, 0)], dimension_numbers=('NCHW', 'OIHW', 'NCHW'))
        hg, wg = (offsets.shape[2], offsets.shape[3])
        ref_x = (jnp.arange(wg, dtype=x.dtype) + 0.5) * (2.0 / wg) - 1.0
        ref_y = (jnp.arange(hg, dtype=x.dtype) + 0.5) * (2.0 / hg) - 1.0
        gx, gy = jnp.meshgrid(ref_x, ref_y, indexing='ij')
        refs = jnp.stack([gx, gy], axis=0)
        deformed = refs[None] + S * jnp.tanh(offsets)
        deformed = (deformed + 1.0) * (h / R) / 2.0
        grid = deformed[:, ::-1].transpose(0, 2, 3, 1)
        interp = grid_sample_bilinear_zeros(x.transpose(0, 3, 1, 2), grid)
        interp_flat = interp.reshape(b, hg * wg, c)
        v = interp_flat @ wv + bv
        k = interp_flat @ wv + bv
        hd = c // NH

        def heads(t):
            return t.reshape(b, -1, NH, hd).transpose(0, 2, 1, 3)
        qh = heads(q @ mq_w + mq_b)
        kh = heads(k @ mk_w + mk_b)
        vh = heads(v @ mv_w + mv_b)
        attn = jax.nn.softmax(jnp.einsum('bnqd,bnkd->bnqk', qh, kh), axis=-1)
        att = jnp.einsum('bnqk,bnkd->bnqd', attn, vh).transpose(0, 2, 1, 3).reshape(b, h * w, c)
        msa = att @ mo_w + mo_b
        z = msa + x.reshape(b, h * w, c)
        z_ln = layernorm(z, ln_g, ln_b)
        out = jax.nn.gelu(z_ln @ mlp_w + mlp_b, approximate=False) + z
        return out.reshape(b, w, h, c)

    def _gn(v, G=32, eps=1e-5):
        B_, H_, W_, C_ = v.shape
        g = v.reshape(B_, H_, W_, G, C_ // G)
        m = jnp.mean(g, axis=(1, 2, 4), keepdims=True)
        s = jnp.var(g, axis=(1, 2, 4), keepdims=True)
        return ((g - m) / jnp.sqrt(s + eps)).reshape(v.shape)

    def _ln_c(v, eps=1e-6):
        m = jnp.mean(v, axis=-1, keepdims=True)
        s = jnp.var(v, axis=-1, keepdims=True)
        return (v - m) / jnp.sqrt(s + eps)

    def _ln_t(v, eps=1e-5):
        m = jnp.mean(v, axis=-1, keepdims=True)
        s = jnp.var(v, axis=-1, keepdims=True)
        return (v - m) / jnp.sqrt(s + eps)

    def _to_tokens(v):
        B_, H_, W_, C_ = v.shape
        return v.reshape(B_, H_ * W_, C_)
    def _from_tokens(t, like):
        return t.reshape(like.shape)

    x = _L0_conv_ref(x, L0_conv_gn_scale, L0_conv_gn_bias, L0_conv_w_qkv, L0_conv_b_qkv, L0_conv_w_out, L0_conv_b_out)
    x = _L1_conv_ref(x, L1_conv_ln_g, L1_conv_ln_b, L1_conv_wq, L1_conv_bq, L1_conv_wv, L1_conv_bv, L1_conv_dw_w, L1_conv_dw_b, L1_conv_pw_w, L1_conv_mq_w, L1_conv_mq_b, L1_conv_mk_w, L1_conv_mk_b, L1_conv_mv_w, L1_conv_mv_b, L1_conv_mo_w, L1_conv_mo_b, L1_conv_mlp_w, L1_conv_mlp_b)
    return x


_drawn_inputs = setup_inputs


def setup_inputs(seed=0):
    import zlib

    import numpy as np

    out = dict(_drawn_inputs(seed))
    spreads = {'L0_conv_gn_scale': (1.0, 0.6),
     'L0_conv_gn_bias': (0.0, 0.1),
     'L0_conv_b_qkv': (0.0, 0.1),
     'L0_conv_b_out': (0.0, 0.1),
     'L1_conv_ln_g': (1.0, 0.2),
     'L1_conv_ln_b': (0.0, 0.3),
     'L1_conv_bq': (0.0, 0.8),
     'L1_conv_bv': (0.0, 0.398),
     'L1_conv_dw_b': (0.0, 0.8),
     'L1_conv_mq_b': (0.0, 0.8),
     'L1_conv_mk_b': (0.0, 0.8),
     'L1_conv_mv_b': (0.0, 0.1),
     'L1_conv_mo_b': (0.0, 0.1),
     'L1_conv_mlp_b': (0.0, 0.1)}
    factors = {'L1_conv_wq': 8.0,
     'L1_conv_wv': 8.0,
     'L1_conv_dw_w': 8.0,
     'L1_conv_pw_w': 8.0,
     'L1_conv_mq_w': 8.0,
     'L1_conv_mk_w': 8.0}
    for name, (base, spread) in spreads.items():
        noise = np.random.default_rng([zlib.crc32(name.encode()), seed]).standard_normal(out[name].shape)
        drawn = base * np.exp(spread * noise) if base else spread * noise
        out[name] = jnp.asarray(drawn.astype(out[name].dtype))
    for name, factor in factors.items():
        out[name] = (out[name] * factor).astype(out[name].dtype)
    return out
```

```python
from contextlib import ExitStack

import concourse.bass as bass
from concourse import mybir

F32 = mybir.dt.float32
F32R = mybir.dt.float32r
ACT = mybir.ActivationFunctionType
ALU = mybir.AluOpType
AX = mybir.AxisListType.X

P = 128
B = 8
TOK = 1024
C = 512
CT = C // P
TT = TOK // P
NH = 8
HD = C // NH
HALF = TOK // 2
HW = 32
GRID = 16
NS = GRID * GRID
KS = 7
PADW = HW + KS - 1
SB_START = 16512
SB_END = 229344


class Region:

    def __init__(self, nc, start, end):
        self.nc, self.at, self.end = nc, start, end

    def take(self, name, shape, dt=F32):
        size = 4
        for n in shape[1:]:
            size *= n
        size = (size + 31) // 32 * 32
        assert self.at + size <= self.end, (name, self.at + size - self.end)
        t = self.nc.alloc_sbuf_tensor_at(name, shape, dt, offset=self.at)
        self.at += size
        return t


def raw(ap):
    return ap.bitcast(F32)


def own_half(h):
    return slice(HD * (h % 2), HD * (h % 2) + HD)


def other_half(h):
    return slice(HD * (1 - h % 2), HD * (1 - h % 2) + HD)


def v_hi(tile):
    return tile.rearrange("p (q f d) -> p q f d", q=NH // 2, f=4)[:, :, 0:4:3, :]


def v_lo(tile):
    return tile.rearrange("p (q f d) -> p q f d", q=NH // 2, f=4)[:, :, 1:3, :]


def by_head(ap):
    return ap.rearrange("p (q e d) -> p q e d", q=NH // 2, e=2)


def make_identity(pool, ident, done):
    pool.memset(ident[:], 0.0).then_inc(done, 1)
    pool.wait_ge(done, 1)
    pool.affine_select(out=ident[:], in_=ident[:], compare_op=ALU.not_equal, fill=1.0, base=0,
                       pattern=[[-1, P]], channel_multiplier=1).then_inc(done, 1)


def layer0(nc, x, gn_scale, gn_bias, w_qkv, b_qkv, w_out, b_out, x2, n_images=B):
    NB = TOK // 256
    U = NH * TT
    QSCALE = 1.0 / HD

    with ExitStack() as ctx:
        def sem(name):
            return ctx.enter_context(nc.semaphore("a_" + name))

        ps = ctx.enter_context(nc.psum_tensor("a_ps", [P, 8, 512], F32))
        R = Region(nc, SB_START, SB_END)
        wqh = R.take("wqkv_hi", [P, CT, 3 * C], F32R)
        wql = R.take("wqkv_lo", [P, CT, 3 * C], F32R)
        woh = R.take("wout_hi", [P, CT, C], F32R)
        wol = R.take("wout_lo", [P, CT, C], F32R)
        ident = R.take("a_ident", [P, P])
        group = R.take("a_group", [P, P])
        bout = R.take("a_bout", [P, C])
        vec = R.take("a_vec", [P, 20])
        bq = R.take("a_bq", [P, CT])
        neg_half = R.take("a_neg_half", [P, CT])
        small = R.take("a_small", [P, 40])
        bn = R.take("a_bn", [P, CT, 2, 6])
        neg_max = R.take("a_neg_max", [P, U])
        row_sum = R.take("a_row_sum", [P, U])
        row_inv = R.take("a_row_inv", [P, U])
        tok = R.take("a_tok", [P, 3, C])
        fold_t = R.take("a_fold_t", [P, 256])
        fold_r = R.take("a_fold_r", [P, 2, 256])
        fold_s = R.take("a_fold_s", [P, 2, 256])
        qk = R.take("a_qk", [P, 2 * CT, TOK])
        v = R.take("a_v", [P, TT, NH * P], F32R)
        qs = R.take("a_qs", [P, 2, TOK], F32R)
        kh = R.take("a_kh", [P, 2, TOK], F32R)
        kl = R.take("a_kl", [P, 2, TOK], F32R)
        work = R.at
        prob = R.take("a_prob", [P, 2, TOK])
        split = R.at
        ph = R.take("a_ph", [P, 2, TT, 256], F32R)
        pl = R.take("a_pl", [P, 2, TT, 256], F32R)
        S = Region(nc, split, SB_END)
        xh = S.take("a_xh", [P, CT, TOK], F32R)
        xl = S.take("a_xl", [P, CT, TOK], F32R)
        xt = Region(nc, work - 16384 - 8192, SB_END).take("a_xt", [P, CT, TOK])
        W = Region(nc, work - 60000 // 32 * 32, SB_END)
        wq_raw = W.take("a_wq_raw", [P, CT, 3 * C])
        wo_raw = W.take("a_wo_raw", [P, CT, C])
        rows = W.take("a_rows", [20, P])
        bo_raw = W.take("a_bo_raw", [P, C])
        bv_wide = W.take("a_bv_wide", [P, CT, P])

        ld, cst, spl, pe_s, chn = sem("s_ld"), sem("s_cst"), sem("s_spl"), sem("s_pe"), sem("s_chn")
        with nc.Block() as block:
            @block.sync
            def _(sp):
                sp.dma_start(wq_raw[:], w_qkv.rearrange("(t p) n -> p t n", p=P)).then_inc(ld, 16)
                sp.dma_start(wo_raw[:], w_out.rearrange("(t p) n -> p t n", p=P)).then_inc(ld, 16)
                sp.dma_start(rows[0:4, :], gn_scale.rearrange("(t p) -> t p", p=P)).then_inc(ld, 16)
                sp.dma_start(rows[4:8, :], gn_bias.rearrange("(t p) -> t p", p=P)).then_inc(ld, 16)
                sp.dma_start(rows[8:20, :], b_qkv.rearrange("(t p) -> t p", p=P)).then_inc(ld, 16)
                sp.dma_start(bo_raw[:], b_out.partition_broadcast(P)).then_inc(ld, 16)

            @block.gpsimd
            def _(pool):
                make_identity(pool, ident, cst)
                pool.memset(group[:], 1.0 / 16).then_inc(cst, 1)
                pool.memset(neg_half[:], -0.5).then_inc(cst, 1)
                blocks = group[:].rearrange("p (g j) -> p g j", j=16)
                pool.wait_ge(cst, 3)
                pool.affine_select(out=blocks, in_=blocks, compare_op=ALU.is_ge, fill=0.0, base=0,
                                   pattern=[[-16, 8], [0, 16]], channel_multiplier=1).then_inc(cst, 1)
                pool.wait_ge(cst, 5)
                pool.affine_select(out=blocks, in_=blocks, compare_op=ALU.is_ge, fill=0.0, base=15,
                                   pattern=[[16, 8], [0, 16]], channel_multiplier=-1).then_inc(cst, 1)

            @block.scalar
            def _(act):
                act.wait_ge(ld, 96)
                act.activation(wqh[:], wq_raw[:], ACT.Copy).then_inc(spl, 1)
                act.activation(woh[:], wo_raw[:], ACT.Copy).then_inc(spl, 1)

            @block.tensor
            def _(pe):
                pe.wait_ge(ld, 96)
                pe.wait_ge(cst, 2)
                pe.transpose(ps[:, 0, 0:20], rows[:], ident[0:20, 0:20]).then_inc(pe_s, 1)
                pe.wait_ge(chn, 3)
                for k in range(CT):
                    mm = pe.matmul(ps[:, 1, :], bv_wide[:, k, :], wo_raw[:, k, :], start=k == 0, stop=k == CT - 1)
                mm.then_inc(pe_s, 1)

            @block.vector
            def _(dve):
                dve.wait_ge(pe_s, 1)
                dve.tensor_copy(vec[:], ps[:, 0, 0:20]).then_inc(chn, 1)
                dve.wait_ge(chn, 1)
                dve.tensor_scalar(bq[:], vec[:, 8:12], QSCALE, None, ALU.mult).then_inc(chn, 1)
                dve.tensor_copy(bv_wide[:], vec[:, 16:20].unsqueeze(2).to_broadcast([P, CT, P])).then_inc(chn, 1)
                dve.wait_ge(spl, 1)
                dve.tensor_tensor(wql[:], wq_raw[:], raw(wqh[:]), ALU.subtract).then_inc(chn, 1)
                dve.wait_ge(spl, 2)
                dve.tensor_tensor(wol[:], wo_raw[:], raw(woh[:]), ALU.subtract).then_inc(chn, 1)
                dve.wait_ge(pe_s, 2)
                dve.tensor_tensor(bout[:], ps[:, 1, :], bo_raw[:], ALU.add).then_inc(chn, 1)

        x_ld = [sem(f"x_ld{i}") for i in range(3)]
        r_ld = [sem(f"r_ld{i}") for i in range(3)]
        o_st = [sem(f"o_st{i}") for i in range(3)]
        s_ld = [sem(f"s_ld{i}") for i in range(2)]
        xt_ps, xt_sb, bn_ok, bn_ag = sem("xt_ps"), sem("xt_sb"), sem("bn_ok"), sem("bn_ag")
        st_ok, st_ps, var_ok, rstd_ok = sem("st_ok"), sem("st_ps"), sem("var_ok"), sem("rstd_ok")
        chain = sem("chain")
        xn_ok, xh_ok, xl_ok = sem("xn_ok"), sem("xh_ok"), sem("xl_ok")
        pr_ps, qk_sb, vh_ok, vl_ok = sem("pr_ps"), sem("qk_sb"), sem("vh_ok"), sem("vl_ok")
        staged, score, max_ok, exp_ok = sem("staged"), sem("score"), sem("max_ok"), sem("exp_ok")
        tr_ps, ph_ok, pl_ok, inv_ok = sem("tr_ps"), sem("ph_ok"), sem("pl_ok"), sem("inv_ok")
        av_ps, fold_cp, fold_add, att_ok = sem("av_ps"), sem("fold_cp"), sem("fold_add"), sem("att_ok")
        ah_ok, al_ok, out_ps, res_ok, out_ok = sem("ah_ok"), sem("al_ok"), sem("out_ps"), sem("res_ok"), sem("out_ok")
        cleared = [*x_ld, *r_ld, *o_st, *s_ld, xt_ps, xt_sb, bn_ok, bn_ag, st_ok, st_ps, var_ok, rstd_ok, chain,
                   xn_ok, xh_ok, xl_ok, pr_ps, qk_sb, vh_ok, vl_ok, staged, score, max_ok, exp_ok, tr_ps, ph_ok,
                   pl_ok, inv_ok, av_ps, fold_cp, fold_add, att_ok, ah_ok, al_ok, out_ps, res_ok, out_ok]
        nums = [s.num for s in cleared]
        assert sorted(nums) == list(range(min(nums), max(nums) + 1))

        groups = [("qk", m, s) for m in (0, 4) for s in range(2)] + [("v", t, 0) for t in range(TT)]
        groups += [("qk", m, s) for m in (1, 5, 2, 6, 3, 7) for s in range(2)]
        qk_upto = [sum(g[0] == "qk" for g in groups[:n]) for n in range(len(groups) + 1)]
        v_upto = [sum(g[0] == "v" for g in groups[:n]) for n in range(len(groups) + 1)]
        n_qk, n_v = qk_upto[-1], v_upto[-1]
        STAGE = 5

        def image(i):
            with nc.Block() as block:
                @block.sync
                def _(sp):
                    for t in range(TT):
                        if t >= 3:
                            sp.wait_ge(xt_ps, t - 2)
                        sp.dma_start(tok[:, t % 3, :], x[i, t * P:(t + 1) * P, :]).then_inc(x_ld[t % 3], 16)
                    for h in range(NH):
                        p, j = h // 2, h % 2
                        sp.wait_ge(qk_sb, 4 if p == 0 else 4 + 4 * p)
                        if h >= 2:
                            sp.wait_ge(score, TT * (h - 1))
                        else:
                            sp.wait_ge(xl_ok, CT)
                        for half in range(2):
                            rows_ = slice(HD * half, HD * half + HD)
                            sp.dma_start(raw(qs[rows_, j, :]), qk[own_half(h), p, :]).then_inc(s_ld[j], 16)
                            sp.dma_start(raw(kl[rows_, j, :]), qk[own_half(h), CT + p, :]).then_inc(s_ld[j], 16)
                        if h == 1:
                            sp.wait_ge(xt_ps, TT)
                            for t in range(3):
                                sp.dma_start(tok[:, t, :], x[i, t * P:(t + 1) * P, :]).then_inc(r_ld[t], 16)
                    for t in range(TT):
                        sp.wait_ge(out_ok, t + 1)
                        sp.dma_start(x2[i, t * P:(t + 1) * P, :], tok[:, t % 3, :]).then_inc(o_st[t % 3], 16)
                        if t + 3 < TT:
                            sp.wait_ge(o_st[t % 3], 16 * (t // 3 + 1))
                            sp.dma_start(tok[:, t % 3, :], x[i, (t + 3) * P:(t + 4) * P, :])\
                                .then_inc(r_ld[t % 3], 16)
                    for t in range(3):
                        sp.wait_ge(o_st[t], 16 * ((TT - t + 2) // 3))

                @block.tensor
                def _(pe):
                    for t in range(TT):
                        pe.wait_ge(x_ld[t % 3], 16 * (t // 3 + 1))
                        for c in range(CT):
                            mm = pe.transpose(ps[:, 4 * (t // 4) + c, (t % 4) * P:(t % 4 + 1) * P],
                                              tok[:, t % 3, c * P:(c + 1) * P], ident[:])
                        mm.then_inc(xt_ps, 1)
                    pe.wait_ge(st_ok, 2)
                    pe.wait_ge(xt_sb, 2 * CT)
                    pe.matmul(ps[:, 7, 0:8], group[:], small[:, 0:8], start=True, stop=True).then_inc(st_ps, 1)

                    pe.wait_ge(xh_ok, CT)
                    pe.wait_ge(xl_ok, CT)
                    for g, (kind, m, s) in enumerate(groups):
                        if g >= 8:
                            pe.wait_ge(qk_sb, qk_upto[g - 7])
                            if v_upto[g - 7]:
                                pe.wait_ge(vl_ok, v_upto[g - 7])
                        bank = ps[:, g % 8, :]
                        for k in range(CT):
                            if kind == "qk":
                                w = slice(m * P, (m + 1) * P)
                                n = slice(s * HALF, (s + 1) * HALF)
                                pairs = ((wqh[:, k, w], xh[:, k, n]), (wqh[:, k, w], xl[:, k, n]),
                                         (wql[:, k, w], xh[:, k, n]))
                            else:
                                w = slice(2 * C, 3 * C)
                                n = slice(m * P, (m + 1) * P)
                                pairs = ((xh[:, k, n], wqh[:, k, w]), (xh[:, k, n], wql[:, k, w]),
                                         (xl[:, k, n], wqh[:, k, w]))
                            for e, (a, b) in enumerate(pairs):
                                mm = pe.matmul(bank, a, b, start=k == 0 and e == 0, stop=k == CT - 1 and e == 2)
                        mm.then_inc(pr_ps, 1)

                    pe.wait_ge(qk_sb, n_qk)
                    pe.wait_ge(vl_ok, n_v)
                    for i_ in range(U + 7):
                        if i_ >= 5:
                            b, part = (i_ - 5) // 2, (i_ - 5) % 2
                            if b < U // 2:
                                h = b // NB
                                if part == 0:
                                    pe.wait_ge(inv_ok, b + 1)
                                    if b >= 2:
                                        pe.wait_ge(fold_add, b - 1)
                                        pe.wait_ge(fold_cp, 2 * b - 2)
                                    for n in range(2):
                                        u = 2 * b + n
                                        pe.transpose(ps[:, 6 + b % 2, 256 + n * P:256 + (n + 1) * P],
                                                     row_inv[:, u:u + 1].to_broadcast([P, P]), ident[:])
                                pe.wait_ge(pl_ok, 4 * b + 3 + part)
                                for kt in range(4 * part, 4 * part + 4):
                                    for e, q_ in enumerate((ph, pl)):
                                        mm = pe.matmul(ps[:, 6 + b % 2, 0:256], v[:, kt, h * P:(h + 1) * P], q_[:, b % 2, kt, :],
                                                       start=kt == 0 and e == 0, stop=kt == TT - 1 and e == 1)
                                if part == 1:
                                    mm.then_inc(av_ps, 1)
                        if i_ < U:
                            h, t = i_ // TT, i_ % TT
                            j = h % 2
                            if t == 0:
                                pe.wait_ge(staged, STAGE * (h + 1))
                            if i_ >= 2:
                                pe.wait_ge(exp_ok, i_ - 1)
                            for kb in range(2):
                                bank = ps[:, 2 * (i_ % 2) + kb, :]
                                q_ = qs[:, j, t * P:(t + 1) * P]
                                n = slice(kb * 512, (kb + 1) * 512)
                                pe.matmul(bank, q_, kh[:, j, n], start=True, stop=False)
                                mm = pe.matmul(bank, q_, kl[:, j, n], start=False, stop=True)
                            mm.then_inc(score, 1)
                        if 2 <= i_ < U + 2:
                            u = i_ - 2
                            pe.wait_ge(exp_ok, u + 1)
                            for g in range(2):
                                n = 2 * u + g
                                if n >= 2:
                                    pe.wait_ge(pl_ok, n - 1)
                                for kk in range(4):
                                    kt = 4 * g + kk
                                    mm = pe.transpose(ps[:, 4 + n % 2, kk * P:(kk + 1) * P],
                                                      prob[:, u % 2, kt * P:(kt + 1) * P], ident[:])
                                mm.then_inc(tr_ps, 1)

                    pe.wait_ge(fold_add, U // 2)
                    pe.wait_ge(fold_cp, U)
                    for t in range(TT):
                        if t == 0:
                            pe.wait_ge(ah_ok, CT)
                            pe.wait_ge(al_ok, CT)
                        n = slice(t * P, (t + 1) * P)
                        for k in range(CT):
                            for e, (a, b) in enumerate(((xh[:, k, n], woh[:, k, :]), (xh[:, k, n], wol[:, k, :]),
                                                        (xl[:, k, n], woh[:, k, :]))):
                                mm = pe.matmul(ps[:, t, :], a, b, start=k == 0 and e == 0, stop=k == CT - 1 and e == 2)
                        mm.then_inc(out_ps, 1)

                @block.scalar
                def _(act):
                    for s in range(2):
                        act.wait_ge(xt_ps, 4 * s + 4)
                        for c in range(CT):
                            act.activation(xt[:, c, s * HALF:(s + 1) * HALF], ps[:, 4 * s + c, :], ACT.Copy)\
                                .then_inc(xt_sb, 1)
                    for c in range(CT):
                        act.wait_ge(xn_ok, c + 1)
                        act.activation(xh[:, c, :], xt[:, c, :], ACT.Copy).then_inc(xh_ok, 1)
                    for g, (kind, m, s) in enumerate(groups):
                        act.wait_ge(pr_ps, g + 1)
                        if kind == "v":
                            act.activation(v_hi(v[:, m, :]), by_head(ps[:, g % 8, :]), ACT.Copy).then_inc(vh_ok, 1)
                        elif m < CT:
                            act.activation(qk[:, m, s * HALF:(s + 1) * HALF], ps[:, g % 8, :], ACT.Identity,
                                           bias=bq[:, m:m + 1], scale=QSCALE).then_inc(qk_sb, 1)
                        else:
                            act.activation(qk[:, m, s * HALF:(s + 1) * HALF], ps[:, g % 8, :], ACT.Identity,
                                           bias=vec[:, 8 + m:9 + m]).then_inc(qk_sb, 1)
                    for i_ in range(U + 7):
                        if 6 <= i_ <= U + 4 and i_ % 2 == 0:
                            b = (i_ - 6) // 2
                            h = b // NB
                            act.wait_ge(av_ps, b + 1)
                            if b >= 1:
                                act.wait_ge(fold_add, b)
                            act.activation(fold_t[own_half(h), :], ps[other_half(h), 6 + b % 2, 0:256], ACT.Copy)\
                                .then_inc(fold_cp, 1)
                            if b >= 2:
                                act.wait_ge(att_ok, b - 1)
                            act.activation(fold_r[own_half(h), b % 2, :], ps[own_half(h), 6 + b % 2, 256:512], ACT.Copy)\
                                .then_inc(fold_cp, 1)
                        if 2 <= i_ < U + 2:
                            u = i_ - 2
                            b = u // 2
                            for g in range(2):
                                n = 2 * u + g
                                act.wait_ge(tr_ps, n + 1)
                                if b >= 2:
                                    act.wait_ge(av_ps, b - 1)
                                act.activation(ph[:, b % 2, 4 * g:4 * g + 4, (u % 2) * P:(u % 2 + 1) * P],
                                               ps[:, 4 + n % 2, :].rearrange("p (k q) -> p k q", k=4),
                                               ACT.Copy).then_inc(ph_ok, 1)
                        if i_ < U:
                            act.wait_ge(max_ok, i_ + 1)
                            if i_ >= 2:
                                act.wait_ge(tr_ps, 2 * i_ - 2)
                            act.activation(prob[:, i_ % 2, :], ps[:, 2 * (i_ % 2):2 * (i_ % 2) + 2, :]
                                           .rearrange("p a b -> p (a b)"), ACT.Exp,
                                           bias=neg_max[:, i_:i_ + 1], accum_out=row_sum[:, i_:i_ + 1]).then_inc(exp_ok, 1)
                    for c in range(CT):
                        act.wait_ge(att_ok, 2 * NB * (c + 1))
                        act.activation(xh[:, c, :], qk[:, c, :], ACT.Copy).then_inc(ah_ok, 1)

                @block.vector
                def _(dve):
                    steps = [0]

                    def link(ins):
                        steps[0] += 1
                        ins.then_inc(chain, 1)
                        dve.wait_ge(chain, steps[0])

                    for s in range(2):
                        for c in range(CT):
                            dve.wait_ge(xt_sb, s * CT + c + 1)
                            dve.bn_stats(bn[:, c, s, :], xt[:, c, s * HALF:(s + 1) * HALF]).then_inc(bn_ok, 1)
                    dve.wait_ge(bn_ok, 2 * CT)
                    mv = small[:, 8:16].rearrange("p (c m) -> p c m", m=2)
                    for c in range(CT):
                        dve.bn_aggr(mv[:, c, :], bn[:, c, :, :].rearrange("p s k -> p (s k)")).then_inc(bn_ag, 1)
                    dve.wait_ge(bn_ag, CT)
                    link(dve.tensor_tensor(small[:, 16:20], mv[:, :, 0], mv[:, :, 0], ALU.mult))
                    dve.tensor_copy(small[:, 0:4], mv[:, :, 0]).then_inc(st_ok, 1)
                    dve.tensor_tensor(small[:, 4:8], small[:, 16:20], mv[:, :, 1], ALU.add).then_inc(st_ok, 1)
                    dve.wait_ge(st_ps, 1)
                    link(dve.tensor_copy(small[:, 20:28], ps[:, 7, 0:8]))
                    link(dve.tensor_tensor(small[:, 28:32], small[:, 20:24], small[:, 20:24], ALU.mult))
                    link(dve.tensor_tensor(small[:, 28:32], small[:, 24:28], small[:, 28:32], ALU.subtract))
                    dve.tensor_scalar(small[:, 28:32], small[:, 28:32], 0.0, 1e-6, ALU.max, ALU.add).then_inc(var_ok, 1)
                    dve.wait_ge(rstd_ok, 1)
                    link(dve.tensor_tensor(small[:, 32:36], small[:, 32:36], vec[:, 0:4], ALU.mult))
                    link(dve.tensor_tensor(small[:, 36:40], small[:, 20:24], small[:, 32:36], ALU.mult))
                    link(dve.tensor_tensor(small[:, 36:40], vec[:, 4:8], small[:, 36:40], ALU.subtract))
                    for c in range(CT):
                        dve.tensor_scalar(xt[:, c, :], xt[:, c, :], small[:, 32 + c:33 + c], small[:, 36 + c:37 + c],
                                          ALU.mult, ALU.add).then_inc(xn_ok, 1)
                    for c in range(CT):
                        dve.wait_ge(xh_ok, c + 1)
                        dve.tensor_tensor(xl[:, c, :], xt[:, c, :], raw(xh[:, c, :]), ALU.subtract).then_inc(xl_ok, 1)
                    for g, (kind, m, s) in enumerate(groups):
                        if kind == "v":
                            dve.wait_ge(vh_ok, m + 1)
                            dve.tensor_tensor(v_lo(v[:, m, :]), by_head(ps[:, g % 8, :]), raw(v_hi(v[:, m, :])),
                                              ALU.subtract).then_inc(vl_ok, 1)
                    for i_ in range(U + 7):
                        if i_ < U:
                            dve.wait_ge(score, i_ + 1)
                            dve.tensor_reduce(neg_max[:, i_:i_ + 1], ps[:, 2 * (i_ % 2):2 * (i_ % 2) + 2, :]
                                              .rearrange("p a b -> p (a b)"), AX, ALU.max, negate=True).then_inc(max_ok, 1)
                        if 6 <= i_ <= U + 4 and i_ % 2 == 0:
                            b = (i_ - 6) // 2
                            h = b // NB
                            dve.wait_ge(fold_cp, 2 * b + 2)
                            if b >= 2:
                                dve.wait_ge(att_ok, b - 1)
                            dve.tensor_tensor(fold_s[own_half(h), b % 2, :], ps[own_half(h), 6 + b % 2, 0:256],
                                              fold_t[own_half(h), :], ALU.add).then_inc(fold_add, 1)
                        if 2 <= i_ < U + 2:
                            u = i_ - 2
                            b = u // 2
                            for g in range(2):
                                n = 2 * u + g
                                here = (slice(None), b % 2, slice(4 * g, 4 * g + 4), slice((u % 2) * P, (u % 2 + 1) * P))
                                dve.wait_ge(ph_ok, n + 1)
                                dve.tensor_tensor(pl[here], ps[:, 4 + n % 2, :].rearrange("p (k q) -> p k q", k=4),
                                                  raw(ph[here]), ALU.subtract).then_inc(pl_ok, 1)
                            if u % 2 == 1:
                                dve.wait_ge(exp_ok, u + 1)
                                dve.reciprocal(row_inv[:, u - 1:u + 1], row_sum[:, u - 1:u + 1]).then_inc(inv_ok, 1)
                    for c in range(CT):
                        dve.wait_ge(ah_ok, c + 1)
                        dve.tensor_tensor(xl[:, c, :], qk[:, c, :], raw(xh[:, c, :]), ALU.subtract).then_inc(al_ok, 1)
                    for t in range(TT):
                        dve.wait_ge(out_ps, t + 1)
                        dve.wait_ge(res_ok, t + 1)
                        dve.tensor_tensor(tok[:, t % 3, :], ps[:, t, :], tok[:, t % 3, :], ALU.add).then_inc(out_ok, 1)

                @block.gpsimd
                def _(pool):
                    pool.wait_ge(var_ok, 1)
                    pool.tensor_tensor(small[:, 32:36], small[:, 28:32], neg_half[:], ALU.pow).then_inc(rstd_ok, 1)

                    def stage(h, parts):
                        j, n = h % 2, STAGE * h
                        hi = kh[:, j, :]
                        if 0 in parts:
                            pool.wait_ge(s_ld[j], 64 * (h // 2 + 1))
                            pool.tensor_scalar(hi, raw(qs[:, j, :]), 1.0, 0.0, ALU.mult, ALU.add).then_inc(staged, 1)
                            pool.wait_ge(staged, n + 1)
                            pool.tensor_tensor(qs[HD:P, j, :], raw(qs[HD:P, j, :]), raw(hi[HD:P, :]), ALU.subtract)\
                                .then_inc(staged, 1)
                            pool.wait_ge(staged, n + 2)
                        if 1 in parts:
                            pool.tensor_scalar(qs[0:HD, j, :], raw(hi[0:HD, :]), 1.0, 0.0, ALU.mult, ALU.add)\
                                .then_inc(staged, 1)
                            pool.wait_ge(staged, n + 3)
                            pool.tensor_scalar(hi, raw(kl[:, j, :]), 1.0, 0.0, ALU.mult, ALU.add).then_inc(staged, 1)
                            pool.wait_ge(staged, n + 4)
                        if 2 in parts:
                            pool.tensor_tensor(kl[:, j, :], raw(kl[:, j, :]), raw(hi), ALU.subtract).then_inc(staged, 1)
                            pool.wait_ge(staged, n + 5)

                    stage(0, (0, 1, 2))
                    stage(1, (0, 1, 2))
                    for b in range(U // 2):
                        h = b // NB
                        pool.wait_ge(fold_add, b + 1)
                        pool.wait_ge(fold_cp, 2 * b + 2)
                        pool.tensor_tensor(qk[own_half(h), h // 2, (b % NB) * 256:(b % NB + 1) * 256],
                                           fold_s[own_half(h), b % 2, :], fold_r[own_half(h), b % 2, :],
                                           ALU.mult).then_inc(att_ok, 1)
                        pool.wait_ge(att_ok, b + 1)
                        k, part = (b + 2) // NB, (b + 2) % NB
                        if 1 <= k <= NH - 2 and part < 3:
                            stage(k + 1, (part,))
                    for t in range(TT):
                        pool.wait_ge(r_ld[t % 3], 16 * (t // 3 + 1))
                        pool.tensor_tensor(tok[:, t % 3, :], tok[:, t % 3, :], bout[:], ALU.add).then_inc(res_ok, 1)

        with nc.Fori(0, n_images) as i:
            image(i)
            nc.all_engine_barrier(sems_to_clear=range(min(nums), max(nums) + 1))


def layer1(nc, x2, ln_g, ln_b, wq, bq, wv, bv, dw_w, dw_b, pw_w, mq_w, mq_b, mk_w, mk_b, mv_w, mv_b,
           mo_w, mo_b, mlp_w, mlp_b, out, n_images=B):
    NK = NS
    KT = NK // P
    QG = 4
    GR = TT // QG
    U = NH * GR
    SLOTS = 3

    with ExitStack() as ctx:
        def sem(name):
            return ctx.enter_context(nc.semaphore("b_" + name))

        ps = ctx.enter_context(nc.psum_tensor("b_ps", [P, 8, 512], F32))
        R = Region(nc, SB_START, SB_END)
        names = ("wq", "wqm", "wvk", "wvv", "mo", "mlp")
        wh = {n: R.take(f"b_{n}_hi", [P, CT, C], F32R) for n in names}
        wl = {n: R.take(f"b_{n}_lo", [P, CT, C], F32R) for n in names}
        ident = R.take("b_ident", [P, P])
        lng = R.take("b_lng", [P, C])
        lnb = R.take("b_lnb", [P, C])
        bqw = R.take("b_bqw", [P, C])
        bmo = R.take("b_bmo", [P, C])
        bmlp = R.take("b_bmlp", [P, C])
        refs = R.take("b_refs", [P, 2, NS])
        vec = R.take("b_vec", [P, 32])
        dww = R.take("b_dww", [P, CT, KS * KS])
        bqm = R.take("b_bqm", [P, CT])
        bkm = R.take("b_bkm", [P, CT])
        bvm = R.take("b_bvm", [P, CT])
        neg_x = R.take("b_neg_x", [P, 1])
        neg_y = R.take("b_neg_y", [P, TT])
        neg_half = R.take("b_neg_half", [P, CT])
        bn = R.take("b_bn", [P, TT, 6])
        mv = R.take("b_mv", [P, TT, 2])
        rstd = R.take("b_rstd", [P, TT])
        neg_max = R.take("b_neg_max", [P, U * QG])
        row_sum = R.take("b_row_sum", [P, U * QG])
        row_inv = R.take("b_row_inv", [P, U * QG])
        xs = R.take("b_xs", [P, TT, C])
        qk = R.take("b_q", [P, CT, TOK])
        split = R.at
        xh = R.take("b_xh", [P, TT, C], F32R)
        xl = R.take("b_xl", [P, TT, C], F32R)
        scene = R.at
        ln = Region(nc, split - 16384, SB_END).take("b_ln", [P, TT, C])
        E = Region(nc, scene, SB_END)
        qpad = E.take("b_qpad", [P, CT, PADW * PADW])
        E = Region(nc, scene + 24576, SB_END)
        acc = E.take("b_acc", [P, CT, NS])
        o = E.take("b_o", [P, CT, NS])
        E = Region(nc, scene, SB_END)
        hat = E.take("b_hat", [P, TT, NS])
        hath = E.take("b_hat_hi", [P, TT, NS], F32R)
        hatl = E.take("b_hat_lo", [P, TT, NS], F32R)
        xy = E.take("b_xy", [P, 2, NS])
        hx = E.take("b_hx", [P, NS])
        E = Region(nc, scene, SB_END)
        ith = E.take("b_it_hi", [P, KT, 2, NK], F32R)
        itl = E.take("b_it_lo", [P, KT, 2, NK], F32R)
        v = E.take("b_v", [P, KT, NH * P], F32R)
        kraw = E.take("b_k", [P, CT, NK])
        kh = E.take("b_kh", [P, SLOTS, NK], F32R)
        kl = E.take("b_kl", [P, SLOTS, NK], F32R)
        fold_t = E.take("b_fold_t", [P, 512])
        fold_r = E.take("b_fold_r", [P, 512])
        fold_s = E.take("b_fold_s", [P, 512])
        E = Region(nc, scene, SB_END)
        q_hi = E.take("b_q_hi", [P, TOK], F32R)
        qs2 = E.take("b_qs2", [P, TOK], F32R)
        A = Region(nc, split, scene)
        qs = [A.take("b_qs0", [P, TOK], F32R), A.take("b_qs1", [P, TOK], F32R), qs2]
        prob = A.take("b_prob", [P, 2, QG, NK])
        ph = A.take("b_ph", [P, 2, KT, 512], F32R)
        pl = A.take("b_pl", [P, 2, KT, 512], F32R)
        D = Region(nc, split, scene)
        ah = D.take("b_ah", [P, CT, TOK], F32R)
        al = D.take("b_al", [P, CT, TOK], F32R)
        E = Region(nc, scene, SB_END)
        zn = E.take("b_zn", [P, 2, C])
        zh = E.take("b_zh", [P, 2, CT, P], F32R)
        zl = E.take("b_zl", [P, 2, CT, P], F32R)
        ot = E.take("b_ot", [P, 3, C])
        W = Region(nc, split - 32768, SB_END)
        raws = {n: W.take(f"b_{n}_raw", [P, CT, C]) for n in ("wq", "mq", "wv", "mk", "mv", "mo", "mlp")}
        wqt = W.take("b_wq_t", [P, CT, C])
        wvt = W.take("b_wv_t", [P, CT, C])
        rows = W.take("b_rows", [32, P])
        wide = W.take("b_wide", [P, CT, P])
        bo_raw = W.take("b_bo_raw", [P, C])
        assert W.at <= SB_END

        ld, cst, hi_ok, lo_ok, pe_s, chn = (sem("s_" + n) for n in ("ld", "cst", "hi", "lo", "pe", "chn"))
        wt_sb = sem("s_wt")
        with nc.Block() as block:
            @block.sync
            def _(sp):
                for n, w in (("wq", wq), ("mq", mq_w), ("wv", wv), ("mk", mk_w), ("mv", mv_w), ("mo", mo_w),
                             ("mlp", mlp_w)):
                    sp.dma_start(raws[n][:], w.rearrange("(t p) n -> p t n", p=P)).then_inc(ld, 16)
                for n, vv in enumerate((bq, bv, mq_b, mk_b, mv_b)):
                    sp.dma_start(rows[4 * n:4 * n + 4, :], vv.rearrange("(t p) -> t p", p=P)).then_inc(ld, 16)
                sp.dma_start(rows[20:28, :], pw_w.rearrange("k (t p) -> (k t) p", p=P)).then_inc(ld, 16)
                sp.dma_start(rows[28:32, :], dw_b.rearrange("(t p) -> t p", p=P)).then_inc(ld, 16)
                sp.dma_start(dww[:], dw_w.rearrange("(t p) k -> p t k", p=P)).then_inc(ld, 16)
                for d, s in ((lng, ln_g), (lnb, ln_b), (bqw, bq), (bo_raw, mo_b), (bmlp, mlp_b)):
                    sp.dma_start(d[:], s.partition_broadcast(P)).then_inc(ld, 16)
                sp.wait_ge(ld, 20 * 16)

            @block.gpsimd
            def _(pool):
                make_identity(pool, ident, cst)
                pool.memset(neg_half[:], -0.5).then_inc(cst, 1)
                for g in range(4):
                    here = slice(32 * g, 32 * g + 32)
                    pool.wait_ge(cst, 3 + 2 * g)
                    pool.iota(neg_x[here, :], [[0, 1]], base=0, channel_multiplier=-1,
                              allow_small_or_imprecise_dtypes=True).then_inc(cst, 1)
                    pool.iota(neg_y[here, :], [[-4, TT]], base=-g, channel_multiplier=0,
                              allow_small_or_imprecise_dtypes=True).then_inc(cst, 1)
                pool.wait_ge(cst, 11)
                pool.iota(refs[:, 0, :], [[1, GRID], [0, GRID]], base=0, channel_multiplier=0,
                          allow_small_or_imprecise_dtypes=True).then_inc(cst, 1)
                pool.wait_ge(cst, 12)
                pool.iota(refs[:, 1, :], [[0, GRID], [1, GRID]], base=0, channel_multiplier=0,
                          allow_small_or_imprecise_dtypes=True).then_inc(cst, 1)

            products = (("wqm", wqt, "mq"), ("wvk", wvt, "mk"), ("wvv", wvt, "mv"))

            @block.scalar
            def _(act):
                act.wait_ge(ld, 20 * 16)
                for n in ("wq", "mo", "mlp"):
                    act.activation(wh[n][:], raws[n][:], ACT.Copy).then_inc(hi_ok, 1)
                for g in range(12):
                    n, j = products[g // 4][0], g % 4
                    act.wait_ge(pe_s, 9 + g + 1)
                    act.activation(wh[n][:, j, :], ps[:, g % 8, :], ACT.Copy).then_inc(hi_ok, 1)

            @block.tensor
            def _(pe):
                pe.wait_ge(ld, 20 * 16)
                pe.wait_ge(cst, 2)
                for w, n in enumerate(("wq", "wv")):
                    for k in range(CT):
                        for j in range(CT):
                            mm = pe.transpose(ps[:, 4 * w + k, j * P:(j + 1) * P],
                                              raws[n][:, j, k * P:(k + 1) * P], ident[:])
                        mm.then_inc(pe_s, 1)
                pe.wait_ge(wt_sb, 8)
                pe.transpose(ps[:, 0, 0:32], rows[:], ident[0:32, 0:32]).then_inc(pe_s, 1)
                for g in range(12):
                    n, wt, m = products[g // 4]
                    j = g % 4
                    pe.wait_ge(chn, 1)
                    if g >= 8:
                        pe.wait_ge(lo_ok, g - 7)
                    for k in range(CT):
                        mm = pe.matmul(ps[:, g % 8, :], wt[:, k, j * P:(j + 1) * P], raws[m][:, k, :],
                                       start=k == 0, stop=k == CT - 1)
                    mm.then_inc(pe_s, 1)
                pe.wait_ge(lo_ok, 12)
                for g, (at, m) in enumerate(((0, "mq"), (4, "mk"), (4, "mv"))):
                    for j in range(CT):
                        for k in range(CT):
                            mm = pe.matmul(ps[:, 5, 4 * g + j:4 * g + j + 1], raws[m][:, k, j * P:(j + 1) * P],
                                           vec[:, at + k:at + k + 1], start=k == 0, stop=k == CT - 1)
                mm.then_inc(pe_s, 1)
                pe.wait_ge(chn, 7)
                for k in range(CT):
                    mm = pe.matmul(ps[:, 6, :], wide[:, k, :], raws["mo"][:, k, :], start=k == 0, stop=k == CT - 1)
                mm.then_inc(pe_s, 1)

            @block.vector
            def _(dve):
                for g in range(8):
                    dve.wait_ge(pe_s, g + 1)
                    dve.tensor_copy((wqt if g < 4 else wvt)[:, g % 4, :], ps[:, g, :]).then_inc(wt_sb, 1)
                dve.wait_ge(pe_s, 9)
                dve.tensor_copy(vec[:], ps[:, 0, 0:32]).then_inc(chn, 1)
                for n, w in enumerate(("wq", "mo", "mlp")):
                    dve.wait_ge(hi_ok, n + 1)
                    dve.tensor_tensor(wl[w][:], raws[w][:], raw(wh[w][:]), ALU.subtract).then_inc(wt_sb, 1)
                for g in range(12):
                    n, j = products[g // 4][0], g % 4
                    dve.wait_ge(hi_ok, 3 + g + 1)
                    dve.tensor_tensor(wl[n][:, j, :], ps[:, g % 8, :], raw(wh[n][:, j, :]), ALU.subtract)\
                       .then_inc(lo_ok, 1)
                dve.wait_ge(cst, 13)
                dve.tensor_scalar(refs[:], refs[:], 0.5, 2.0 / GRID, ALU.add, ALU.mult).then_inc(chn, 1)
                dve.wait_ge(chn, 2)
                dve.tensor_scalar(refs[:], refs[:], -1.0, None, ALU.add).then_inc(chn, 1)
                dve.wait_ge(pe_s, 22)
                for g, (dst, at) in enumerate(((bqm, 8), (bkm, 12), (bvm, 16))):
                    dve.tensor_tensor(dst[:], ps[:, 5, 4 * g:4 * g + 4], vec[:, at:at + 4], ALU.add).then_inc(chn, 1)
                dve.wait_ge(chn, 6)
                dve.tensor_copy(wide[:], bvm[:].unsqueeze(2).to_broadcast([P, CT, P])).then_inc(chn, 1)
                dve.wait_ge(pe_s, 23)
                dve.tensor_tensor(bmo[:], ps[:, 6, :], bo_raw[:], ALU.add).then_inc(chn, 1)

        x_ld = [sem(f"x_ld{t}") for t in range(TT)]
        s_ld = [sem(f"s_ld{j}") for j in range(SLOTS)]
        o_st = [sem(f"o_st{j}") for j in range(3)]
        (bn_ok, bn_ag, var_ok, rstd_ok, ln1, ln_ok, xh_ok, xl_ok, pad_ok, q_ps, q_sb, tap, gelu_ok, qh_ps, qh_sb,
         sh_ok, sl_ok, off_ps, tanh_ok, xy_ok, hx_ok, hy_ok, hat_ok, hh_ok, hl_ok, it_ps, ih_ok, il_ok, k_ps, k_sb,
         v_ps, vh_ok, vl_ok, staged, score, max_ok, exp_ok, tr_ps, ph_ok, pl_ok, inv_ok, av_ps, fold_cp, fold_add,
         att_ok, ah_ok, al_ok, mo_ps, z1_ok, z_ok, zn1, zn_ok, zt_ps, zh_ok, zl_ok, ml_ps, y_ok, ge_ok, out_ok,
         chain, zvar, zrstd) = singles = [sem(n) for n in (
             "bn_ok bn_ag var_ok rstd_ok ln1 ln_ok xh_ok xl_ok pad_ok q_ps q_sb tap gelu_ok qh_ps qh_sb sh_ok sl_ok "
             "off_ps tanh_ok xy_ok hx_ok hy_ok hat_ok hh_ok hl_ok it_ps ih_ok il_ok k_ps k_sb v_ps vh_ok vl_ok staged "
             "score max_ok exp_ok tr_ps ph_ok pl_ok inv_ok av_ps fold_cp fold_add att_ok ah_ok al_ok mo_ps z1_ok z_ok "
             "zn1 zn_ok zt_ps zh_ok zl_ok ml_ps y_ok ge_ok out_ok chain zvar zrstd").split()]
        nums = [s.num for s in [*x_ld, *s_ld, *o_st, *singles]]
        assert sorted(nums) == list(range(min(nums), max(nums) + 1))
        STAGE = 5

        def image(i):
            with nc.Block() as block:
                @block.sync
                def _(sp):
                    for t in range(TT):
                        sp.dma_start(xs[:, t, :], x2[i, t * P:(t + 1) * P, :]).then_inc(x_ld[t], 16)
                    sp.wait_ge(qh_sb, 2 * CT)
                    sp.wait_ge(k_sb, CT)
                    sp.wait_ge(vl_ok, KT)
                    for h in range(NH):
                        p, j = h // 2, h % SLOTS
                        if h >= SLOTS:
                            sp.wait_ge(score, GR * (h - SLOTS + 1))
                        for half in range(2):
                            rows_ = slice(HD * half, HD * half + HD)
                            sp.dma_start(raw(qs[j][rows_, :]), qk[own_half(h), p, :]).then_inc(s_ld[j], 16)
                            sp.dma_start(raw(kl[rows_, j, :]), kraw[own_half(h), p, :]).then_inc(s_ld[j], 16)
                    for t in range(TT):
                        sp.wait_ge(out_ok, t + 1)
                        sp.dma_start(out[i, t * P:(t + 1) * P, :], ot[:, t % 3, :]).then_inc(o_st[t % 3], 16)
                    for t in range(3):
                        sp.wait_ge(o_st[t], 16 * ((TT - t + 2) // 3))

                @block.tensor
                def _(pe):
                    def three(bank, left, right, first, last):
                        (lh, ll), (rh, rl) = left, right
                        for e, (a, b) in enumerate(((lh, rh), (lh, rl), (ll, rh))):
                            mm = pe.matmul(bank, a, b, start=first and e == 0, stop=last and e == 2)
                        return mm

                    for s in range(2):
                        pe.wait_ge(xh_ok, 4 * s + 4)
                        pe.wait_ge(xl_ok, 4 * s + 4)
                        for c in range(CT):
                            n = slice(c * P, (c + 1) * P)
                            for k in range(CT):
                                t = 4 * s + k
                                mm = three(ps[:, 4 * s + c, :], (xh[:, t, n], xl[:, t, n]),
                                           (wh["wq"][:, k, :], wl["wq"][:, k, :]), k == 0, k == CT - 1)
                            mm.then_inc(q_ps, 1)
                    for g in range(2 * CT):
                        m, s = g // 2, g % 2
                        pe.wait_ge(q_sb, g + 1)
                        n = slice(m * P, (m + 1) * P)
                        for k in range(CT):
                            t = 4 * s + k
                            mm = three(ps[:, g, :], (wh["wqm"][:, k, n], wl["wqm"][:, k, n]),
                                       (xh[:, t, :], xl[:, t, :]), k == 0, k == CT - 1)
                        mm.then_inc(qh_ps, 1)
                    pe.wait_ge(qh_sb, 1)
                    for c in range(2):
                        for k in range(CT):
                            if c == 0:
                                pe.wait_ge(gelu_ok, k + 1)
                            mm = pe.matmul(ps[:, 0, c * NS:(c + 1) * NS],
                                           vec[:, 20 + 4 * c + k:21 + 4 * c + k].to_broadcast([P, P]), o[:, k, :],
                                           start=k == 0, stop=k == CT - 1)
                    mm.then_inc(off_ps, 1)
                    for st in range(KT):
                        pe.wait_ge(qh_sb, 2 + st)
                        for t in range(TT):
                            if st == 0 and t % 4 == 0:
                                pe.wait_ge(hh_ok, t // 4 + 1)
                                pe.wait_ge(hl_ok, t // 4 + 1)
                                pe.wait_ge(sh_ok, TT)
                                pe.wait_ge(sl_ok, TT)
                            n = slice(st * P, (st + 1) * P)
                            mm = three(ps[:, 1 + st, :], (hath[:, t, n], hatl[:, t, n]), (xh[:, t, :], xl[:, t, :]),
                                       t == 0, t == TT - 1)
                        mm.then_inc(it_ps, 1)
                    pe.wait_ge(ih_ok, KT)
                    pe.wait_ge(il_ok, KT)
                    pe.wait_ge(qh_sb, 2 * CT)
                    for m in range(CT):
                        n = slice(m * P, (m + 1) * P)
                        for f in range(4):
                            e, st = f // 2, f % 2
                            mm = three(ps[:, 3 + m, 0:NK], (wh["wvk"][:, f, n], wl["wvk"][:, f, n]),
                                       (ith[:, st, e, :], itl[:, st, e, :]), f == 0, f == 3)
                        mm.then_inc(k_ps, 1)
                    pe.wait_ge(tanh_ok, 1)
                    for r in range(KT):
                        n = slice(r * P, (r + 1) * P)
                        for f in range(4):
                            e, st = f // 2, f % 2
                            mm = three(ps[:, 7 * (1 - r), :], (ith[:, st, e, n], itl[:, st, e, n]),
                                       (wh["wvv"][:, f, :], wl["wvv"][:, f, :]), f == 0, f == 3)
                        mm.then_inc(v_ps, 1)

                    pe.wait_ge(k_sb, CT)
                    pe.wait_ge(vl_ok, KT)
                    for i_ in range(U + 4):
                        if i_ >= 4:
                            u = i_ - 4
                            h = u // GR
                            pe.wait_ge(inv_ok, u + 1)
                            if u >= 1:
                                pe.wait_ge(fold_add, u)
                                pe.wait_ge(fold_cp, 2 * u)
                            pe.wait_ge(pl_ok, 2 * u + 2)
                            for kt in range(KT):
                                for e, q_ in enumerate((ph, pl)):
                                    pe.matmul(ps[:, 6, :], v[:, kt, h * P:(h + 1) * P], q_[:, u % 2, kt, :],
                                              start=kt == 0 and e == 0, stop=kt == KT - 1 and e == 1)
                            for n in range(QG):
                                c = QG * u + n
                                mm = pe.transpose(ps[:, 7, n * P:(n + 1) * P],
                                                  row_inv[:, c:c + 1].to_broadcast([P, P]), ident[:])
                            mm.then_inc(av_ps, 1)
                        if i_ < U:
                            h, g = i_ // GR, i_ % GR
                            j = h % SLOTS
                            if g == 0:
                                pe.wait_ge(staged, STAGE * (h + 1))
                            if i_ >= 2:
                                pe.wait_ge(exp_ok, QG * (i_ - 1))
                            for t in range(QG):
                                dst = ps[:, 2 * (i_ % 2) + t // 2, (t % 2) * NK:(t % 2 + 1) * NK]
                                q_ = qs[j][:, (QG * g + t) * P:(QG * g + t + 1) * P]
                                pe.matmul(dst, q_, kh[:, j, :], start=True, stop=False)
                                mm = pe.matmul(dst, q_, kl[:, j, :], start=False, stop=True)
                            mm.then_inc(score, 1)
                        if 2 <= i_ < U + 2:
                            u = i_ - 2
                            pe.wait_ge(exp_ok, QG * (u + 1))
                            for kt in range(KT):
                                if u >= 1:
                                    pe.wait_ge(pl_ok, 2 * u - 1 + kt)
                                for t in range(QG):
                                    mm = pe.transpose(ps[:, 4 + kt, t * P:(t + 1) * P],
                                                      prob[:, u % 2, t, kt * P:(kt + 1) * P], ident[:])
                                mm.then_inc(tr_ps, 1)

                    for t in range(TT + 2):
                        if t < TT:
                            if t == 0:
                                pe.wait_ge(ah_ok, CT)
                                pe.wait_ge(al_ok, CT)
                            if t >= 2:
                                pe.wait_ge(z1_ok, t - 1)
                            n = slice(t * P, (t + 1) * P)
                            for k in range(CT):
                                mm = three(ps[:, t % 2, :], (ah[:, k, n], al[:, k, n]),
                                           (wh["mo"][:, k, :], wl["mo"][:, k, :]), k == 0, k == CT - 1)
                            mm.then_inc(mo_ps, 1)
                        if 1 <= t <= TT:
                            u = t - 1
                            pe.wait_ge(zn_ok, u + 1)
                            if u >= 2:
                                pe.wait_ge(zl_ok, u - 1)
                            for k in range(CT):
                                mm = pe.transpose(ps[:, 2 + u % 2, k * P:(k + 1) * P], zn[:, u % 2, k * P:(k + 1) * P],
                                                  ident[:])
                            mm.then_inc(zt_ps, 1)
                        if t >= 2:
                            u = t - 2
                            pe.wait_ge(zl_ok, u + 1)
                            if u >= 2:
                                pe.wait_ge(y_ok, u - 1)
                            for k in range(CT):
                                mm = three(ps[:, 4 + u % 2, :], (zh[:, u % 2, k, :], zl[:, u % 2, k, :]),
                                           (wh["mlp"][:, k, :], wl["mlp"][:, k, :]), k == 0, k == CT - 1)
                            mm.then_inc(ml_ps, 1)

                @block.scalar
                def _(act):
                    for t in range(TT):
                        act.wait_ge(ln_ok, t + 1)
                        act.activation(xh[:, t, :], ln[:, t, :], ACT.Copy).then_inc(xh_ok, 1)
                    act.wait_ge(q_ps, 2 * CT)
                    for g in range(2 * CT):
                        m, s = g // 2, g % 2
                        act.wait_ge(qh_ps, g + 1)
                        act.activation(qk[:, m, :].rearrange("p (c s) -> p s c", s=2)[:, s, :], ps[:, g, :],
                                       ACT.Identity, bias=bqm[:, m:m + 1]).then_inc(qh_sb, 1)
                    for t in range(TT):
                        act.activation(xh[:, t, :], xs[:, t, :], ACT.Copy).then_inc(sh_ok, 1)
                    for c in range(CT):
                        act.wait_ge(tap, CT * (KS * KS - 1) + c + 1)
                        act.activation(o[:, c, :], acc[:, c, :], ACT.Gelu).then_inc(gelu_ok, 1)
                    act.wait_ge(off_ps, 1)
                    act.activation(xy[:].rearrange("p k n -> p (k n)"), ps[:, 0, :], ACT.Tanh).then_inc(tanh_ok, 1)
                    act.wait_ge(xy_ok, 3)
                    act.activation(hx[:], xy[:, 1, :], ACT.Abs, bias=neg_x[:, 0:1]).then_inc(hx_ok, 1)
                    for t in range(TT):
                        act.activation(hat[:, t, :], xy[:, 0, :], ACT.Abs, bias=neg_y[:, t:t + 1]).then_inc(hy_ok, 1)
                        if t == 0:
                            act.wait_ge(hx_ok, 1)
                            act.activation(hx[:], hx[:], ACT.Relu, bias=1.0, scale=-1.0).then_inc(hx_ok, 1)
                        if t % 4 == 3:
                            half = hat[:, t - 3:t + 1, :]
                            act.wait_ge(hy_ok, t + 1 + t // 4)
                            act.activation(half, half, ACT.Relu, bias=1.0, scale=-1.0).then_inc(hy_ok, 1)
                    for s in range(2):
                        act.wait_ge(hat_ok, s + 1)
                        act.activation(hath[:, 4 * s:4 * s + 4, :], hat[:, 4 * s:4 * s + 4, :], ACT.Copy).then_inc(hh_ok, 1)
                    act.wait_ge(hl_ok, 2)
                    for st in range(KT):
                        act.wait_ge(it_ps, st + 1)
                        act.activation(ith[:, st, :, :], ps[:, 1 + st, :].rearrange("p (r e) -> p e r", e=2), ACT.Copy)\
                            .then_inc(ih_ok, 1)
                    for m in range(CT):
                        act.wait_ge(k_ps, m + 1)
                        act.activation(kraw[:, m, :], ps[:, 3 + m, 0:NK], ACT.Identity, bias=bkm[:, m:m + 1])\
                            .then_inc(k_sb, 1)
                    for r in range(KT):
                        act.wait_ge(v_ps, r + 1)
                        act.activation(v_hi(v[:, r, :]), by_head(ps[:, 7 * (1 - r), :]), ACT.Copy).then_inc(vh_ok, 1)
                    for i_ in range(U + 5):
                        if i_ >= 4 and i_ - 4 < U:
                            u = i_ - 4
                            h = u // GR
                            act.wait_ge(av_ps, u + 1)
                            if u >= 1:
                                act.wait_ge(fold_add, u)
                            act.activation(fold_t[own_half(h), :], ps[other_half(h), 6, :], ACT.Copy).then_inc(fold_cp, 1)
                            if u >= 1:
                                act.wait_ge(att_ok, u)
                            act.activation(fold_r[own_half(h), :], ps[own_half(h), 7, :], ACT.Copy).then_inc(fold_cp, 1)
                        if 2 <= i_ < U + 2:
                            u = i_ - 2
                            for kt in range(KT):
                                n = KT * u + kt
                                act.wait_ge(tr_ps, n + 1)
                                if u >= 2:
                                    act.wait_ge(av_ps, u - 1)
                                act.activation(ph[:, u % 2, kt, :], ps[:, 4 + kt, :], ACT.Copy).then_inc(ph_ok, 1)
                        if i_ < U:
                            act.wait_ge(max_ok, i_ + 1)
                            if i_ >= 2:
                                act.wait_ge(tr_ps, KT * (i_ - 1))
                            for t in range(QG):
                                c = QG * i_ + t
                                act.activation(prob[:, i_ % 2, t, :],
                                               ps[:, 2 * (i_ % 2) + t // 2, (t % 2) * NK:(t % 2 + 1) * NK], ACT.Exp,
                                               bias=neg_max[:, c:c + 1], accum_out=row_sum[:, c:c + 1]).then_inc(exp_ok, 1)
                    for c in range(CT):
                        act.wait_ge(att_ok, 2 * GR * (c + 1))
                        if c == 0:
                            act.wait_ge(av_ps, U)
                        act.activation(ah[:, c, :], qk[:, c, :], ACT.Copy).then_inc(ah_ok, 1)
                    for t in range(1, TT + 2):
                        if t <= TT:
                            u = t - 1
                            act.wait_ge(zt_ps, u + 1)
                            if u >= 2:
                                act.wait_ge(ml_ps, u - 1)
                            act.activation(zh[:, u % 2, :, :], ps[:, 2 + u % 2, :].rearrange("p (k q) -> p k q", k=CT),
                                           ACT.Copy).then_inc(zh_ok, 1)
                        if t >= 2:
                            u = t - 2
                            act.wait_ge(y_ok, u + 1)
                            act.activation(ot[:, u % 3, :], ot[:, u % 3, :], ACT.Gelu).then_inc(ge_ok, 1)

                @block.vector
                def _(dve):
                    steps = [0]

                    def link(ins):
                        steps[0] += 1
                        ins.then_inc(chain, 1)
                        dve.wait_ge(chain, steps[0])

                    for s in range(2):
                        for t in range(4 * s, 4 * s + 4):
                            dve.wait_ge(x_ld[t], 16)
                            dve.bn_stats(bn[:, t, :], xs[:, t, :]).then_inc(bn_ok, 1)
                        for t in range(4 * s, 4 * s + 4):
                            dve.wait_ge(bn_ok, t + 1)
                            dve.bn_aggr(mv[:, t, :], bn[:, t, :]).then_inc(bn_ag, 1)
                        dve.wait_ge(bn_ag, 4 * s + 4)
                        dve.tensor_scalar(rstd[:, 4 * s:4 * s + 4], mv[:, 4 * s:4 * s + 4, 1], 1e-5, None, ALU.add)\
                           .then_inc(var_ok, 1)
                        for t in range(4 * s, 4 * s + 4):
                            dve.scalar_tensor_tensor(ln[:, t, :], xs[:, t, :], mv[:, t, 0:1], lng[:], ALU.subtract,
                                                     ALU.mult).then_inc(ln1, 1)
                        dve.wait_ge(rstd_ok, s + 1)
                        for t in range(4 * s, 4 * s + 4):
                            dve.wait_ge(ln1, t + 1)
                            dve.scalar_tensor_tensor(ln[:, t, :], ln[:, t, :], rstd[:, t:t + 1], lnb[:], ALU.mult,
                                                     ALU.add).then_inc(ln_ok, 1)
                        for t in range(4 * s, 4 * s + 4):
                            dve.wait_ge(xh_ok, t + 1)
                            dve.tensor_tensor(xl[:, t, :], ln[:, t, :], raw(xh[:, t, :]), ALU.subtract).then_inc(xl_ok, 1)
                    dve.wait_ge(pad_ok, 1)
                    for g in range(2 * CT):
                        s, c = g // 4, g % 4
                        dve.wait_ge(q_ps, g + 1)
                        inside = qpad[:, c, :].rearrange("p (y x) -> p y x", x=PADW)[
                            :, KS // 2 + 16 * s:KS // 2 + 16 * s + 16, KS // 2:KS // 2 + HW]
                        dve.tensor_tensor(inside, ps[:, g, :].rearrange("p (y x) -> p y x", x=HW),
                                          bqw[:].rearrange("p (y x) -> p y x", x=HW), ALU.add).then_inc(q_sb, 1)
                    dve.wait_ge(q_sb, 2 * CT)
                    for n in range(KS * KS):
                        dy, dx = n // KS, n % KS
                        for c in range(CT):
                            src = qpad[:, c, :].rearrange("p (y x) -> p y x", x=PADW)[
                                :, dy:dy + 2 * GRID - 1:2, dx:dx + 2 * GRID - 1:2]
                            dst = acc[:, c, :].rearrange("p (y x) -> p y x", x=GRID)
                            if n == 0:
                                dve.tensor_scalar(dst, src, dww[:, c, n:n + 1], vec[:, 28 + c:29 + c], ALU.mult,
                                                  ALU.add).then_inc(tap, 1)
                            else:
                                dve.wait_ge(tap, CT * (n - 1) + c + 1)
                                dve.scalar_tensor_tensor(dst, src, dww[:, c, n:n + 1], dst, ALU.mult, ALU.add)\
                                   .then_inc(tap, 1)
                    dve.wait_ge(tanh_ok, 1)
                    dve.tensor_tensor(xy[:], xy[:], refs[:], ALU.add).then_inc(xy_ok, 1)
                    dve.wait_ge(xy_ok, 1)
                    dve.tensor_scalar(xy[:], xy[:], 1.0, HW / 2 / 2.0, ALU.add, ALU.mult).then_inc(xy_ok, 1)
                    dve.wait_ge(xy_ok, 2)
                    dve.tensor_scalar(xy[:], xy[:], 1.0, 0.5 * (HW - 1), ALU.add, ALU.mult).then_inc(xy_ok, 1)
                    for s in range(2):
                        dve.wait_ge(hx_ok, 2)
                        dve.wait_ge(hy_ok, 5 * s + 5)
                        half = hat[:, 4 * s:4 * s + 4, :]
                        dve.tensor_tensor(half, half, hx[:].unsqueeze(1).to_broadcast([P, 4, NS]), ALU.mult)\
                           .then_inc(hat_ok, 1)
                    for s in range(2):
                        dve.wait_ge(hh_ok, s + 1)
                        here = (slice(None), slice(4 * s, 4 * s + 4), slice(None))
                        dve.tensor_tensor(hatl[here], hat[here], raw(hath[here]), ALU.subtract).then_inc(hl_ok, 1)
                    for st in range(KT):
                        dve.wait_ge(ih_ok, st + 1)
                        dve.tensor_tensor(itl[:, st, :, :], ps[:, 1 + st, :].rearrange("p (r e) -> p e r", e=2),
                                          raw(ith[:, st, :, :]), ALU.subtract).then_inc(il_ok, 1)
                    for r in range(KT):
                        dve.wait_ge(vh_ok, r + 1)
                        dve.tensor_tensor(v_lo(v[:, r, :]), by_head(ps[:, 7 * (1 - r), :]), raw(v_hi(v[:, r, :])),
                                          ALU.subtract).then_inc(vl_ok, 1)
                    for i_ in range(U + 5):
                        if i_ < U:
                            dve.wait_ge(score, i_ + 1)
                            dve.tensor_reduce(neg_max[:, QG * i_:QG * i_ + QG],
                                              ps[:, 2 * (i_ % 2):2 * (i_ % 2) + 2, :].rearrange("p a (b k) -> p (a b) k", b=2),
                                              AX, ALU.max, negate=True).then_inc(max_ok, 1)
                        if i_ >= 4 and i_ - 4 < U:
                            u = i_ - 4
                            h = u // GR
                            dve.wait_ge(fold_cp, 2 * u + 2)
                            if u >= 1:
                                dve.wait_ge(att_ok, u)
                            dve.tensor_tensor(fold_s[own_half(h), :], ps[own_half(h), 6, :], fold_t[own_half(h), :],
                                              ALU.add).then_inc(fold_add, 1)
                        if 2 <= i_ < U + 2:
                            u = i_ - 2
                            for kt in range(KT):
                                dve.wait_ge(ph_ok, KT * u + kt + 1)
                                dve.tensor_tensor(pl[:, u % 2, kt, :], ps[:, 4 + kt, :], raw(ph[:, u % 2, kt, :]),
                                                  ALU.subtract).then_inc(pl_ok, 1)
                            dve.wait_ge(exp_ok, QG * (u + 1))
                            dve.reciprocal(row_inv[:, QG * u:QG * u + QG], row_sum[:, QG * u:QG * u + QG])\
                               .then_inc(inv_ok, 1)
                    for c in range(CT):
                        dve.wait_ge(ah_ok, c + 1)
                        dve.tensor_tensor(al[:, c, :], qk[:, c, :], raw(ah[:, c, :]), ALU.subtract).then_inc(al_ok, 1)
                    for t in range(TT + 2):
                        if t < TT:
                            dve.wait_ge(mo_ps, t + 1)
                            dve.tensor_tensor(xs[:, t, :], ps[:, t % 2, :], xs[:, t, :], ALU.add).then_inc(z1_ok, 1)
                        if 1 <= t <= TT:
                            u = t - 1
                            dve.wait_ge(zh_ok, u + 1)
                            dve.tensor_tensor(zl[:, u % 2, :, :], ps[:, 2 + u % 2, :].rearrange("p (k q) -> p k q", k=CT),
                                              raw(zh[:, u % 2, :, :]), ALU.subtract).then_inc(zl_ok, 1)
                        if t < TT:
                            dve.wait_ge(z_ok, t + 1)
                            link(dve.bn_stats(bn[:, t, :], xs[:, t, :]))
                            link(dve.bn_aggr(mv[:, t, :], bn[:, t, :]))
                            dve.tensor_scalar(rstd[:, t:t + 1], mv[:, t, 1:2], 1e-5, None, ALU.add).then_inc(zvar, 1)
                            if t >= 2:
                                dve.wait_ge(zt_ps, t - 1)
                            link(dve.scalar_tensor_tensor(zn[:, t % 2, :], xs[:, t, :], mv[:, t, 0:1], lng[:],
                                                          ALU.subtract, ALU.mult))
                            dve.wait_ge(zrstd, t + 1)
                            dve.scalar_tensor_tensor(zn[:, t % 2, :], zn[:, t % 2, :], rstd[:, t:t + 1], lnb[:],
                                                     ALU.mult, ALU.add).then_inc(zn_ok, 1)
                        if t >= 2:
                            u = t - 2
                            dve.wait_ge(ml_ps, u + 1)
                            if u >= 3:
                                dve.wait_ge(o_st[u % 3], 16 * (u // 3))
                            dve.tensor_tensor(ot[:, u % 3, :], ps[:, 4 + u % 2, :], bmlp[:], ALU.add).then_inc(y_ok, 1)

                @block.gpsimd
                def _(pool):
                    pool.memset(qpad[:], 0.0).then_inc(pad_ok, 1)
                    pool.wait_ge(pad_ok, 1)
                    for s in range(2):
                        here = slice(4 * s, 4 * s + 4)
                        pool.wait_ge(var_ok, s + 1)
                        pool.tensor_tensor(rstd[:, here], rstd[:, here], neg_half[:], ALU.pow).then_inc(rstd_ok, 1)
                    pool.wait_ge(rstd_ok, 2)
                    for t in range(TT):
                        pool.wait_ge(sh_ok, t + 1)
                        pool.tensor_tensor(xl[:, t, :], xs[:, t, :], raw(xh[:, t, :]), ALU.subtract).then_inc(sl_ok, 1)
                    pool.wait_ge(sl_ok, TT)

                    def stage(h):
                        j, n = h % SLOTS, STAGE * h
                        tmp = q_hi
                        pool.wait_ge(s_ld[j], 64 * (h // SLOTS + 1))
                        pool.tensor_scalar(kh[:, j, :], raw(kl[:, j, :]), 1.0, 0.0, ALU.mult, ALU.add).then_inc(staged, 1)
                        pool.wait_ge(staged, n + 1)
                        pool.tensor_tensor(kl[:, j, :], raw(kl[:, j, :]), raw(kh[:, j, :]), ALU.subtract)\
                            .then_inc(staged, 1)
                        pool.wait_ge(staged, n + 2)
                        pool.tensor_scalar(tmp[:], raw(qs[j][:]), 1.0, 0.0, ALU.mult, ALU.add).then_inc(staged, 1)
                        pool.wait_ge(staged, n + 3)
                        pool.tensor_tensor(qs[j][HD:P, :], raw(qs[j][HD:P, :]), raw(tmp[HD:P, :]), ALU.subtract)\
                            .then_inc(staged, 1)
                        pool.wait_ge(staged, n + 4)
                        pool.tensor_scalar(qs[j][0:HD, :], raw(tmp[0:HD, :]), 1.0, 0.0, ALU.mult, ALU.add)\
                            .then_inc(staged, 1)
                        pool.wait_ge(staged, n + 5)

                    for h in range(SLOTS + 1):
                        stage(h)
                    for u in range(U):
                        h, g = u // GR, u % GR
                        pool.wait_ge(fold_add, u + 1)
                        pool.wait_ge(fold_cp, 2 * u + 2)
                        pool.tensor_tensor(qk[own_half(h), h // 2, g * 512:(g + 1) * 512], fold_s[own_half(h), :],
                                           fold_r[own_half(h), :], ALU.mult).then_inc(att_ok, 1)
                        pool.wait_ge(att_ok, u + 1)
                        if g == 0 and u // 2 + SLOTS + 1 < NH:
                            stage(u // 2 + SLOTS + 1)
                    for t in range(TT + 2):
                        if t < TT:
                            pool.wait_ge(z1_ok, t + 1)
                            pool.tensor_tensor(xs[:, t, :], xs[:, t, :], bmo[:], ALU.add).then_inc(z_ok, 1)
                            pool.wait_ge(zvar, t + 1)
                            pool.wait_ge(z_ok, t + 1)
                            pool.tensor_tensor(rstd[:, t:t + 1], rstd[:, t:t + 1], neg_half[:, 0:1], ALU.pow)\
                                .then_inc(zrstd, 1)
                            pool.wait_ge(zrstd, t + 1)
                        if t >= 2:
                            u = t - 2
                            pool.wait_ge(ge_ok, u + 1)
                            pool.tensor_tensor(ot[:, u % 3, :], ot[:, u % 3, :], xs[:, u, :], ALU.add).then_inc(out_ok, 1)
                            pool.wait_ge(out_ok, u + 1)

        with nc.Fori(0, n_images) as i:
            image(i)
            nc.all_engine_barrier(sems_to_clear=range(min(nums), max(nums) + 1))


_INS = ["x", "L0_conv_gn_scale", "L0_conv_gn_bias", "L0_conv_w_qkv", "L0_conv_b_qkv", "L0_conv_w_out", "L0_conv_b_out",
        "L1_conv_ln_g", "L1_conv_ln_b", "L1_conv_wq", "L1_conv_bq", "L1_conv_wv", "L1_conv_bv", "L1_conv_dw_w",
        "L1_conv_dw_b", "L1_conv_pw_w", "L1_conv_mq_w", "L1_conv_mq_b", "L1_conv_mk_w", "L1_conv_mk_b",
        "L1_conv_mv_w", "L1_conv_mv_b", "L1_conv_mo_w", "L1_conv_mo_b", "L1_conv_mlp_w", "L1_conv_mlp_b"]


def build(nc, a, out, n_images=B):
    x2 = nc.dram_tensor("x2", [B, TOK, C], F32, kind="Internal").ap()
    l0 = [a["L0_conv_" + n] for n in ("gn_scale", "gn_bias", "w_qkv", "b_qkv", "w_out", "b_out")]
    layer0(nc, a["x"].rearrange("b h w c -> b (h w) c"), *l0, x2, n_images)
    l1 = {n: a["L1_conv_" + n] for n in ("ln_g", "ln_b", "wq", "bq", "wv", "bv", "dw_w", "dw_b", "pw_w", "mq_w", "mq_b",
                                         "mk_w", "mk_b", "mv_w", "mv_b", "mo_w", "mo_b", "mlp_w", "mlp_b")}
    l1["dw_w"] = l1["dw_w"].rearrange("c o y x -> c (o y x)")
    l1["pw_w"] = l1["pw_w"].rearrange("k c y x -> k (c y x)")
    layer1(nc, x2, *l1.values(), out.rearrange("b h w c -> b (h w) c"), n_images)


def kernel(**inputs):
    import numpy as _np
    import concourse.bacc as _bacc
    from concourse.bass_utils import run_bass_kernel_spmd as _run

    nc = _bacc.Bacc("TRN2", target_bir_lowering=False, num_devices=1)
    arrays, args = {}, {}
    for name in _INS:
        arr = _np.ascontiguousarray(inputs[name])
        arrays[f"in_{name}"] = arr
        args[name] = nc.dram_tensor(f"in_{name}", arr.shape, mybir.dt.from_np(arr.dtype), kind="ExternalInput").ap()
    out = nc.dram_tensor("out_0", (B, HW, HW, C), F32, kind="ExternalOutput").ap()
    build(nc, args, out)
    r = _run(nc, [arrays], core_ids=[0])
    return r.results[0]["out_0"]
```

```python
from contextlib import ExitStack

import concourse.bass as bass
from concourse import mybir

F32 = mybir.dt.float32
F32R = mybir.dt.float32r
ACT = mybir.ActivationFunctionType
ALU = mybir.AluOpType
AX = mybir.AxisListType.X

P = 128
B = 8
TOK = 1024
C = 512
CT = C // P
TT = TOK // P
NH = 8
HD = C // NH
HALF = TOK // 2
HW = 32
GRID = 16
NS = GRID * GRID
KS = 7
PADW = HW + KS - 1
SB_START = 16512
SB_END = 229344


class Region:

    def __init__(self, nc, start, end):
        self.nc, self.at, self.end = nc, start, end

    def take(self, name, shape, dt=F32):
        size = 4
        for n in shape[1:]:
            size *= n
        size = (size + 31) // 32 * 32
        assert self.at + size <= self.end, (name, self.at + size - self.end)
        t = self.nc.alloc_sbuf_tensor_at(name, shape, dt, offset=self.at)
        self.at += size
        return t


def raw(ap):
    return ap.bitcast(F32)


def own_half(h):
    return slice(HD * (h % 2), HD * (h % 2) + HD)


def other_half(h):
    return slice(HD * (1 - h % 2), HD * (1 - h % 2) + HD)


def v_hi(tile):
    return tile.rearrange("p (q f d) -> p q f d", q=NH // 2, f=4)[:, :, 0:4:3, :]


def v_lo(tile):
    return tile.rearrange("p (q f d) -> p q f d", q=NH // 2, f=4)[:, :, 1:3, :]


def by_head(ap):
    return ap.rearrange("p (q e d) -> p q e d", q=NH // 2, e=2)


def make_identity(pool, ident, done):
    pool.memset(ident[:], 0.0).then_inc(done, 1)
    pool.wait_ge(done, 1)
    pool.affine_select(out=ident[:], in_=ident[:], compare_op=ALU.not_equal, fill=1.0, base=0,
                       pattern=[[-1, P]], channel_multiplier=1).then_inc(done, 1)


def layer0(nc, x, gn_scale, gn_bias, w_qkv, b_qkv, w_out, b_out, x2, n_images=B):
    NB = TOK // 256
    U = NH * TT
    QSCALE = 1.0 / HD

    with ExitStack() as ctx:
        def sem(name):
            return ctx.enter_context(nc.semaphore("a_" + name))

        ps = ctx.enter_context(nc.psum_tensor("a_ps", [P, 8, 512], F32))
        R = Region(nc, SB_START, SB_END)
        wqh = R.take("wqkv_hi", [P, CT, 3 * C], F32R)
        wql = R.take("wqkv_lo", [P, CT, 3 * C], F32R)
        woh = R.take("wout_hi", [P, CT, C], F32R)
        wol = R.take("wout_lo", [P, CT, C], F32R)
        ident = R.take("a_ident", [P, P])
        group = R.take("a_group", [P, P])
        bout = R.take("a_bout", [P, C])
        vec = R.take("a_vec", [P, 20])
        bq = R.take("a_bq", [P, CT])
        neg_half = R.take("a_neg_half", [P, CT])
        small = R.take("a_small", [P, 40])
        bn = R.take("a_bn", [P, CT, 2, 6])
        neg_max = R.take("a_neg_max", [P, U])
        row_sum = R.take("a_row_sum", [P, U])
        row_inv = R.take("a_row_inv", [P, U])
        tok = R.take("a_tok", [P, 3, C])
        fold_t = R.take("a_fold_t", [P, 256])
        fold_r = R.take("a_fold_r", [P, 2, 256])
        fold_s = R.take("a_fold_s", [P, 2, 256])
        qk = R.take("a_qk", [P, 2 * CT, TOK])
        v = R.take("a_v", [P, TT, NH * P], F32R)
        qs = R.take("a_qs", [P, 2, TOK], F32R)
        kh = R.take("a_kh", [P, 2, TOK], F32R)
        kl = R.take("a_kl", [P, 2, TOK], F32R)
        work = R.at
        prob = R.take("a_prob", [P, 2, TOK])
        split = R.at
        ph = R.take("a_ph", [P, 2, TT, 256], F32R)
        pl = R.take("a_pl", [P, 2, TT, 256], F32R)
        S = Region(nc, split, SB_END)
        xh = S.take("a_xh", [P, CT, TOK], F32R)
        xl = S.take("a_xl", [P, CT, TOK], F32R)
        xt = Region(nc, work - 16384 - 8192, SB_END).take("a_xt", [P, CT, TOK])
        W = Region(nc, work - 60000 // 32 * 32, SB_END)
        wq_raw = W.take("a_wq_raw", [P, CT, 3 * C])
        wo_raw = W.take("a_wo_raw", [P, CT, C])
        rows = W.take("a_rows", [20, P])
        bo_raw = W.take("a_bo_raw", [P, C])
        bv_wide = W.take("a_bv_wide", [P, CT, P])

        ld, cst, spl, pe_s, chn = sem("s_ld"), sem("s_cst"), sem("s_spl"), sem("s_pe"), sem("s_chn")
        with nc.Block() as block:
            @block.sync
            def _(sp):
                sp.dma_start(wq_raw[:], w_qkv.rearrange("(t p) n -> p t n", p=P)).then_inc(ld, 16)
                sp.dma_start(wo_raw[:], w_out.rearrange("(t p) n -> p t n", p=P)).then_inc(ld, 16)
                sp.dma_start(rows[0:4, :], gn_scale.rearrange("(t p) -> t p", p=P)).then_inc(ld, 16)
                sp.dma_start(rows[4:8, :], gn_bias.rearrange("(t p) -> t p", p=P)).then_inc(ld, 16)
                sp.dma_start(rows[8:20, :], b_qkv.rearrange("(t p) -> t p", p=P)).then_inc(ld, 16)
                sp.dma_start(bo_raw[:], b_out.partition_broadcast(P)).then_inc(ld, 16)

            @block.gpsimd
            def _(pool):
                make_identity(pool, ident, cst)
                pool.memset(group[:], 1.0 / 16).then_inc(cst, 1)
                pool.memset(neg_half[:], -0.5).then_inc(cst, 1)
                blocks = group[:].rearrange("p (g j) -> p g j", j=16)
                pool.wait_ge(cst, 3)
                pool.affine_select(out=blocks, in_=blocks, compare_op=ALU.is_ge, fill=0.0, base=0,
                                   pattern=[[-16, 8], [0, 16]], channel_multiplier=1).then_inc(cst, 1)
                pool.wait_ge(cst, 5)
                pool.affine_select(out=blocks, in_=blocks, compare_op=ALU.is_ge, fill=0.0, base=15,
                                   pattern=[[16, 8], [0, 16]], channel_multiplier=-1).then_inc(cst, 1)

            @block.scalar
            def _(act):
                act.wait_ge(ld, 96)
                act.activation(wqh[:], wq_raw[:], ACT.Copy).then_inc(spl, 1)
                act.activation(woh[:], wo_raw[:], ACT.Copy).then_inc(spl, 1)

            @block.tensor
            def _(pe):
                pe.wait_ge(ld, 96)
                pe.wait_ge(cst, 2)
                pe.transpose(ps[:, 0, 0:20], rows[:], ident[0:20, 0:20]).then_inc(pe_s, 1)
                pe.wait_ge(chn, 3)
                for k in range(CT):
                    mm = pe.matmul(ps[:, 1, :], bv_wide[:, k, :], wo_raw[:, k, :], start=k == 0, stop=k == CT - 1)
                mm.then_inc(pe_s, 1)

            @block.vector
            def _(dve):
                dve.wait_ge(pe_s, 1)
                dve.tensor_copy(vec[:], ps[:, 0, 0:20]).then_inc(chn, 1)
                dve.wait_ge(chn, 1)
                dve.tensor_scalar(bq[:], vec[:, 8:12], QSCALE, None, ALU.mult).then_inc(chn, 1)
                dve.tensor_copy(bv_wide[:], vec[:, 16:20].unsqueeze(2).to_broadcast([P, CT, P])).then_inc(chn, 1)
                dve.wait_ge(spl, 1)
                dve.tensor_tensor(wql[:], wq_raw[:], raw(wqh[:]), ALU.subtract).then_inc(chn, 1)
                dve.wait_ge(spl, 2)
                dve.tensor_tensor(wol[:], wo_raw[:], raw(woh[:]), ALU.subtract).then_inc(chn, 1)
                dve.wait_ge(pe_s, 2)
                dve.tensor_tensor(bout[:], ps[:, 1, :], bo_raw[:], ALU.add).then_inc(chn, 1)

        x_ld = [sem(f"x_ld{i}") for i in range(3)]
        r_ld = [sem(f"r_ld{i}") for i in range(3)]
        o_st = [sem(f"o_st{i}") for i in range(3)]
        s_ld = [sem(f"s_ld{i}") for i in range(2)]
        xt_ps, xt_sb, bn_ok, bn_ag = sem("xt_ps"), sem("xt_sb"), sem("bn_ok"), sem("bn_ag")
        st_ok, st_ps, var_ok, rstd_ok = sem("st_ok"), sem("st_ps"), sem("var_ok"), sem("rstd_ok")
        chain = sem("chain")
        xn_ok, xh_ok, xl_ok = sem("xn_ok"), sem("xh_ok"), sem("xl_ok")
        pr_ps, qk_sb, vh_ok, vl_ok = sem("pr_ps"), sem("qk_sb"), sem("vh_ok"), sem("vl_ok")
        staged, score, max_ok, exp_ok = sem("staged"), sem("score"), sem("max_ok"), sem("exp_ok")
        tr_ps, ph_ok, pl_ok, inv_ok = sem("tr_ps"), sem("ph_ok"), sem("pl_ok"), sem("inv_ok")
        av_ps, fold_cp, fold_add, att_ok = sem("av_ps"), sem("fold_cp"), sem("fold_add"), sem("att_ok")
        ah_ok, al_ok, out_ps, res_ok, out_ok = sem("ah_ok"), sem("al_ok"), sem("out_ps"), sem("res_ok"), sem("out_ok")
        cleared = [*x_ld, *r_ld, *o_st, *s_ld, xt_ps, xt_sb, bn_ok, bn_ag, st_ok, st_ps, var_ok, rstd_ok, chain,
                   xn_ok, xh_ok, xl_ok, pr_ps, qk_sb, vh_ok, vl_ok, staged, score, max_ok, exp_ok, tr_ps, ph_ok,
                   pl_ok, inv_ok, av_ps, fold_cp, fold_add, att_ok, ah_ok, al_ok, out_ps, res_ok, out_ok]
        nums = [s.num for s in cleared]
        assert sorted(nums) == list(range(min(nums), max(nums) + 1))

        groups = [("qk", m, s) for m in (0, 4) for s in range(2)] + [("v", t, 0) for t in range(TT)]
        groups += [("qk", m, s) for m in (1, 5, 2, 6, 3, 7) for s in range(2)]
        qk_upto = [sum(g[0] == "qk" for g in groups[:n]) for n in range(len(groups) + 1)]
        v_upto = [sum(g[0] == "v" for g in groups[:n]) for n in range(len(groups) + 1)]
        n_qk, n_v = qk_upto[-1], v_upto[-1]
        STAGE = 5

        def image(i):
            with nc.Block() as block:
                @block.sync
                def _(sp):
                    for t in range(TT):
                        if t >= 3:
                            sp.wait_ge(xt_ps, t - 2)
                        sp.dma_start(tok[:, t % 3, :], x[i, t * P:(t + 1) * P, :]).then_inc(x_ld[t % 3], 16)
                    for h in range(NH):
                        p, j = h // 2, h % 2
                        sp.wait_ge(qk_sb, 4 if p == 0 else 4 + 4 * p)
                        if h >= 2:
                            sp.wait_ge(score, TT * (h - 1))
                        else:
                            sp.wait_ge(xl_ok, CT)
                        for half in range(2):
                            rows_ = slice(HD * half, HD * half + HD)
                            sp.dma_start(raw(qs[rows_, j, :]), qk[own_half(h), p, :]).then_inc(s_ld[j], 16)
                            sp.dma_start(raw(kl[rows_, j, :]), qk[own_half(h), CT + p, :]).then_inc(s_ld[j], 16)
                        if h == 1:
                            sp.wait_ge(xt_ps, TT)
                            for t in range(3):
                                sp.dma_start(tok[:, t, :], x[i, t * P:(t + 1) * P, :]).then_inc(r_ld[t], 16)
                    for t in range(TT):
                        sp.wait_ge(out_ok, t + 1)
                        sp.dma_start(x2[i, t * P:(t + 1) * P, :], tok[:, t % 3, :]).then_inc(o_st[t % 3], 16)
                        if t + 3 < TT:
                            sp.wait_ge(o_st[t % 3], 16 * (t // 3 + 1))
                            sp.dma_start(tok[:, t % 3, :], x[i, (t + 3) * P:(t + 4) * P, :])\
                                .then_inc(r_ld[t % 3], 16)
                    for t in range(3):
                        sp.wait_ge(o_st[t], 16 * ((TT - t + 2) // 3))

                @block.tensor
                def _(pe):
                    for t in range(TT):
                        pe.wait_ge(x_ld[t % 3], 16 * (t // 3 + 1))
                        for c in range(CT):
                            mm = pe.transpose(ps[:, 4 * (t // 4) + c, (t % 4) * P:(t % 4 + 1) * P],
                                              tok[:, t % 3, c * P:(c + 1) * P], ident[:])
                        mm.then_inc(xt_ps, 1)
                    pe.wait_ge(st_ok, 2)
                    pe.wait_ge(xt_sb, 2 * CT)
                    pe.matmul(ps[:, 7, 0:8], group[:], small[:, 0:8], start=True, stop=True).then_inc(st_ps, 1)

                    pe.wait_ge(xh_ok, CT)
                    pe.wait_ge(xl_ok, CT)
                    for g, (kind, m, s) in enumerate(groups):
                        if g >= 8:
                            pe.wait_ge(qk_sb, qk_upto[g - 7])
                            if v_upto[g - 7]:
                                pe.wait_ge(vl_ok, v_upto[g - 7])
                        bank = ps[:, g % 8, :]
                        for k in range(CT):
                            if kind == "qk":
                                w = slice(m * P, (m + 1) * P)
                                n = slice(s * HALF, (s + 1) * HALF)
                                pairs = ((wqh[:, k, w], xh[:, k, n]), (wqh[:, k, w], xl[:, k, n]),
                                         (wql[:, k, w], xh[:, k, n]))
                            else:
                                w = slice(2 * C, 3 * C)
                                n = slice(m * P, (m + 1) * P)
                                pairs = ((xh[:, k, n], wqh[:, k, w]), (xh[:, k, n], wql[:, k, w]),
                                         (xl[:, k, n], wqh[:, k, w]))
                            for e, (a, b) in enumerate(pairs):
                                mm = pe.matmul(bank, a, b, start=k == 0 and e == 0, stop=k == CT - 1 and e == 2)
                        mm.then_inc(pr_ps, 1)

                    pe.wait_ge(qk_sb, n_qk)
                    pe.wait_ge(vl_ok, n_v)
                    for i_ in range(U + 7):
                        if i_ >= 5:
                            b, part = (i_ - 5) // 2, (i_ - 5) % 2
                            if b < U // 2:
                                h = b // NB
                                if part == 0:
                                    pe.wait_ge(inv_ok, b + 1)
                                    if b >= 2:
                                        pe.wait_ge(fold_add, b - 1)
                                        pe.wait_ge(fold_cp, 2 * b - 2)
                                    for n in range(2):
                                        u = 2 * b + n
                                        pe.transpose(ps[:, 6 + b % 2, 256 + n * P:256 + (n + 1) * P],
                                                     row_inv[:, u:u + 1].to_broadcast([P, P]), ident[:])
                                pe.wait_ge(pl_ok, 4 * b + 3 + part)
                                for kt in range(4 * part, 4 * part + 4):
                                    for e, q_ in enumerate((ph, pl)):
                                        mm = pe.matmul(ps[:, 6 + b % 2, 0:256], v[:, kt, h * P:(h + 1) * P], q_[:, b % 2, kt, :],
                                                       start=kt == 0 and e == 0, stop=kt == TT - 1 and e == 1)
                                if part == 1:
                                    mm.then_inc(av_ps, 1)
                        if i_ < U:
                            h, t = i_ // TT, i_ % TT
                            j = h % 2
                            if t == 0:
                                pe.wait_ge(staged, STAGE * (h + 1))
                            if i_ >= 2:
                                pe.wait_ge(exp_ok, i_ - 1)
                            for kb in range(2):
                                bank = ps[:, 2 * (i_ % 2) + kb, :]
                                q_ = qs[:, j, t * P:(t + 1) * P]
                                n = slice(kb * 512, (kb + 1) * 512)
                                pe.matmul(bank, q_, kh[:, j, n], start=True, stop=False)
                                mm = pe.matmul(bank, q_, kl[:, j, n], start=False, stop=True)
                            mm.then_inc(score, 1)
                        if 2 <= i_ < U + 2:
                            u = i_ - 2
                            pe.wait_ge(exp_ok, u + 1)
                            for g in range(2):
                                n = 2 * u + g
                                if n >= 2:
                                    pe.wait_ge(pl_ok, n - 1)
                                for kk in range(4):
                                    kt = 4 * g + kk
                                    mm = pe.transpose(ps[:, 4 + n % 2, kk * P:(kk + 1) * P],
                                                      prob[:, u % 2, kt * P:(kt + 1) * P], ident[:])
                                mm.then_inc(tr_ps, 1)

                    pe.wait_ge(fold_add, U // 2)
                    pe.wait_ge(fold_cp, U)
                    for t in range(TT):
                        if t == 0:
                            pe.wait_ge(ah_ok, CT)
                            pe.wait_ge(al_ok, CT)
                        n = slice(t * P, (t + 1) * P)
                        for k in range(CT):
                            for e, (a, b) in enumerate(((xh[:, k, n], woh[:, k, :]), (xh[:, k, n], wol[:, k, :]),
                                                        (xl[:, k, n], woh[:, k, :]))):
                                mm = pe.matmul(ps[:, t, :], a, b, start=k == 0 and e == 0, stop=k == CT - 1 and e == 2)
                        mm.then_inc(out_ps, 1)

                @block.scalar
                def _(act):
                    for s in range(2):
                        act.wait_ge(xt_ps, 4 * s + 4)
                        for c in range(CT):
                            act.activation(xt[:, c, s * HALF:(s + 1) * HALF], ps[:, 4 * s + c, :], ACT.Copy)\
                                .then_inc(xt_sb, 1)
                    for c in range(CT):
                        act.wait_ge(xn_ok, c + 1)
                        act.activation(xh[:, c, :], xt[:, c, :], ACT.Copy).then_inc(xh_ok, 1)
                    for g, (kind, m, s) in enumerate(groups):
                        act.wait_ge(pr_ps, g + 1)
                        if kind == "v":
                            act.activation(v_hi(v[:, m, :]), by_head(ps[:, g % 8, :]), ACT.Copy).then_inc(vh_ok, 1)
                        elif m < CT:
                            act.activation(qk[:, m, s * HALF:(s + 1) * HALF], ps[:, g % 8, :], ACT.Identity,
                                           bias=bq[:, m:m + 1], scale=QSCALE).then_inc(qk_sb, 1)
                        else:
                            act.activation(qk[:, m, s * HALF:(s + 1) * HALF], ps[:, g % 8, :], ACT.Identity,
                                           bias=vec[:, 8 + m:9 + m]).then_inc(qk_sb, 1)
                    for i_ in range(U + 7):
                        if 6 <= i_ <= U + 4 and i_ % 2 == 0:
                            b = (i_ - 6) // 2
                            h = b // NB
                            act.wait_ge(av_ps, b + 1)
                            if b >= 1:
                                act.wait_ge(fold_add, b)
                            act.activation(fold_t[own_half(h), :], ps[other_half(h), 6 + b % 2, 0:256], ACT.Copy)\
                                .then_inc(fold_cp, 1)
                            if b >= 2:
                                act.wait_ge(att_ok, b - 1)
                            act.activation(fold_r[own_half(h), b % 2, :], ps[own_half(h), 6 + b % 2, 256:512], ACT.Copy)\
                                .then_inc(fold_cp, 1)
                        if 2 <= i_ < U + 2:
                            u = i_ - 2
                            b = u // 2
                            for g in range(2):
                                n = 2 * u + g
                                act.wait_ge(tr_ps, n + 1)
                                if b >= 2:
                                    act.wait_ge(av_ps, b - 1)
                                act.activation(ph[:, b % 2, 4 * g:4 * g + 4, (u % 2) * P:(u % 2 + 1) * P],
                                               ps[:, 4 + n % 2, :].rearrange("p (k q) -> p k q", k=4),
                                               ACT.Copy).then_inc(ph_ok, 1)
                        if i_ < U:
                            act.wait_ge(max_ok, i_ + 1)
                            if i_ >= 2:
                                act.wait_ge(tr_ps, 2 * i_ - 2)
                            act.activation(prob[:, i_ % 2, :], ps[:, 2 * (i_ % 2):2 * (i_ % 2) + 2, :]
                                           .rearrange("p a b -> p (a b)"), ACT.Exp,
                                           bias=neg_max[:, i_:i_ + 1], accum_out=row_sum[:, i_:i_ + 1]).then_inc(exp_ok, 1)
                    for c in range(CT):
                        act.wait_ge(att_ok, 2 * NB * (c + 1))
                        act.activation(xh[:, c, :], qk[:, c, :], ACT.Copy).then_inc(ah_ok, 1)

                @block.vector
                def _(dve):
                    steps = [0]

                    def link(ins):
                        steps[0] += 1
                        ins.then_inc(chain, 1)
                        dve.wait_ge(chain, steps[0])

                    for s in range(2):
                        for c in range(CT):
                            dve.wait_ge(xt_sb, s * CT + c + 1)
                            dve.bn_stats(bn[:, c, s, :], xt[:, c, s * HALF:(s + 1) * HALF]).then_inc(bn_ok, 1)
                    dve.wait_ge(bn_ok, 2 * CT)
                    mv = small[:, 8:16].rearrange("p (c m) -> p c m", m=2)
                    for c in range(CT):
                        dve.bn_aggr(mv[:, c, :], bn[:, c, :, :].rearrange("p s k -> p (s k)")).then_inc(bn_ag, 1)
                    dve.wait_ge(bn_ag, CT)
                    link(dve.tensor_tensor(small[:, 16:20], mv[:, :, 0], mv[:, :, 0], ALU.mult))
                    dve.tensor_copy(small[:, 0:4], mv[:, :, 0]).then_inc(st_ok, 1)
                    dve.tensor_tensor(small[:, 4:8], small[:, 16:20], mv[:, :, 1], ALU.add).then_inc(st_ok, 1)
                    dve.wait_ge(st_ps, 1)
                    link(dve.tensor_copy(small[:, 20:28], ps[:, 7, 0:8]))
                    link(dve.tensor_tensor(small[:, 28:32], small[:, 20:24], small[:, 20:24], ALU.mult))
                    link(dve.tensor_tensor(small[:, 28:32], small[:, 24:28], small[:, 28:32], ALU.subtract))
                    dve.tensor_scalar(small[:, 28:32], small[:, 28:32], 0.0, 1e-6, ALU.max, ALU.add).then_inc(var_ok, 1)
                    dve.wait_ge(rstd_ok, 1)
                    link(dve.tensor_tensor(small[:, 32:36], small[:, 32:36], vec[:, 0:4], ALU.mult))
                    link(dve.tensor_tensor(small[:, 36:40], small[:, 20:24], small[:, 32:36], ALU.mult))
                    link(dve.tensor_tensor(small[:, 36:40], vec[:, 4:8], small[:, 36:40], ALU.subtract))
                    for c in range(CT):
                        dve.tensor_scalar(xt[:, c, :], xt[:, c, :], small[:, 32 + c:33 + c], small[:, 36 + c:37 + c],
                                          ALU.mult, ALU.add).then_inc(xn_ok, 1)
                    for c in range(CT):
                        dve.wait_ge(xh_ok, c + 1)
                        dve.tensor_tensor(xl[:, c, :], xt[:, c, :], raw(xh[:, c, :]), ALU.subtract).then_inc(xl_ok, 1)
                    for g, (kind, m, s) in enumerate(groups):
                        if kind == "v":
                            dve.wait_ge(vh_ok, m + 1)
                            dve.tensor_tensor(v_lo(v[:, m, :]), by_head(ps[:, g % 8, :]), raw(v_hi(v[:, m, :])),
                                              ALU.subtract).then_inc(vl_ok, 1)
                    for i_ in range(U + 7):
                        if i_ < U:
                            dve.wait_ge(score, i_ + 1)
                            dve.tensor_reduce(neg_max[:, i_:i_ + 1], ps[:, 2 * (i_ % 2):2 * (i_ % 2) + 2, :]
                                              .rearrange("p a b -> p (a b)"), AX, ALU.max, negate=True).then_inc(max_ok, 1)
                        if 6 <= i_ <= U + 4 and i_ % 2 == 0:
                            b = (i_ - 6) // 2
                            h = b // NB
                            dve.wait_ge(fold_cp, 2 * b + 2)
                            if b >= 2:
                                dve.wait_ge(att_ok, b - 1)
                            dve.tensor_tensor(fold_s[own_half(h), b % 2, :], ps[own_half(h), 6 + b % 2, 0:256],
                                              fold_t[own_half(h), :], ALU.add).then_inc(fold_add, 1)
                        if 2 <= i_ < U + 2:
                            u = i_ - 2
                            b = u // 2
                            for g in range(2):
                                n = 2 * u + g
                                here = (slice(None), b % 2, slice(4 * g, 4 * g + 4), slice((u % 2) * P, (u % 2 + 1) * P))
                                dve.wait_ge(ph_ok, n + 1)
                                dve.tensor_tensor(pl[here], ps[:, 4 + n % 2, :].rearrange("p (k q) -> p k q", k=4),
                                                  raw(ph[here]), ALU.subtract).then_inc(pl_ok, 1)
                            if u % 2 == 1:
                                dve.wait_ge(exp_ok, u + 1)
                                dve.reciprocal(row_inv[:, u - 1:u + 1], row_sum[:, u - 1:u + 1]).then_inc(inv_ok, 1)
                    for c in range(CT):
                        dve.wait_ge(ah_ok, c + 1)
                        dve.tensor_tensor(xl[:, c, :], qk[:, c, :], raw(xh[:, c, :]), ALU.subtract).then_inc(al_ok, 1)
                    for t in range(TT):
                        dve.wait_ge(out_ps, t + 1)
                        dve.wait_ge(res_ok, t + 1)
                        dve.tensor_tensor(tok[:, t % 3, :], ps[:, t, :], tok[:, t % 3, :], ALU.add).then_inc(out_ok, 1)

                @block.gpsimd
                def _(pool):
                    pool.wait_ge(var_ok, 1)
                    pool.tensor_tensor(small[:, 32:36], small[:, 28:32], neg_half[:], ALU.pow).then_inc(rstd_ok, 1)

                    def stage(h, parts):
                        j, n = h % 2, STAGE * h
                        hi = kh[:, j, :]
                        if 0 in parts:
                            pool.wait_ge(s_ld[j], 64 * (h // 2 + 1))
                            pool.tensor_scalar(hi, raw(qs[:, j, :]), 1.0, 0.0, ALU.mult, ALU.add).then_inc(staged, 1)
                            pool.wait_ge(staged, n + 1)
                            pool.tensor_tensor(qs[HD:P, j, :], raw(qs[HD:P, j, :]), raw(hi[HD:P, :]), ALU.subtract)\
                                .then_inc(staged, 1)
                            pool.wait_ge(staged, n + 2)
                        if 1 in parts:
                            pool.tensor_scalar(qs[0:HD, j, :], raw(hi[0:HD, :]), 1.0, 0.0, ALU.mult, ALU.add)\
                                .then_inc(staged, 1)
                            pool.wait_ge(staged, n + 3)
                            pool.tensor_scalar(hi, raw(kl[:, j, :]), 1.0, 0.0, ALU.mult, ALU.add).then_inc(staged, 1)
                            pool.wait_ge(staged, n + 4)
                        if 2 in parts:
                            pool.tensor_tensor(kl[:, j, :], raw(kl[:, j, :]), raw(hi), ALU.subtract).then_inc(staged, 1)
                            pool.wait_ge(staged, n + 5)

                    stage(0, (0, 1, 2))
                    stage(1, (0, 1, 2))
                    for b in range(U // 2):
                        h = b // NB
                        pool.wait_ge(fold_add, b + 1)
                        pool.wait_ge(fold_cp, 2 * b + 2)
                        pool.tensor_tensor(qk[own_half(h), h // 2, (b % NB) * 256:(b % NB + 1) * 256],
                                           fold_s[own_half(h), b % 2, :], fold_r[own_half(h), b % 2, :],
                                           ALU.mult).then_inc(att_ok, 1)
                        pool.wait_ge(att_ok, b + 1)
                        k, part = (b + 2) // NB, (b + 2) % NB
                        if 1 <= k <= NH - 2 and part < 3:
                            stage(k + 1, (part,))
                    for t in range(TT):
                        pool.wait_ge(r_ld[t % 3], 16 * (t // 3 + 1))
                        pool.tensor_tensor(tok[:, t % 3, :], tok[:, t % 3, :], bout[:], ALU.add).then_inc(res_ok, 1)

        with nc.Fori(0, n_images) as i:
            image(i)
            nc.all_engine_barrier(sems_to_clear=range(min(nums), max(nums) + 1))


def layer1(nc, x2, ln_g, ln_b, wq, bq, wv, bv, dw_w, dw_b, pw_w, mq_w, mq_b, mk_w, mk_b, mv_w, mv_b,
           mo_w, mo_b, mlp_w, mlp_b, out, n_images=B):
    NK = NS
    KT = NK // P
    QG = 4
    GR = TT // QG
    U = NH * GR
    SLOTS = 4
    DIAGS = 16
    DVE_TAPS = [29, 29, 28, 28]
    SOLO = 20
    left = [[(c, n) for n in range(DVE_TAPS[c])] + [(c, None)] for c in range(CT)]
    taps = [left[0].pop(0) for _ in range(SOLO)]
    while any(left):
        for l in [l for l in left if l][:4]:
            taps.append(l.pop(0))
    tap_before = [max([m + 1 for m in range(k) if taps[m][0] == taps[k][0]], default=0) for k in range(len(taps))]
    taps_upto = [taps.index((c, None)) + 1 for c in range(CT)]
    pe_taps = [(c, n) for c in range(CT) for n in range(DVE_TAPS[c], KS * KS)]
    pe_upto = [sum(e[0] <= c for e in pe_taps) for c in range(CT)]

    with ExitStack() as ctx:
        def sem(name):
            return ctx.enter_context(nc.semaphore("b_" + name))

        ps = ctx.enter_context(nc.psum_tensor("b_ps", [P, 8, 512], F32))
        R = Region(nc, SB_START, SB_END)
        names = ("wq", "wqm", "wvk", "wvv", "mo", "mlp")
        wh = {n: R.take(f"b_{n}_hi", [P, CT, C], F32R) for n in names}
        wl = {n: R.take(f"b_{n}_lo", [P, CT, C], F32R) for n in names}
        ident = R.take("b_ident", [P, P])
        lng = R.take("b_lng", [P, C])
        lnb = R.take("b_lnb", [P, C])
        bqw = R.take("b_bqw", [P, C])
        bmo = R.take("b_bmo", [P, C])
        bmlp = R.take("b_bmlp", [P, C])
        refs = R.take("b_refs", [P, 2, NS])
        vec = R.take("b_vec", [P, 32])
        dww = R.take("b_dww", [P, CT, KS * KS])
        bqm = R.take("b_bqm", [P, CT])
        bkm = R.take("b_bkm", [P, CT])
        bvm = R.take("b_bvm", [P, CT])
        neg_x = R.take("b_neg_x", [P, 1])
        neg_y = R.take("b_neg_y", [P, TT])
        neg_half = R.take("b_neg_half", [P, CT])
        bn = R.take("b_bn", [P, TT, 6])
        mv = R.take("b_mv", [P, TT, 2])
        rstd = R.take("b_rstd", [P, TT])
        nbn = R.take("b_nbn", [P, TT, 6])
        zmv = R.take("b_zmv", [P, TT, 2])
        zrs = R.take("b_zrs", [P, TT])
        neg_max = R.take("b_neg_max", [P, U * QG])
        row_sum = R.take("b_row_sum", [P, U * QG])
        row_inv = R.take("b_row_inv", [P, U * QG])
        x_at = R.at
        xs = R.take("b_xs", [P, TT, C])
        q_at = R.at
        qh = R.take("b_qh", [P, CT, TOK], F32R)
        ql = R.take("b_ql", [P, CT, TOK], F32R)
        l_at = R.at
        xh, xl, ln = [], [], []
        for s in range(2):
            xh.append(R.take(f"b_xh{s}", [P, CT, C], F32R))
            ln.append(Region(nc, R.at, SB_END).take(f"b_ln{s}", [P, CT, C]))
            xl.append(R.take(f"b_xl{s}", [P, CT, C], F32R))
        t_at = R.at
        assert t_at + 16384 <= SB_END
        qpad = Region(nc, q_at, l_at).take("b_qpad", [P, CT, PADW * PADW])
        E = Region(nc, t_at, SB_END)
        acc = E.take("b_acc", [P, CT, NS])
        o = E.take("b_o", [P, CT, NS])
        diag = E.take("b_diag", [P, DIAGS, P])
        E = Region(nc, t_at, SB_END)
        ith = E.take("b_it_hi", [P, KT, 2, NK], F32R)
        itl = E.take("b_it_lo", [P, KT, 2, NK], F32R)
        hat = E.take("b_hat", [P, TT, NS])
        E = Region(nc, t_at, SB_END)
        xy = E.take("b_xy", [P, 2, NS])
        hx = E.take("b_hx", [P, NS])
        E = Region(nc, x_at, q_at)
        kch = E.take("b_kc_hi", [P, CT, NK], F32R)
        kcl = E.take("b_kc_lo", [P, CT, NK], F32R)
        vh = E.take("b_v_hi", [P, KT, C], F32R)
        vl = E.take("b_v_lo", [P, KT, C], F32R)
        E = Region(nc, l_at, t_at)
        kh = E.take("b_kh", [P, SLOTS, NK], F32R)
        kl = E.take("b_kl", [P, SLOTS, NK], F32R)
        prob = E.take("b_prob", [P, 2, QG, NK])
        qs = E.take("b_qs", [P, SLOTS, TOK], F32R)
        E = Region(nc, t_at, SB_END)
        ph = E.take("b_ph", [P, 2, KT, 512], F32R)
        pl = E.take("b_pl", [P, 2, KT, 512], F32R)
        z = Region(nc, l_at + 16384, t_at).take("b_z", [P, TT, C])
        E = Region(nc, t_at, SB_END)
        zn = E.take("b_zn", [P, 2, C])
        zh = E.take("b_zh", [P, 2, CT, P], F32R)
        zl = E.take("b_zl", [P, 2, CT, P], F32R)
        ot = E.take("b_ot", [P, 2, C])
        W = Region(nc, x_at, SB_END)
        raws = {n: W.take(f"b_{n}_raw", [P, CT, C]) for n in ("wq", "mq", "wv", "mk", "mv", "mo", "mlp")}
        wqt = W.take("b_wq_t", [P, CT, C])
        wvt = W.take("b_wv_t", [P, CT, C])
        rows = W.take("b_rows", [32, P])
        wide = W.take("b_wide", [P, CT, P])
        bo_raw = W.take("b_bo_raw", [P, C])
        assert W.at <= SB_END

        ld, cst, hi_ok, lo_ok, pe_s, chn = (sem("s_" + n) for n in ("ld", "cst", "hi", "lo", "pe", "chn"))
        wt_sb = sem("s_wt")
        with nc.Block() as block:
            @block.sync
            def _(sp):
                for n, w in (("wq", wq), ("mq", mq_w), ("wv", wv), ("mk", mk_w), ("mv", mv_w), ("mo", mo_w),
                             ("mlp", mlp_w)):
                    sp.dma_start(raws[n][:], w.rearrange("(t p) n -> p t n", p=P)).then_inc(ld, 16)
                for n, vv in enumerate((bq, bv, mq_b, mk_b, mv_b)):
                    sp.dma_start(rows[4 * n:4 * n + 4, :], vv.rearrange("(t p) -> t p", p=P)).then_inc(ld, 16)
                sp.dma_start(rows[20:28, :], pw_w.rearrange("k (t p) -> (k t) p", p=P)).then_inc(ld, 16)
                sp.dma_start(rows[28:32, :], dw_b.rearrange("(t p) -> t p", p=P)).then_inc(ld, 16)
                sp.dma_start(dww[:], dw_w.rearrange("(t p) k -> p t k", p=P)).then_inc(ld, 16)
                for d, s in ((lng, ln_g), (lnb, ln_b), (bqw, bq), (bo_raw, mo_b), (bmlp, mlp_b)):
                    sp.dma_start(d[:], s.partition_broadcast(P)).then_inc(ld, 16)
                sp.wait_ge(ld, 20 * 16)

            @block.gpsimd
            def _(pool):
                make_identity(pool, ident, cst)
                pool.memset(neg_half[:], -0.5).then_inc(cst, 1)
                for g in range(4):
                    here = slice(32 * g, 32 * g + 32)
                    pool.wait_ge(cst, 3 + 2 * g)
                    pool.iota(neg_x[here, :], [[0, 1]], base=0, channel_multiplier=-1,
                              allow_small_or_imprecise_dtypes=True).then_inc(cst, 1)
                    pool.iota(neg_y[here, :], [[-4, TT]], base=-g, channel_multiplier=0,
                              allow_small_or_imprecise_dtypes=True).then_inc(cst, 1)
                pool.wait_ge(cst, 11)
                pool.iota(refs[:, 0, :], [[1, GRID], [0, GRID]], base=0, channel_multiplier=0,
                          allow_small_or_imprecise_dtypes=True).then_inc(cst, 1)
                pool.wait_ge(cst, 12)
                pool.iota(refs[:, 1, :], [[0, GRID], [1, GRID]], base=0, channel_multiplier=0,
                          allow_small_or_imprecise_dtypes=True).then_inc(cst, 1)

            products = (("wqm", wqt, "mq"), ("wvk", wvt, "mk"), ("wvv", wvt, "mv"))

            @block.scalar
            def _(act):
                act.wait_ge(ld, 20 * 16)
                for n in ("wq", "mo", "mlp"):
                    act.activation(wh[n][:], raws[n][:], ACT.Copy).then_inc(hi_ok, 1)
                for g in range(12):
                    n, j = products[g // 4][0], g % 4
                    act.wait_ge(pe_s, 9 + g + 1)
                    act.activation(wh[n][:, j, :], ps[:, g % 8, :], ACT.Copy).then_inc(hi_ok, 1)

            @block.tensor
            def _(pe):
                pe.wait_ge(ld, 20 * 16)
                pe.wait_ge(cst, 2)
                for w, n in enumerate(("wq", "wv")):
                    for k in range(CT):
                        for j in range(CT):
                            mm = pe.transpose(ps[:, 4 * w + k, j * P:(j + 1) * P],
                                              raws[n][:, j, k * P:(k + 1) * P], ident[:])
                        mm.then_inc(pe_s, 1)
                pe.wait_ge(wt_sb, 8)
                pe.transpose(ps[:, 0, 0:32], rows[:], ident[0:32, 0:32]).then_inc(pe_s, 1)
                for g in range(12):
                    n, wt, m = products[g // 4]
                    j = g % 4
                    pe.wait_ge(chn, 1)
                    if g >= 8:
                        pe.wait_ge(lo_ok, g - 7)
                    for k in range(CT):
                        mm = pe.matmul(ps[:, g % 8, :], wt[:, k, j * P:(j + 1) * P], raws[m][:, k, :],
                                       start=k == 0, stop=k == CT - 1)
                    mm.then_inc(pe_s, 1)
                pe.wait_ge(lo_ok, 12)
                for g, (at, m) in enumerate(((0, "mq"), (4, "mk"), (4, "mv"))):
                    for j in range(CT):
                        for k in range(CT):
                            mm = pe.matmul(ps[:, 5, 4 * g + j:4 * g + j + 1], raws[m][:, k, j * P:(j + 1) * P],
                                           vec[:, at + k:at + k + 1], start=k == 0, stop=k == CT - 1)
                mm.then_inc(pe_s, 1)
                pe.wait_ge(chn, 7)
                for k in range(CT):
                    mm = pe.matmul(ps[:, 6, :], wide[:, k, :], raws["mo"][:, k, :], start=k == 0, stop=k == CT - 1)
                mm.then_inc(pe_s, 1)

            @block.vector
            def _(dve):
                for g in range(8):
                    dve.wait_ge(pe_s, g + 1)
                    dve.tensor_copy((wqt if g < 4 else wvt)[:, g % 4, :], ps[:, g, :]).then_inc(wt_sb, 1)
                dve.wait_ge(pe_s, 9)
                dve.tensor_copy(vec[:], ps[:, 0, 0:32]).then_inc(chn, 1)
                for n, w in enumerate(("wq", "mo", "mlp")):
                    dve.wait_ge(hi_ok, n + 1)
                    dve.tensor_tensor(wl[w][:], raws[w][:], raw(wh[w][:]), ALU.subtract).then_inc(wt_sb, 1)
                for g in range(12):
                    n, j = products[g // 4][0], g % 4
                    dve.wait_ge(hi_ok, 3 + g + 1)
                    dve.tensor_tensor(wl[n][:, j, :], ps[:, g % 8, :], raw(wh[n][:, j, :]), ALU.subtract)\
                       .then_inc(lo_ok, 1)
                dve.wait_ge(cst, 13)
                dve.tensor_scalar(refs[:], refs[:], 0.5, 2.0 / GRID, ALU.add, ALU.mult).then_inc(chn, 1)
                dve.wait_ge(chn, 2)
                dve.tensor_scalar(refs[:], refs[:], -1.0, None, ALU.add).then_inc(chn, 1)
                dve.wait_ge(pe_s, 22)
                for g, (dst, at) in enumerate(((bqm, 8), (bkm, 12), (bvm, 16))):
                    dve.tensor_tensor(dst[:], ps[:, 5, 4 * g:4 * g + 4], vec[:, at:at + 4], ALU.add).then_inc(chn, 1)
                dve.wait_ge(chn, 6)
                dve.tensor_copy(wide[:], bvm[:].unsqueeze(2).to_broadcast([P, CT, P])).then_inc(chn, 1)
                dve.wait_ge(pe_s, 23)
                dve.tensor_tensor(bmo[:], ps[:, 6, :], bo_raw[:], ALU.add).then_inc(chn, 1)

        x_ld = [sem(f"x_ld{t}") for t in range(TT)]
        z_ld = [sem(f"z_ld{t}") for t in range(TT)]
        s_ld = [sem(f"s_ld{j}") for j in range(SLOTS)]
        o_st = [sem(f"o_st{j}") for j in range(2)]
        (bn_ok, bn_ag, var_ok, rstd_ok, ln1, ln_ok, xh_ok, xl_ok, pad_ok, q_ps, q_sb, dg_ok, dg_used, tap,
         gelu_ok, qh_ps, qh_sb, ql_sb, off_ps, tanh_ok, xy_ok, hx_ok, hy_ok, hat_ok, it_ps, ih_ok, il_ok, k_ps, k_sb,
         kl_sb, v_ps, vh_ok, vl_ok, score, max_ok, exp_ok, inv_ok, sc_ok, tr_ps, ph_ok, pl_ok, av_ps, ah_ok, al_ok,
         mo_ps, z1_ok, z_ok, zvar, zrstd, zn_ok, zt_ps, zh_ok, zl_ok, ml_ps, y_ok, ge_ok, out_ok, chain) = singles = [
            sem(n) for n in (
                "bn_ok bn_ag var_ok rstd_ok ln1 ln_ok xh_ok xl_ok pad_ok q_ps q_sb dg_ok dg_used tap "
                "gelu_ok qh_ps qh_sb ql_sb off_ps tanh_ok xy_ok hx_ok hy_ok hat_ok it_ps ih_ok il_ok k_ps k_sb "
                "kl_sb v_ps vh_ok vl_ok score max_ok exp_ok inv_ok sc_ok tr_ps ph_ok pl_ok av_ps ah_ok al_ok "
                "mo_ps z1_ok z_ok zvar zrstd zn_ok zt_ps zh_ok zl_ok ml_ps y_ok ge_ok out_ok chain").split()]
        nums = [s.num for s in [*x_ld, *z_ld, *s_ld, *o_st, *singles]]
        assert sorted(nums) == list(range(min(nums), max(nums) + 1))

        def centre(dve, t):
            return dve.scalar_tensor_tensor(ln[t // 4][:, t % 4, :], xs[:, t, :], mv[:, t, 0:1], lng[:],
                                            ALU.subtract, ALU.mult)

        def scale(dve, t):
            here = ln[t // 4][:, t % 4, :]
            return dve.scalar_tensor_tensor(here, here, rstd[:, t:t + 1], lnb[:], ALU.mult, ALU.add)

        def high(act, t):
            return act.activation(xh[t // 4][:, t % 4, :], ln[t // 4][:, t % 4, :], ACT.Copy)

        def low(dve, t):
            return dve.tensor_tensor(xl[t // 4][:, t % 4, :], ln[t // 4][:, t % 4, :], raw(xh[t // 4][:, t % 4, :]),
                                     ALU.subtract)

        with nc.Block() as block:
            @block.sync
            def _(sp):
                for t in range(TT):
                    sp.dma_start(xs[:, t, :], x2[0, t * P:(t + 1) * P, :]).then_inc(x_ld[t], 16)

            @block.vector
            def _(dve):
                for s in range(2):
                    for t in range(4 * s, 4 * s + 4):
                        dve.wait_ge(x_ld[t], 16)
                        dve.bn_stats(bn[:, t, :], xs[:, t, :]).then_inc(bn_ok, 1)
                    for t in range(4 * s, 4 * s + 4):
                        dve.wait_ge(bn_ok, t + 1)
                        dve.bn_aggr(mv[:, t, :], bn[:, t, :]).then_inc(bn_ag, 1)
                    dve.wait_ge(bn_ag, 4 * s + 4)
                    dve.tensor_scalar(rstd[:, 4 * s:4 * s + 4], mv[:, 4 * s:4 * s + 4, 1], 1e-5, None, ALU.add)\
                       .then_inc(var_ok, 1)
                for t in range(4):
                    centre(dve, t).then_inc(ln1, 1)
                dve.wait_ge(rstd_ok, 1)
                for t in range(4):
                    dve.wait_ge(ln1, t + 1)
                    scale(dve, t).then_inc(ln_ok, 1)
                for t in range(4):
                    dve.wait_ge(xh_ok, t + 1)
                    low(dve, t).then_inc(xl_ok, 1)

            @block.scalar
            def _(act):
                for t in range(4):
                    act.wait_ge(ln_ok, t + 1)
                    high(act, t).then_inc(xh_ok, 1)

            @block.gpsimd
            def _(pool):
                for s in range(2):
                    here = slice(4 * s, 4 * s + 4)
                    pool.wait_ge(var_ok, s + 1)
                    pool.tensor_tensor(rstd[:, here], rstd[:, here], neg_half[:], ALU.pow).then_inc(rstd_ok, 1)

        nc.all_engine_barrier(sems_to_clear=range(min(nums), max(nums) + 1))

        QH_BANK = (4, 5, 6, 0, 1, 2, 4, 5)
        IT_BANK = (7, 3)
        K_BANK = (6, 0, 1, 2)
        V_BANK = (7, 6)

        def image(i, after=None):
            with nc.Block() as block:
                @block.sync
                def _(sp):
                    def q_copies(h):
                        j = h % SLOTS
                        sp.dma_start(raw(qs[0:HD, j, :]), raw(qh[own_half(h), h // 2, :])).then_inc(s_ld[j], 16)
                        sp.dma_start(raw(qs[HD:P, j, :]), raw(ql[own_half(h), h // 2, :])).then_inc(s_ld[j], 16)

                    def k_copies(h):
                        j = h % SLOTS
                        for half in range(2):
                            rows_ = slice(HD * half, HD * half + HD)
                            sp.dma_start(raw(kh[rows_, j, :]), raw(kch[own_half(h), h // 2, :])).then_inc(s_ld[j], 16)
                            sp.dma_start(raw(kl[rows_, j, :]), raw(kcl[own_half(h), h // 2, :])).then_inc(s_ld[j], 16)

                    sp.wait_ge(qh_ps, 2 * CT)
                    for h in range(SLOTS):
                        sp.wait_ge(qh_sb, 2 * (h // 2) + 2)
                        sp.wait_ge(ql_sb, 2 * (h // 2) + 2)
                        q_copies(h)
                    for h in range(SLOTS):
                        sp.wait_ge(k_sb, h // 2 + 1)
                        sp.wait_ge(kl_sb, h // 2 + 1)
                        k_copies(h)
                    sp.wait_ge(qh_sb, 2 * CT)
                    sp.wait_ge(ql_sb, 2 * CT)
                    sp.wait_ge(k_sb, CT)
                    sp.wait_ge(kl_sb, CT)
                    for h in range(SLOTS, NH):
                        sp.wait_ge(score, GR * (h - SLOTS + 1))
                        q_copies(h)
                        k_copies(h)
                    for t in range(TT):
                        sp.wait_ge(score, GR * (NH - SLOTS + t // 2 + 1))
                        sp.dma_start(z[:, t, :], x2[i, t * P:(t + 1) * P, :]).then_inc(z_ld[t], 16)
                    if after is not None:
                        sp.wait_ge(av_ps, U)
                        for t in range(TT):
                            sp.dma_start(xs[:, t, :], after[i, t * P:(t + 1) * P, :]).then_inc(x_ld[t], 16)
                    for t in range(TT):
                        sp.wait_ge(out_ok, t + 1)
                        sp.dma_start(out[i, t * P:(t + 1) * P, :], ot[:, t % 2, :]).then_inc(o_st[t % 2], 16)
                    for t in range(2):
                        sp.wait_ge(o_st[t], 16 * (TT // 2))

                @block.tensor
                def _(pe):
                    def three(bank, left, right, first, last):
                        (lh, ll), (rh, rl) = left, right
                        for e, (a, b) in enumerate(((lh, rh), (lh, rl), (ll, rh))):
                            mm = pe.matmul(bank, a, b, start=first and e == 0, stop=last and e == 2)
                        return mm

                    for s in range(2):
                        for c in range(CT):
                            n = slice(c * P, (c + 1) * P)
                            for k in range(CT):
                                if s == 1 and c == 0:
                                    pe.wait_ge(xh_ok, k + 1)
                                    pe.wait_ge(xl_ok, k + 1)
                                mm = three(ps[:, 4 * s + c, :], (xh[s][:, k, n], xl[s][:, k, n]),
                                           (wh["wq"][:, k, :], wl["wq"][:, k, :]), k == 0, k == CT - 1)
                            mm.then_inc(q_ps, 1)
                    for e, (c, n) in enumerate(pe_taps):
                        first, last = n == DVE_TAPS[c], n == KS * KS - 1
                        if first:
                            pe.wait_ge(q_sb, CT + c + 1)
                        pe.wait_ge(dg_ok, e + 1)
                        dy, dx = n // KS, n % KS
                        src = qpad[:, c, :].rearrange("p (y x) -> p y x", x=PADW)[
                            :, dy:dy + 2 * GRID - 1:2, dx:dx + 2 * GRID - 1:2]
                        mm = pe.matmul(ps[:, c, 0:NS], diag[:, e % DIAGS, :], src, start=first, stop=last)
                        mm.then_inc(dg_used, 1)

                    def queries(groups):
                        for g in groups:
                            if g >= 6:
                                pe.wait_ge(qh_sb, g - 5)
                                pe.wait_ge(ql_sb, g - 5)
                            m, s = g // 2, g % 2
                            n = slice(m * P, (m + 1) * P)
                            for k in range(CT):
                                mm = three(ps[:, QH_BANK[g], :], (wh["wqm"][:, k, n], wl["wqm"][:, k, n]),
                                           (xh[s][:, k, :], xl[s][:, k, :]), k == 0, k == CT - 1)
                            mm.then_inc(qh_ps, 1)

                    pe.wait_ge(q_sb, 2 * CT)
                    queries(range(3))
                    for c in range(2):
                        for k in range(CT):
                            if c == 0:
                                pe.wait_ge(gelu_ok, k + 1)
                            mm = pe.matmul(ps[:, 7, c * NS:(c + 1) * NS],
                                           vec[:, 20 + 4 * c + k:21 + 4 * c + k].to_broadcast([P, P]), o[:, k, :],
                                           start=k == 0, stop=k == CT - 1)
                    mm.then_inc(off_ps, 1)
                    queries(range(3, 6))
                    pe.wait_ge(tanh_ok, 1)
                    for st in range(KT):
                        n = slice(st * P, (st + 1) * P)
                        for t in range(TT):
                            pe.wait_ge(hat_ok, t // 4 + 1)
                            mm = pe.matmul(ps[:, IT_BANK[st], :], hat[:, t, n], xs[:, t, :], start=t == 0, stop=t == TT - 1)
                        mm.then_inc(it_ps, 1)
                    queries(range(6, 8))
                    pe.wait_ge(ih_ok, KT)
                    pe.wait_ge(il_ok, KT)
                    for m in range(CT):
                        pe.wait_ge(qh_sb, m + 3)
                        pe.wait_ge(ql_sb, m + 3)
                        n = slice(m * P, (m + 1) * P)
                        for f in range(4):
                            e, st = f // 2, f % 2
                            mm = three(ps[:, K_BANK[m], 0:NK], (wh["wvk"][:, f, n], wl["wvk"][:, f, n]),
                                       (ith[:, st, e, :], itl[:, st, e, :]), f == 0, f == 3)
                        mm.then_inc(k_ps, 1)
                    for r in range(KT):
                        if r == 1:
                            pe.wait_ge(k_sb, 1)
                            pe.wait_ge(kl_sb, 1)
                        n = slice(r * P, (r + 1) * P)
                        for f in range(4):
                            e, st = f // 2, f % 2
                            mm = three(ps[:, V_BANK[r], :], (ith[:, st, e, n], itl[:, st, e, n]),
                                       (wh["wvv"][:, f, :], wl["wvv"][:, f, :]), f == 0, f == 3)
                        mm.then_inc(v_ps, 1)

                    pe.wait_ge(k_sb, CT)
                    pe.wait_ge(kl_sb, CT)
                    pe.wait_ge(qh_sb, 2 * CT)
                    pe.wait_ge(ql_sb, 2 * CT)

                    def output(u):
                        h = u // GR
                        if u == 0:
                            pe.wait_ge(vh_ok, KT)
                            pe.wait_ge(vl_ok, KT)
                        if u >= 2:
                            pe.wait_ge(ah_ok, u - 1)
                            pe.wait_ge(al_ok, u - 1)
                        pe.wait_ge(pl_ok, 2 * u + 2)
                        n = slice(h // 2 * P, h // 2 * P + P)
                        for kt in range(KT):
                            mm = three(ps[:, 6 + u % 2, :], (vh[:, kt, n], vl[:, kt, n]),
                                       (ph[:, u % 2, kt, :], pl[:, u % 2, kt, :]), kt == 0, kt == KT - 1)
                        mm.then_inc(av_ps, 1)

                    def scores(u):
                        h, g = u // GR, u % GR
                        j = h % SLOTS
                        if g == 0:
                            pe.wait_ge(s_ld[j], 96 * (h // SLOTS + 1))
                        if u >= 2:
                            pe.wait_ge(exp_ok, QG * (u - 1))
                        for t in range(QG):
                            dst = ps[:, 2 * (u % 2) + t // 2, (t % 2) * NK:(t % 2 + 1) * NK]
                            q_ = qs[:, j, (QG * g + t) * P:(QG * g + t + 1) * P]
                            pe.matmul(dst, q_, kh[:, j, :], start=True, stop=False)
                            mm = pe.matmul(dst, q_, kl[:, j, :], start=False, stop=True)
                        mm.then_inc(score, 1)

                    def transposes(u):
                        pe.wait_ge(sc_ok, QG * (u + 1))
                        for kt in range(KT):
                            if u >= 1:
                                pe.wait_ge(pl_ok, 2 * u - 1 + kt)
                            for t in range(QG):
                                mm = pe.transpose(ps[:, 4 + kt, t * P:(t + 1) * P],
                                                  prob[:, u % 2, t, kt * P:(kt + 1) * P], ident[:])
                            mm.then_inc(tr_ps, 1)

                    for n in range(U + 4):
                        if n < U:
                            scores(n)
                        if n >= 4:
                            output(n - 4)
                        if 2 <= n < U + 2:
                            transposes(n - 2)

                    for t in range(TT + 2):
                        if t < TT:
                            if t == 0:
                                pe.wait_ge(ah_ok, U)
                                pe.wait_ge(al_ok, U)
                            if t >= 2:
                                pe.wait_ge(z1_ok, t - 1)
                            n = slice(t * P, (t + 1) * P)
                            for k in range(CT):
                                mm = three(ps[:, t % 2, :], (qh[:, k, n], ql[:, k, n]),
                                           (wh["mo"][:, k, :], wl["mo"][:, k, :]), k == 0, k == CT - 1)
                            mm.then_inc(mo_ps, 1)
                        if 1 <= t <= TT:
                            u = t - 1
                            pe.wait_ge(zn_ok, u + 1)
                            if u >= 2:
                                pe.wait_ge(zl_ok, u - 1)
                            for k in range(CT):
                                mm = pe.transpose(ps[:, 2 + u % 2, k * P:(k + 1) * P], zn[:, u % 2, k * P:(k + 1) * P],
                                                  ident[:])
                            mm.then_inc(zt_ps, 1)
                        if t >= 2:
                            u = t - 2
                            pe.wait_ge(zl_ok, u + 1)
                            if u >= 2:
                                pe.wait_ge(y_ok, u - 1)
                            for k in range(CT):
                                mm = three(ps[:, 4 + u % 2, :], (zh[:, u % 2, k, :], zl[:, u % 2, k, :]),
                                           (wh["mlp"][:, k, :], wl["mlp"][:, k, :]), k == 0, k == CT - 1)
                            mm.then_inc(ml_ps, 1)

                @block.scalar
                def _(act):
                    def diagonal(e):
                        c, n = pe_taps[e]
                        act.activation(diag[:, e % DIAGS, :], ident[:], ACT.Copy, scale=dww[:, c, n:n + 1])\
                           .then_inc(dg_ok, 1)

                    for e in range(DIAGS):
                        diagonal(e)
                    for t in range(4):
                        act.wait_ge(ln_ok, t + 1)
                        high(act, 4 + t).then_inc(xh_ok, 1)
                    for e in range(DIAGS, len(pe_taps)):
                        act.wait_ge(dg_used, e - DIAGS + 1)
                        diagonal(e)
                    for c in range(CT):
                        act.wait_ge(tap, taps_upto[c])
                        act.activation(o[:, c, :], acc[:, c, :], ACT.Gelu).then_inc(gelu_ok, 1)

                    def query(g):
                        m, s = g // 2, g % 2
                        act.wait_ge(qh_ps, g + 1)
                        act.activation(qh[:, m, :].rearrange("p (c s) -> p s c", s=2)[:, s, :], ps[:, QH_BANK[g], :],
                                       ACT.Identity, bias=bqm[:, m:m + 1]).then_inc(qh_sb, 1)

                    act.wait_ge(tap, len(taps))
                    query(0)
                    act.wait_ge(off_ps, 1)
                    act.activation(xy[:].rearrange("p k n -> p (k n)"), ps[:, 7, :], ACT.Tanh).then_inc(tanh_ok, 1)
                    query(1)
                    act.wait_ge(xy_ok, 3)
                    act.activation(hx[:], xy[:, 1, :], ACT.Abs, bias=neg_x[:, 0:1]).then_inc(hx_ok, 1)
                    for t in range(TT):
                        act.activation(hat[:, t, :], xy[:, 0, :], ACT.Abs, bias=neg_y[:, t:t + 1]).then_inc(hy_ok, 1)
                        if t == 0:
                            act.wait_ge(hx_ok, 1)
                            act.activation(hx[:], hx[:], ACT.Relu, bias=1.0, scale=-1.0).then_inc(hx_ok, 1)
                        if t % 4 == 3:
                            half = hat[:, t - 3:t + 1, :]
                            act.wait_ge(hy_ok, t + 1 + t // 4)
                            act.activation(half, half, ACT.Relu, bias=1.0, scale=-1.0).then_inc(hy_ok, 1)
                    for g in range(2, 6):
                        query(g)
                    for st in range(KT):
                        act.wait_ge(it_ps, st + 1)
                        act.activation(ith[:, st, :, :], ps[:, IT_BANK[st], :].rearrange("p (r e) -> p e r", e=2),
                                       ACT.Copy).then_inc(ih_ok, 1)
                    for g in range(6, 8):
                        query(g)
                    for m in range(CT):
                        act.wait_ge(k_ps, m + 1)
                        act.activation(kch[:, m, :], ps[:, K_BANK[m], 0:NK], ACT.Identity, bias=bkm[:, m:m + 1])\
                            .then_inc(k_sb, 1)
                    for r in range(KT):
                        act.wait_ge(v_ps, r + 1)
                        act.activation(vh[:, r, :], ps[:, V_BANK[r], :], ACT.Copy).then_inc(vh_ok, 1)
                    def output(u):
                        h, g = u // GR, u % GR
                        act.wait_ge(av_ps, u + 1)
                        act.activation(qh[own_half(h), h // 2, g * 512:(g + 1) * 512],
                                       ps[own_half(h), 6 + u % 2, :], ACT.Copy).then_inc(ah_ok, 1)

                    def transposes(u):
                        for kt in range(KT):
                            n = KT * u + kt
                            act.wait_ge(tr_ps, n + 1)
                            if u >= 2:
                                act.wait_ge(av_ps, u - 1)
                            act.activation(ph[:, u % 2, kt, :], ps[:, 4 + kt, :], ACT.Copy).then_inc(ph_ok, 1)

                    def exponents(u):
                        act.wait_ge(max_ok, u + 1)
                        if u >= 2:
                            act.wait_ge(tr_ps, KT * (u - 1))
                        for t in range(QG):
                            c = QG * u + t
                            act.activation(prob[:, u % 2, t, :],
                                           ps[:, 2 * (u % 2) + t // 2, (t % 2) * NK:(t % 2 + 1) * NK], ACT.Exp,
                                           bias=neg_max[:, c:c + 1], accum_out=row_sum[:, c:c + 1]).then_inc(exp_ok, 1)

                    for n in range(U + 4):
                        if n >= 4:
                            output(n - 4)
                        if 2 <= n < U + 2:
                            transposes(n - 2)
                        if n < U:
                            exponents(n)
                    for t in range(1, TT + 2):
                        if t <= TT:
                            u = t - 1
                            act.wait_ge(zt_ps, u + 1)
                            if u >= 2:
                                act.wait_ge(ml_ps, u - 1)
                            act.activation(zh[:, u % 2, :, :], ps[:, 2 + u % 2, :].rearrange("p (k q) -> p k q", k=CT),
                                           ACT.Copy).then_inc(zh_ok, 1)
                        if t >= 2:
                            u = t - 2
                            act.wait_ge(y_ok, u + 1)
                            act.activation(ot[:, u % 2, :], ot[:, u % 2, :], ACT.Gelu).then_inc(ge_ok, 1)
                        if after is not None and 5 <= t < 9:
                            act.wait_ge(ln_ok, t)
                            high(act, t - 5).then_inc(xh_ok, 1)

                @block.vector
                def _(dve):
                    steps = [0]

                    def link(ins):
                        steps[0] += 1
                        ins.then_inc(chain, 1)
                        dve.wait_ge(chain, steps[0])

                    for t in range(4):
                        centre(dve, 4 + t).then_inc(ln1, 1)
                    for t in range(4):
                        dve.wait_ge(ln1, t + 1)
                        scale(dve, 4 + t).then_inc(ln_ok, 1)
                    for t in range(4):
                        dve.wait_ge(xh_ok, t + 1)
                        low(dve, 4 + t).then_inc(xl_ok, 1)
                    done = 0

                    def convolve(upto):
                        nonlocal done
                        while done < upto:
                            c, n = taps[done]
                            if tap_before[done]:
                                dve.wait_ge(tap, tap_before[done])
                            if n is None:
                                dve.wait_ge(dg_used, pe_upto[c])
                                dve.tensor_tensor(acc[:, c, :], ps[:, c, 0:NS], acc[:, c, :], ALU.add).then_inc(tap, 1)
                                done += 1
                                continue
                            if n == 0:
                                dve.wait_ge(q_sb, CT + c + 1)
                            dy, dx = n // KS, n % KS
                            src = qpad[:, c, :].rearrange("p (y x) -> p y x", x=PADW)[
                                :, dy:dy + 2 * GRID - 1:2, dx:dx + 2 * GRID - 1:2]
                            dst = acc[:, c, :].rearrange("p (y x) -> p y x", x=GRID)
                            if n == 0:
                                dve.tensor_scalar(dst, src, dww[:, c, n:n + 1], vec[:, 28 + c:29 + c], ALU.mult,
                                                  ALU.add).then_inc(tap, 1)
                            else:
                                dve.scalar_tensor_tensor(dst, src, dww[:, c, n:n + 1], dst, ALU.mult, ALU.add)\
                                   .then_inc(tap, 1)
                            done += 1

                    for g in range(2 * CT):
                        s, c = g // 4, g % 4
                        dve.wait_ge(pad_ok, c + 1)
                        dve.wait_ge(q_ps, g + 1)
                        inside = qpad[:, c, :].rearrange("p (y x) -> p y x", x=PADW)[
                            :, KS // 2 + 16 * s:KS // 2 + 16 * s + 16, KS // 2:KS // 2 + HW]
                        dve.tensor_tensor(inside, ps[:, g, :].rearrange("p (y x) -> p y x", x=HW),
                                          bqw[:].rearrange("p (y x) -> p y x", x=HW), ALU.add).then_inc(q_sb, 1)
                        if s == 1 and c < CT - 1:
                            convolve(SOLO * (c + 1) // (CT - 1))
                    convolve(len(taps))

                    def query(g):
                        m, s = g // 2, g % 2
                        here = (slice(None), m)
                        dve.wait_ge(qh_sb, g + 1)
                        dve.scalar_tensor_tensor(ql[here].rearrange("p (c s) -> p s c", s=2)[:, s, :],
                                                 ps[:, QH_BANK[g], :], bqm[:, m:m + 1],
                                                 raw(qh[here]).rearrange("p (c s) -> p s c", s=2)[:, s, :],
                                                 ALU.add, ALU.subtract).then_inc(ql_sb, 1)

                    query(0)
                    dve.wait_ge(tanh_ok, 1)
                    dve.tensor_tensor(xy[:], xy[:], refs[:], ALU.add).then_inc(xy_ok, 1)
                    dve.wait_ge(xy_ok, 1)
                    dve.tensor_scalar(xy[:], xy[:], 1.0, HW / 2 / 2.0, ALU.add, ALU.mult).then_inc(xy_ok, 1)
                    dve.wait_ge(xy_ok, 2)
                    dve.tensor_scalar(xy[:], xy[:], 1.0, 0.5 * (HW - 1), ALU.add, ALU.mult).then_inc(xy_ok, 1)
                    query(1)
                    for s in range(2):
                        dve.wait_ge(hx_ok, 2)
                        dve.wait_ge(hy_ok, 5 * s + 5)
                        half = hat[:, 4 * s:4 * s + 4, :]
                        dve.tensor_tensor(half, half, hx[:].unsqueeze(1).to_broadcast([P, 4, NS]), ALU.mult)\
                           .then_inc(hat_ok, 1)
                    for g in range(2, 6):
                        query(g)
                    for st in range(KT):
                        dve.wait_ge(ih_ok, st + 1)
                        dve.tensor_tensor(itl[:, st, :, :], ps[:, IT_BANK[st], :].rearrange("p (r e) -> p e r", e=2),
                                          raw(ith[:, st, :, :]), ALU.subtract).then_inc(il_ok, 1)
                    for g in range(6, 8):
                        query(g)
                    for m in range(CT):
                        dve.wait_ge(k_sb, m + 1)
                        dve.scalar_tensor_tensor(kcl[:, m, :], ps[:, K_BANK[m], 0:NK], bkm[:, m:m + 1],
                                                 raw(kch[:, m, :]), ALU.add, ALU.subtract).then_inc(kl_sb, 1)
                    for r in range(KT):
                        dve.wait_ge(vh_ok, r + 1)
                        dve.tensor_tensor(vl[:, r, :], ps[:, V_BANK[r], :], raw(vh[:, r, :]), ALU.subtract)\
                           .then_inc(vl_ok, 1)
                    def output(u):
                        h, g = u // GR, u % GR
                        here = (own_half(h), h // 2, slice(g * 512, (g + 1) * 512))
                        dve.wait_ge(ah_ok, u + 1)
                        dve.tensor_tensor(ql[here], ps[own_half(h), 6 + u % 2, :], raw(qh[here]), ALU.subtract)\
                           .then_inc(al_ok, 1)

                    def inverses(u):
                        dve.wait_ge(exp_ok, QG * (u + 1))
                        dve.reciprocal(row_inv[:, QG * u:QG * u + QG], row_sum[:, QG * u:QG * u + QG])\
                           .then_inc(inv_ok, 1)

                    def maxima(u):
                        dve.wait_ge(score, u + 1)
                        dve.tensor_reduce(neg_max[:, QG * u:QG * u + QG],
                                          ps[:, 2 * (u % 2):2 * (u % 2) + 2, :].rearrange("p a (b k) -> p (a b) k", b=2),
                                          AX, ALU.max, negate=True).then_inc(max_ok, 1)

                    def transposes(u):
                        for kt in range(KT):
                            dve.wait_ge(ph_ok, KT * u + kt + 1)
                            dve.tensor_tensor(pl[:, u % 2, kt, :], ps[:, 4 + kt, :], raw(ph[:, u % 2, kt, :]),
                                              ALU.subtract).then_inc(pl_ok, 1)

                    for n in range(U + 4):
                        if 1 <= n < U + 1:
                            inverses(n - 1)
                        if n < U:
                            maxima(n)
                        if n >= 4:
                            output(n - 4)
                        if 2 <= n < U + 2:
                            transposes(n - 2)
                    for t in range(TT + 2):
                        if t < TT:
                            dve.wait_ge(mo_ps, t + 1)
                            dve.wait_ge(z_ld[t], 16)
                            dve.tensor_tensor(z[:, t, :], ps[:, t % 2, :], z[:, t, :], ALU.add).then_inc(z1_ok, 1)
                        if 1 <= t <= TT:
                            u = t - 1
                            dve.wait_ge(zh_ok, u + 1)
                            dve.tensor_tensor(zl[:, u % 2, :, :], ps[:, 2 + u % 2, :].rearrange("p (k q) -> p k q", k=CT),
                                              raw(zh[:, u % 2, :, :]), ALU.subtract).then_inc(zl_ok, 1)
                        if t < TT:
                            dve.wait_ge(z_ok, t + 1)
                            link(dve.bn_stats(nbn[:, t, :], z[:, t, :]))
                            link(dve.bn_aggr(zmv[:, t, :], nbn[:, t, :]))
                            dve.tensor_scalar(zrs[:, t:t + 1], zmv[:, t, 1:2], 1e-5, None, ALU.add).then_inc(zvar, 1)
                            if t >= 2:
                                dve.wait_ge(zt_ps, t - 1)
                            link(dve.scalar_tensor_tensor(zn[:, t % 2, :], z[:, t, :], zmv[:, t, 0:1], lng[:],
                                                          ALU.subtract, ALU.mult))
                            dve.wait_ge(zrstd, t + 1)
                            dve.scalar_tensor_tensor(zn[:, t % 2, :], zn[:, t % 2, :], zrs[:, t:t + 1], lnb[:],
                                                     ALU.mult, ALU.add).then_inc(zn_ok, 1)
                        if t >= 2:
                            u = t - 2
                            dve.wait_ge(ml_ps, u + 1)
                            if u >= 2:
                                dve.wait_ge(o_st[u % 2], 16 * (u // 2))
                            dve.tensor_tensor(ot[:, u % 2, :], ps[:, 4 + u % 2, :], bmlp[:], ALU.add).then_inc(y_ok, 1)
                        if after is not None:
                            if t < TT:
                                dve.wait_ge(x_ld[t], 16)
                                dve.bn_stats(bn[:, t, :], xs[:, t, :]).then_inc(bn_ok, 1)
                                dve.wait_ge(bn_ok, t + 1)
                                dve.bn_aggr(mv[:, t, :], bn[:, t, :]).then_inc(bn_ag, 1)
                            if t % 4 == 3:
                                dve.wait_ge(bn_ag, t + 1)
                                dve.tensor_scalar(rstd[:, t - 3:t + 1], mv[:, t - 3:t + 1, 1], 1e-5, None, ALU.add)\
                                   .then_inc(var_ok, 1)
                            if 5 <= t < 9:
                                dve.wait_ge(xh_ok, t)
                                low(dve, t - 5).then_inc(xl_ok, 1)
                            if 4 <= t < 8:
                                centre(dve, t - 4).then_inc(ln1, 1)
                                dve.wait_ge(ln1, t + 1)
                                dve.wait_ge(rstd_ok, 1)
                                scale(dve, t - 4).then_inc(ln_ok, 1)

                @block.gpsimd
                def _(pool):
                    for c in range(CT):
                        pool.memset(qpad[:, c, :], 0.0).then_inc(pad_ok, 1)
                        pool.wait_ge(pad_ok, c + 1)
                    for c in range(U * QG):
                        u, t = c // QG, c % QG
                        pool.wait_ge(inv_ok, u + 1)
                        pool.tensor_scalar(prob[:, u % 2, t, :], prob[:, u % 2, t, :], row_inv[:, c:c + 1], 0.0,
                                           ALU.mult, ALU.add).then_inc(sc_ok, 1)
                        pool.wait_ge(sc_ok, c + 1)
                    for t in range(TT + 2):
                        if t < TT:
                            pool.wait_ge(z1_ok, t + 1)
                            pool.tensor_tensor(z[:, t, :], z[:, t, :], bmo[:], ALU.add).then_inc(z_ok, 1)
                            pool.wait_ge(zvar, t + 1)
                            pool.wait_ge(z_ok, t + 1)
                            pool.tensor_tensor(zrs[:, t:t + 1], zrs[:, t:t + 1], neg_half[:, 0:1], ALU.pow)\
                                .then_inc(zrstd, 1)
                            pool.wait_ge(zrstd, t + 1)
                        if after is not None and t % 4 == 3:
                            here = slice(t - 3, t + 1)
                            pool.wait_ge(var_ok, t // 4 + 1)
                            pool.tensor_tensor(rstd[:, here], rstd[:, here], neg_half[:], ALU.pow).then_inc(rstd_ok, 1)
                            pool.wait_ge(rstd_ok, t // 4 + 1)
                        if t >= 2:
                            u = t - 2
                            pool.wait_ge(ge_ok, u + 1)
                            pool.tensor_tensor(ot[:, u % 2, :], ot[:, u % 2, :], z[:, u, :], ALU.add).then_inc(out_ok, 1)
                            pool.wait_ge(out_ok, u + 1)

        if n_images > 1:
            with nc.Fori(0, n_images - 1) as i:
                image(i, x2[1:])
                nc.all_engine_barrier(sems_to_clear=range(min(nums), max(nums) + 1))
        image(n_images - 1)


_INS = ["x", "L0_conv_gn_scale", "L0_conv_gn_bias", "L0_conv_w_qkv", "L0_conv_b_qkv", "L0_conv_w_out", "L0_conv_b_out",
        "L1_conv_ln_g", "L1_conv_ln_b", "L1_conv_wq", "L1_conv_bq", "L1_conv_wv", "L1_conv_bv", "L1_conv_dw_w",
        "L1_conv_dw_b", "L1_conv_pw_w", "L1_conv_mq_w", "L1_conv_mq_b", "L1_conv_mk_w", "L1_conv_mk_b",
        "L1_conv_mv_w", "L1_conv_mv_b", "L1_conv_mo_w", "L1_conv_mo_b", "L1_conv_mlp_w", "L1_conv_mlp_b"]


def build(nc, a, out, n_images=B):
    x2 = nc.dram_tensor("x2", [B, TOK, C], F32, kind="Internal").ap()
    l0 = [a["L0_conv_" + n] for n in ("gn_scale", "gn_bias", "w_qkv", "b_qkv", "w_out", "b_out")]
    layer0(nc, a["x"].rearrange("b h w c -> b (h w) c"), *l0, x2, n_images)
    l1 = {n: a["L1_conv_" + n] for n in ("ln_g", "ln_b", "wq", "bq", "wv", "bv", "dw_w", "dw_b", "pw_w", "mq_w", "mq_b",
                                         "mk_w", "mk_b", "mv_w", "mv_b", "mo_w", "mo_b", "mlp_w", "mlp_b")}
    l1["dw_w"] = l1["dw_w"].rearrange("c o y x -> c (o y x)")
    l1["pw_w"] = l1["pw_w"].rearrange("k c y x -> k (c y x)")
    layer1(nc, x2, *l1.values(), out.rearrange("b h w c -> b (h w) c"), n_images)


def kernel(**inputs):
    import numpy as _np
    import concourse.bacc as _bacc
    from concourse.bass_utils import run_bass_kernel_spmd as _run

    nc = _bacc.Bacc("TRN2", target_bir_lowering=False, num_devices=1)
    arrays, args = {}, {}
    for name in _INS:
        arr = _np.ascontiguousarray(inputs[name])
        arrays[f"in_{name}"] = arr
        args[name] = nc.dram_tensor(f"in_{name}", arr.shape, mybir.dt.from_np(arr.dtype), kind="ExternalInput").ap()
    out = nc.dram_tensor("out_0", (B, HW, HW, C), F32, kind="ExternalOutput").ap()
    build(nc, args, out)
    r = _run(nc, [arrays], core_ids=[0])
    return r.results[0]["out_0"]
```

```python
from contextlib import ExitStack

import concourse.bass as bass
from concourse import mybir

F32 = mybir.dt.float32
F32R = mybir.dt.float32r
ACT = mybir.ActivationFunctionType
ALU = mybir.AluOpType
AX = mybir.AxisListType.X

P = 128
B = 8
TOK = 1024
C = 512
CT = C // P
TT = TOK // P
NH = 8
HD = C // NH
HALF = TOK // 2
HW = 32
GRID = 16
NS = GRID * GRID
KS = 7
PADW = HW + KS - 1
SB_START = 16512
SB_END = 229344


class Region:

    def __init__(self, nc, start, end):
        self.nc, self.at, self.end = nc, start, end

    def take(self, name, shape, dt=F32):
        size = 4
        for n in shape[1:]:
            size *= n
        size = (size + 31) // 32 * 32
        assert self.at + size <= self.end, (name, self.at + size - self.end)
        t = self.nc.alloc_sbuf_tensor_at(name, shape, dt, offset=self.at)
        self.at += size
        return t


def raw(ap):
    return ap.bitcast(F32)


def own_half(h):
    return slice(HD * (h % 2), HD * (h % 2) + HD)


def other_half(h):
    return slice(HD * (1 - h % 2), HD * (1 - h % 2) + HD)


def v_hi(tile):
    return tile.rearrange("p (q f d) -> p q f d", q=NH // 2, f=4)[:, :, 0:4:3, :]


def v_lo(tile):
    return tile.rearrange("p (q f d) -> p q f d", q=NH // 2, f=4)[:, :, 1:3, :]


def by_head(ap):
    return ap.rearrange("p (q e d) -> p q e d", q=NH // 2, e=2)


def make_identity(pool, ident, done):
    pool.memset(ident[:], 0.0).then_inc(done, 1)
    pool.wait_ge(done, 1)
    pool.affine_select(out=ident[:], in_=ident[:], compare_op=ALU.not_equal, fill=1.0, base=0,
                       pattern=[[-1, P]], channel_multiplier=1).then_inc(done, 1)


def layer0(nc, x, gn_scale, gn_bias, w_qkv, b_qkv, w_out, b_out, x2, n_images=B):
    NB = TOK // 256
    U = NH * TT
    QSCALE = 1.0 / HD

    with ExitStack() as ctx:
        def sem(name):
            return ctx.enter_context(nc.semaphore("a_" + name))

        ps = ctx.enter_context(nc.psum_tensor("a_ps", [P, 8, 512], F32))
        R = Region(nc, SB_START, SB_END)
        wqh = R.take("wqkv_hi", [P, CT, 3 * C], F32R)
        wql = R.take("wqkv_lo", [P, CT, 3 * C], F32R)
        woh = R.take("wout_hi", [P, CT, C], F32R)
        wol = R.take("wout_lo", [P, CT, C], F32R)
        ident = R.take("a_ident", [P, P])
        group = R.take("a_group", [P, P])
        bout = R.take("a_bout", [P, C])
        vec = R.take("a_vec", [P, 20])
        bq = R.take("a_bq", [P, CT])
        neg_half = R.take("a_neg_half", [P, CT])
        small = R.take("a_small", [P, 40])
        bn = R.take("a_bn", [P, CT, 2, 6])
        neg_max = R.take("a_neg_max", [P, U])
        row_sum = R.take("a_row_sum", [P, U])
        row_inv = R.take("a_row_inv", [P, U])
        fold_t = R.take("a_fold_t", [P, 256])
        fold_r = R.take("a_fold_r", [P, 2, 256])
        fold_s = R.take("a_fold_s", [P, 2, 256])
        qk = R.take("a_qk", [P, 2 * CT, TOK])
        v_at = R.at
        v = R.take("a_v", [P, TT, NH * P], F32R)
        qs = R.take("a_qs", [P, 2, TOK], F32R)
        kh = R.take("a_kh", [P, 2, TOK], F32R)
        kl = R.take("a_kl", [P, 2, TOK], F32R)
        work = R.at
        prob = R.take("a_prob", [P, 2, TOK])
        split = R.at
        ph = R.take("a_ph", [P, 2, TT, 256], F32R)
        pl = R.take("a_pl", [P, 2, TT, 256], F32R)
        S = Region(nc, split, SB_END)
        xh = S.take("a_xh", [P, CT, TOK], F32R)
        xl = S.take("a_xl", [P, CT, TOK], F32R)
        S = Region(nc, v_at, v_at + 32768)
        ah = S.take("a_ah", [P, CT, TOK], F32R)
        al = S.take("a_al", [P, CT, TOK], F32R)
        xtok = Region(nc, v_at - 16384, v_at).take("a_xtok", [P, TT, C])
        xt = Region(nc, work - 16384 - 8192, SB_END).take("a_xt", [P, CT, TOK])
        tok = Region(nc, work - 8192, work + 8192).take("a_tok", [P, TT, C])
        W = Region(nc, v_at, v_at + 32768)
        wq_raw = W.take("a_wq_raw", [P, CT, 3 * C])
        wo_raw = W.take("a_wo_raw", [P, CT, C])
        W = Region(nc, work, split)
        rows = W.take("a_rows", [20, P])
        bo_raw = W.take("a_bo_raw", [P, C])
        bv_wide = W.take("a_bv_wide", [P, CT, P])

        wq_ld, wo_ld, wql_ok = [sem(f"s_wq{k}") for k in range(CT)], sem("s_wo"), sem("s_wql")
        ld, cst, spl, pe_s, chn = sem("s_ld"), sem("s_cst"), sem("s_spl"), sem("s_pe"), sem("s_chn")
        x_ld = [sem(f"x_ld{i}") for i in range(TT)]
        r_ld = [sem(f"r_ld{i}") for i in range(TT)]
        o_st = sem("o_st")
        s_ld = [sem(f"s_ld{i}") for i in range(2)]
        xt_ps, xt_sb, bn_ok, bn_ag = sem("xt_ps"), sem("xt_sb"), sem("bn_ok"), sem("bn_ag")
        st_ok, st_ps, var_ok, rstd_ok = sem("st_ok"), sem("st_ps"), sem("var_ok"), sem("rstd_ok")
        chain = sem("chain")
        xn_ok, xh_ok, xl_ok = sem("xn_ok"), sem("xh_ok"), sem("xl_ok")
        pr_ps, qk_sb, vh_ok, vl_ok = sem("pr_ps"), sem("qk_sb"), sem("vh_ok"), sem("vl_ok")
        staged, score, max_ok, exp_ok = sem("staged"), sem("score"), sem("max_ok"), sem("exp_ok")
        tr_ps, ph_ok, pl_ok, inv_ok = sem("tr_ps"), sem("ph_ok"), sem("pl_ok"), sem("inv_ok")
        av_ps, fold_cp, fold_add, att_ok = sem("av_ps"), sem("fold_cp"), sem("fold_add"), sem("att_ok")
        ah_ok, al_ok, out_ps, res_ok, out_ok = sem("ah_ok"), sem("al_ok"), sem("out_ps"), sem("res_ok"), sem("out_ok")
        cleared = [*x_ld, *r_ld, o_st, *s_ld, xt_ps, xt_sb, bn_ok, bn_ag, st_ok, st_ps, var_ok, rstd_ok, chain,
                   xn_ok, xh_ok, xl_ok, pr_ps, qk_sb, vh_ok, vl_ok, staged, score, max_ok, exp_ok, tr_ps, ph_ok,
                   pl_ok, inv_ok, av_ps, fold_cp, fold_add, att_ok, ah_ok, al_ok, out_ps, res_ok, out_ok]
        nums = [s.num for s in cleared]
        assert sorted(nums) == list(range(min(nums), max(nums) + 1))

        groups = [("qk", m, s) for m in (0, 4) for s in range(2)] + [("v", t, 0) for t in range(TT)]
        groups += [("qk", m, s) for m in (1, 5, 2, 6, 3, 7) for s in range(2)]
        qk_upto = [sum(g[0] == "qk" for g in groups[:n]) for n in range(len(groups) + 1)]
        v_upto = [sum(g[0] == "v" for g in groups[:n]) for n in range(len(groups) + 1)]
        n_qk, n_v = qk_upto[-1], v_upto[-1]
        STAGE = 5
        AVERAGE_AT = 2
        POWER_AT = 3

        mv = small[:, 8:16].rearrange("p (c m) -> p c m", m=2)

        def turn_tile(pe, t):
            for c in range(CT):
                mm = pe.transpose(ps[:, t % 4, c * P:(c + 1) * P], xtok[:, t, c * P:(c + 1) * P], ident[:])
            return mm

        def keep_tile(act, t):
            return act.activation(xt[:, :, t * P:(t + 1) * P], ps[:, t % 4, :].rearrange("p (c n) -> p c n", c=CT),
                                  ACT.Copy)

        def average(pe):
            return pe.matmul(ps[:, 0, 0:8], group[:], small[:, 0:8], start=True, stop=True)

        def stats(dve, s):
            for c in range(CT):
                dve.bn_stats(bn[:, c, s, :], xt[:, c, s * HALF:(s + 1) * HALF]).then_inc(bn_ok, 1)

        def moments(dve, link):
            dve.wait_ge(bn_ok, 2 * CT)
            for c in range(CT):
                dve.bn_aggr(mv[:, c, :], bn[:, c, :, :].rearrange("p s k -> p (s k)")).then_inc(bn_ag, 1)
            dve.wait_ge(bn_ag, CT)
            link(dve.tensor_tensor(small[:, 16:20], mv[:, :, 0], mv[:, :, 0], ALU.mult))
            dve.tensor_copy(small[:, 0:4], mv[:, :, 0]).then_inc(st_ok, 1)
            dve.tensor_tensor(small[:, 4:8], small[:, 16:20], mv[:, :, 1], ALU.add).then_inc(st_ok, 1)

        def variance(dve, link):
            dve.wait_ge(st_ps, 1)
            link(dve.tensor_copy(small[:, 20:28], ps[:, 0, 0:8]))
            link(dve.tensor_tensor(small[:, 28:32], small[:, 20:24], small[:, 20:24], ALU.mult))
            link(dve.tensor_tensor(small[:, 28:32], small[:, 24:28], small[:, 28:32], ALU.subtract))
            dve.tensor_scalar(small[:, 28:32], small[:, 28:32], 0.0, 1e-6, ALU.max, ALU.add).then_inc(var_ok, 1)

        def affine(dve, link):
            dve.wait_ge(rstd_ok, 1)
            link(dve.tensor_tensor(small[:, 32:36], small[:, 32:36], vec[:, 0:4], ALU.mult))
            link(dve.tensor_tensor(small[:, 36:40], small[:, 20:24], small[:, 32:36], ALU.mult))
            link(dve.tensor_tensor(small[:, 36:40], vec[:, 4:8], small[:, 36:40], ALU.subtract))

        def normalise(dve, c):
            return dve.tensor_scalar(xt[:, c, :], xt[:, c, :], small[:, 32 + c:33 + c], small[:, 36 + c:37 + c],
                                     ALU.mult, ALU.add)

        def high(act, c):
            return act.activation(xh[:, c, :], xt[:, c, :], ACT.Copy)

        def low(dve, c):
            return dve.tensor_tensor(xl[:, c, :], xt[:, c, :], raw(xh[:, c, :]), ALU.subtract)

        def project(pe, g):
            kind, m, s = groups[g]
            for k in range(CT):
                if kind == "qk":
                    w, n = slice(m * P, (m + 1) * P), slice(s * HALF, (s + 1) * HALF)
                    pairs = ((wqh[:, k, w], xh[:, k, n]), (wqh[:, k, w], xl[:, k, n]), (wql[:, k, w], xh[:, k, n]))
                else:
                    w, n = slice(2 * C, 3 * C), slice(m * P, (m + 1) * P)
                    pairs = ((xh[:, k, n], wqh[:, k, w]), (xh[:, k, n], wql[:, k, w]), (xl[:, k, n], wqh[:, k, w]))
                for e, (a, b) in enumerate(pairs):
                    mm = pe.matmul(ps[:, g % 8, :], a, b, start=k == 0 and e == 0, stop=k == CT - 1 and e == 2)
            return mm

        EARLY = 2

        with nc.Block() as block:
            @block.sync
            def _(sp):
                for t in range(TT):
                    sp.dma_start(xtok[:, t, :], x[0, t * P:(t + 1) * P, :]).then_inc(x_ld[t], 16)
                sp.dma_start(rows[0:4, :], gn_scale.rearrange("(t p) -> t p", p=P)).then_inc(ld, 16)
                sp.dma_start(rows[4:8, :], gn_bias.rearrange("(t p) -> t p", p=P)).then_inc(ld, 16)
                sp.dma_start(rows[8:20, :], b_qkv.rearrange("(t p) -> t p", p=P)).then_inc(ld, 16)
                for k in range(CT):
                    sp.dma_start(wq_raw[:, k, :], w_qkv[k * P:(k + 1) * P, :]).then_inc(wq_ld[k], 16)
                sp.dma_start(wo_raw[:], w_out.rearrange("(t p) n -> p t n", p=P)).then_inc(wo_ld, 16)
                sp.dma_start(bo_raw[:], b_out.partition_broadcast(P)).then_inc(wo_ld, 16)

            @block.gpsimd
            def _(pool):
                make_identity(pool, ident, cst)
                pool.memset(group[:], 1.0 / 16).then_inc(cst, 1)
                pool.memset(neg_half[:], -0.5).then_inc(cst, 1)
                blocks = group[:].rearrange("p (g j) -> p g j", j=16)
                pool.wait_ge(cst, 3)
                pool.affine_select(out=blocks, in_=blocks, compare_op=ALU.is_ge, fill=0.0, base=0,
                                   pattern=[[-16, 8], [0, 16]], channel_multiplier=1).then_inc(cst, 1)
                pool.wait_ge(cst, 5)
                pool.affine_select(out=blocks, in_=blocks, compare_op=ALU.is_ge, fill=0.0, base=15,
                                   pattern=[[16, 8], [0, 16]], channel_multiplier=-1).then_inc(cst, 1)
                pool.wait_ge(cst, 6)
                pool.wait_ge(var_ok, 1)
                pool.tensor_tensor(small[:, 32:36], small[:, 28:32], neg_half[:], ALU.pow).then_inc(rstd_ok, 1)

            @block.scalar
            def _(act):
                for t in range(TT):
                    act.wait_ge(xt_ps, t + 1)
                    keep_tile(act, t).then_inc(xt_sb, 1)
                for k in range(CT):
                    act.wait_ge(wq_ld[k], 16)
                    act.activation(wqh[:, k, :], wq_raw[:, k, :], ACT.Copy).then_inc(spl, 1)
                    act.wait_ge(xn_ok, k + 1)
                    high(act, k).then_inc(xh_ok, 1)
                act.wait_ge(wo_ld, 32)
                act.activation(woh[:], wo_raw[:], ACT.Copy).then_inc(spl, 1)

            @block.tensor
            def _(pe):
                pe.wait_ge(cst, 2)
                for t in range(TT):
                    pe.wait_ge(x_ld[t], 16)
                    if t >= 4:
                        pe.wait_ge(xt_sb, t - 3)
                    turn_tile(pe, t).then_inc(xt_ps, 1)
                pe.wait_ge(ld, 48)
                pe.transpose(ps[:, 4, 0:20], rows[:], ident[0:20, 0:20]).then_inc(pe_s, 1)
                pe.wait_ge(cst, 6)
                pe.wait_ge(st_ok, 2)
                average(pe).then_inc(st_ps, 1)
                pe.wait_ge(chn, 3)
                pe.wait_ge(wo_ld, 32)
                for k in range(CT):
                    mm = pe.matmul(ps[:, 5, :], bv_wide[:, k, :], wo_raw[:, k, :], start=k == 0, stop=k == CT - 1)
                mm.then_inc(pe_s, 1)
                pe.wait_ge(wql_ok, CT)
                pe.wait_ge(xh_ok, CT)
                pe.wait_ge(xl_ok, CT)
                for g in range(EARLY):
                    project(pe, g)

            @block.vector
            def _(dve):
                steps = [0]

                def link(ins):
                    steps[0] += 1
                    ins.then_inc(chain, 1)
                    dve.wait_ge(chain, steps[0])

                for s in range(2):
                    dve.wait_ge(xt_sb, 4 * s + 4)
                    stats(dve, s)
                moments(dve, link)
                dve.wait_ge(pe_s, 1)
                dve.tensor_copy(vec[:], ps[:, 4, 0:20]).then_inc(chn, 1)
                dve.wait_ge(chn, 1)
                dve.tensor_scalar(bq[:], vec[:, 8:12], QSCALE, None, ALU.mult).then_inc(chn, 1)
                dve.tensor_copy(bv_wide[:], vec[:, 16:20].unsqueeze(2).to_broadcast([P, CT, P])).then_inc(chn, 1)
                variance(dve, link)
                affine(dve, link)
                for c in range(CT):
                    normalise(dve, c).then_inc(xn_ok, 1)
                for k in range(CT):
                    dve.wait_ge(spl, k + 1)
                    dve.tensor_tensor(wql[:, k, :], wq_raw[:, k, :], raw(wqh[:, k, :]), ALU.subtract)\
                       .then_inc(wql_ok, 1)
                    dve.wait_ge(xh_ok, k + 1)
                    low(dve, k).then_inc(xl_ok, 1)
                dve.wait_ge(spl, CT + 1)
                dve.tensor_tensor(wol[:], wo_raw[:], raw(woh[:]), ALU.subtract).then_inc(chn, 1)
                dve.wait_ge(pe_s, 2)
                dve.tensor_tensor(bout[:], ps[:, 5, :], bo_raw[:], ALU.add).then_inc(chn, 1)

        nc.all_engine_barrier(sems_to_clear=range(min(nums), max(nums) + 1))

        def image(i, after=None):
            with nc.Block() as block:
                @block.sync
                def _(sp):
                    for h in range(NH):
                        p, j = h // 2, h % 2
                        sp.wait_ge(qk_sb, 4 if p == 0 else 4 + 4 * p)
                        if h >= 2:
                            sp.wait_ge(score, TT * (h - 1))
                        for half in range(2):
                            rows_ = slice(HD * half, HD * half + HD)
                            sp.dma_start(raw(qs[rows_, j, :]), qk[own_half(h), p, :]).then_inc(s_ld[j], 16)
                            sp.dma_start(raw(kl[rows_, j, :]), qk[own_half(h), CT + p, :]).then_inc(s_ld[j], 16)
                    if after is not None:
                        for j in range(2):
                            sp.wait_ge(s_ld[j], 64 * (NH // 2))
                        for t in range(TT):
                            sp.dma_start(xtok[:, t, :], after[i, t * P:(t + 1) * P, :]).then_inc(x_ld[t], 16)
                    sp.wait_ge(tr_ps, 2 * U)
                    for t in range(TT):
                        sp.dma_start(tok[:, t, :], x[i, t * P:(t + 1) * P, :]).then_inc(r_ld[t], 16)
                    for t in range(TT):
                        sp.wait_ge(out_ok, t + 1)
                        sp.dma_start(x2[i, t * P:(t + 1) * P, :], tok[:, t, :]).then_inc(o_st, 16)
                    sp.wait_ge(o_st, 16 * TT)

                @block.tensor
                def _(pe):
                    for g in range(EARLY, len(groups)):
                        if g >= 8:
                            pe.wait_ge(qk_sb, qk_upto[g - 7])
                            if v_upto[g - 7]:
                                pe.wait_ge(vl_ok, v_upto[g - 7])
                        project(pe, g).then_inc(pr_ps, 1)

                    def turn(tiles):
                        if after is not None:
                            for t in tiles:
                                pe.wait_ge(x_ld[t], 16)
                                if t >= 4:
                                    pe.wait_ge(xt_sb, t - 3)
                                turn_tile(pe, t).then_inc(xt_ps, 1)

                    pe.wait_ge(qk_sb, n_qk)
                    pe.wait_ge(vl_ok, n_v)
                    for i_ in range(U + 7):
                        if i_ >= 5:
                            b, part = (i_ - 5) // 2, (i_ - 5) % 2
                            if b < U // 2:
                                h = b // NB
                                if part == 0:
                                    pe.wait_ge(inv_ok, b + 1)
                                    if b >= 2:
                                        pe.wait_ge(fold_add, b - 1)
                                        pe.wait_ge(fold_cp, 2 * b - 2)
                                    for n in range(2):
                                        u = 2 * b + n
                                        pe.transpose(ps[:, 6 + b % 2, 256 + n * P:256 + (n + 1) * P],
                                                     row_inv[:, u:u + 1].to_broadcast([P, P]), ident[:])
                                pe.wait_ge(pl_ok, 4 * b + 3 + part)
                                for kt in range(4 * part, 4 * part + 4):
                                    for e, q_ in enumerate((ph, pl)):
                                        mm = pe.matmul(ps[:, 6 + b % 2, 0:256], v[:, kt, h * P:(h + 1) * P], q_[:, b % 2, kt, :],
                                                       start=kt == 0 and e == 0, stop=kt == TT - 1 and e == 1)
                                if part == 1:
                                    mm.then_inc(av_ps, 1)
                        if i_ < U:
                            h, t = i_ // TT, i_ % TT
                            j = h % 2
                            if t == 0:
                                pe.wait_ge(staged, STAGE * (h + 1))
                            if i_ >= 2:
                                pe.wait_ge(exp_ok, i_ - 1)
                            for kb in range(2):
                                bank = ps[:, 2 * (i_ % 2) + kb, :]
                                q_ = qs[:, j, t * P:(t + 1) * P]
                                n = slice(kb * 512, (kb + 1) * 512)
                                pe.matmul(bank, q_, kh[:, j, n], start=True, stop=False)
                                mm = pe.matmul(bank, q_, kl[:, j, n], start=False, stop=True)
                            mm.then_inc(score, 1)
                        if 2 <= i_ < U + 2:
                            u = i_ - 2
                            pe.wait_ge(exp_ok, u + 1)
                            for g in range(2):
                                n = 2 * u + g
                                if n >= 2:
                                    pe.wait_ge(pl_ok, n - 1)
                                for kk in range(4):
                                    kt = 4 * g + kk
                                    mm = pe.transpose(ps[:, 4 + n % 2, kk * P:(kk + 1) * P],
                                                      prob[:, u % 2, kt * P:(kt + 1) * P], ident[:])
                                mm.then_inc(tr_ps, 1)
                        if i_ == U + 2:
                            turn(range(4))

                    for t in range(TT):
                        if t >= 4:
                            pe.wait_ge(out_ok, t - 3)
                        n = slice(t * P, (t + 1) * P)
                        for k in range(CT):
                            if t in (0, TT // 2):
                                pe.wait_ge(ah_ok, CT * (t // 4) + k + 1)
                                pe.wait_ge(al_ok, CT * (t // 4) + k + 1)
                            for e, (a, b) in enumerate(((ah[:, k, n], woh[:, k, :]), (ah[:, k, n], wol[:, k, :]),
                                                        (al[:, k, n], woh[:, k, :]))):
                                mm = pe.matmul(ps[:, 4 + t % 4, :], a, b, start=k == 0 and e == 0,
                                               stop=k == CT - 1 and e == 2)
                        mm.then_inc(out_ps, 1)
                        if t == 0:
                            turn(range(4, TT))
                        if after is not None and t == AVERAGE_AT:
                            pe.wait_ge(st_ok, 2)
                            average(pe).then_inc(st_ps, 1)
                    if after is not None:
                        pe.wait_ge(xh_ok, CT)
                        pe.wait_ge(xl_ok, CT)
                        for g in range(EARLY):
                            project(pe, g)

                @block.scalar
                def _(act):
                    for g, (kind, m, s) in enumerate(groups):
                        if g >= EARLY:
                            act.wait_ge(pr_ps, g + 1 - EARLY)
                        if kind == "v":
                            act.activation(v_hi(v[:, m, :]), by_head(ps[:, g % 8, :]), ACT.Copy).then_inc(vh_ok, 1)
                        elif m < CT:
                            act.activation(qk[:, m, s * HALF:(s + 1) * HALF], ps[:, g % 8, :], ACT.Identity,
                                           bias=bq[:, m:m + 1], scale=QSCALE).then_inc(qk_sb, 1)
                        else:
                            act.activation(qk[:, m, s * HALF:(s + 1) * HALF], ps[:, g % 8, :], ACT.Identity,
                                           bias=vec[:, 8 + m:9 + m]).then_inc(qk_sb, 1)
                    for i_ in range(U + 7):
                        if 6 <= i_ <= U + 4 and i_ % 2 == 0:
                            b = (i_ - 6) // 2
                            h = b // NB
                            act.wait_ge(av_ps, b + 1)
                            if b >= 1:
                                act.wait_ge(fold_add, b)
                            act.activation(fold_t[own_half(h), :], ps[other_half(h), 6 + b % 2, 0:256], ACT.Copy)\
                                .then_inc(fold_cp, 1)
                            if b >= 2:
                                act.wait_ge(att_ok, b - 1)
                            act.activation(fold_r[own_half(h), b % 2, :], ps[own_half(h), 6 + b % 2, 256:512], ACT.Copy)\
                                .then_inc(fold_cp, 1)
                        if 2 <= i_ < U + 2:
                            u = i_ - 2
                            b = u // 2
                            for g in range(2):
                                n = 2 * u + g
                                act.wait_ge(tr_ps, n + 1)
                                if b >= 2:
                                    act.wait_ge(av_ps, b - 1)
                                act.activation(ph[:, b % 2, 4 * g:4 * g + 4, (u % 2) * P:(u % 2 + 1) * P],
                                               ps[:, 4 + n % 2, :].rearrange("p (k q) -> p k q", k=4),
                                               ACT.Copy).then_inc(ph_ok, 1)
                        if i_ < U:
                            act.wait_ge(max_ok, i_ + 1)
                            if i_ >= 2:
                                act.wait_ge(tr_ps, 2 * i_ - 2)
                            act.activation(prob[:, i_ % 2, :], ps[:, 2 * (i_ % 2):2 * (i_ % 2) + 2, :]
                                           .rearrange("p a b -> p (a b)"), ACT.Exp,
                                           bias=neg_max[:, i_:i_ + 1], accum_out=row_sum[:, i_:i_ + 1]).then_inc(exp_ok, 1)
                    act.wait_ge(av_ps, U // 2)
                    for s in range(2):
                        n = slice(s * HALF, (s + 1) * HALF)
                        for c in range(CT):
                            act.wait_ge(att_ok, 2 * NB * (c + 1))
                            act.activation(ah[:, c, n], qk[:, c, n], ACT.Copy).then_inc(ah_ok, 1)
                    if after is not None:
                        for t in range(TT):
                            act.wait_ge(xt_ps, t + 1)
                            keep_tile(act, t).then_inc(xt_sb, 1)
                        for c in range(CT):
                            act.wait_ge(xn_ok, c + 1)
                            high(act, c).then_inc(xh_ok, 1)

                @block.vector
                def _(dve):
                    steps = [0]

                    def link(ins):
                        steps[0] += 1
                        ins.then_inc(chain, 1)
                        dve.wait_ge(chain, steps[0])

                    for g, (kind, m, s) in enumerate(groups):
                        if kind == "v":
                            dve.wait_ge(vh_ok, m + 1)
                            dve.tensor_tensor(v_lo(v[:, m, :]), by_head(ps[:, g % 8, :]), raw(v_hi(v[:, m, :])),
                                              ALU.subtract).then_inc(vl_ok, 1)
                    for i_ in range(U + 7):
                        if i_ < U:
                            dve.wait_ge(score, i_ + 1)
                            dve.tensor_reduce(neg_max[:, i_:i_ + 1], ps[:, 2 * (i_ % 2):2 * (i_ % 2) + 2, :]
                                              .rearrange("p a b -> p (a b)"), AX, ALU.max, negate=True).then_inc(max_ok, 1)
                        if 6 <= i_ <= U + 4 and i_ % 2 == 0:
                            b = (i_ - 6) // 2
                            h = b // NB
                            dve.wait_ge(fold_cp, 2 * b + 2)
                            if b >= 2:
                                dve.wait_ge(att_ok, b - 1)
                            dve.tensor_tensor(fold_s[own_half(h), b % 2, :], ps[own_half(h), 6 + b % 2, 0:256],
                                              fold_t[own_half(h), :], ALU.add).then_inc(fold_add, 1)
                        if 2 <= i_ < U + 2:
                            u = i_ - 2
                            b = u // 2
                            for g in range(2):
                                n = 2 * u + g
                                here = (slice(None), b % 2, slice(4 * g, 4 * g + 4), slice((u % 2) * P, (u % 2 + 1) * P))
                                dve.wait_ge(ph_ok, n + 1)
                                dve.tensor_tensor(pl[here], ps[:, 4 + n % 2, :].rearrange("p (k q) -> p k q", k=4),
                                                  raw(ph[here]), ALU.subtract).then_inc(pl_ok, 1)
                            if u % 2 == 1:
                                dve.wait_ge(exp_ok, u + 1)
                                dve.reciprocal(row_inv[:, u - 1:u + 1], row_sum[:, u - 1:u + 1]).then_inc(inv_ok, 1)
                    for s in range(2):
                        n = slice(s * HALF, (s + 1) * HALF)
                        for c in range(CT):
                            dve.wait_ge(ah_ok, CT * s + c + 1)
                            dve.tensor_tensor(al[:, c, n], qk[:, c, n], raw(ah[:, c, n]), ALU.subtract)\
                               .then_inc(al_ok, 1)
                    for t in range(TT):
                        if after is not None:
                            if t == 0:
                                for s in range(2):
                                    dve.wait_ge(xt_sb, 4 * s + 4)
                                    stats(dve, s)
                                moments(dve, link)
                            if t == 1:
                                variance(dve, link)
                            if t == 2:
                                affine(dve, link)
                            if t in (2, 3):
                                for c in (2 * t - 4, 2 * t - 3):
                                    normalise(dve, c).then_inc(xn_ok, 1)
                            if t >= 4:
                                c = t - 4
                                dve.wait_ge(xh_ok, c + 1)
                                low(dve, c).then_inc(xl_ok, 1)
                        dve.wait_ge(out_ps, t + 1)
                        dve.wait_ge(res_ok, t + 1)
                        dve.tensor_tensor(tok[:, t, :], ps[:, 4 + t % 4, :], tok[:, t, :], ALU.add).then_inc(out_ok, 1)

                @block.gpsimd
                def _(pool):
                    def stage(h, parts):
                        j, n = h % 2, STAGE * h
                        hi = kh[:, j, :]
                        if 0 in parts:
                            pool.wait_ge(s_ld[j], 64 * (h // 2 + 1))
                            pool.tensor_scalar(hi, raw(qs[:, j, :]), 1.0, 0.0, ALU.mult, ALU.add).then_inc(staged, 1)
                            pool.wait_ge(staged, n + 1)
                            pool.tensor_tensor(qs[HD:P, j, :], raw(qs[HD:P, j, :]), raw(hi[HD:P, :]), ALU.subtract)\
                                .then_inc(staged, 1)
                            pool.wait_ge(staged, n + 2)
                        if 1 in parts:
                            pool.tensor_scalar(qs[0:HD, j, :], raw(hi[0:HD, :]), 1.0, 0.0, ALU.mult, ALU.add)\
                                .then_inc(staged, 1)
                            pool.wait_ge(staged, n + 3)
                            pool.tensor_scalar(hi, raw(kl[:, j, :]), 1.0, 0.0, ALU.mult, ALU.add).then_inc(staged, 1)
                            pool.wait_ge(staged, n + 4)
                        if 2 in parts:
                            pool.tensor_tensor(kl[:, j, :], raw(kl[:, j, :]), raw(hi), ALU.subtract).then_inc(staged, 1)
                            pool.wait_ge(staged, n + 5)

                    stage(0, (0, 1, 2))
                    stage(1, (0, 1, 2))
                    for b in range(U // 2):
                        h = b // NB
                        pool.wait_ge(fold_add, b + 1)
                        pool.wait_ge(fold_cp, 2 * b + 2)
                        pool.tensor_tensor(qk[own_half(h), h // 2, (b % NB) * 256:(b % NB + 1) * 256],
                                           fold_s[own_half(h), b % 2, :], fold_r[own_half(h), b % 2, :],
                                           ALU.mult).then_inc(att_ok, 1)
                        pool.wait_ge(att_ok, b + 1)
                        k, part = (b + 2) // NB, (b + 2) % NB
                        if 1 <= k <= NH - 2 and part < 3:
                            stage(k + 1, (part,))
                    for t in range(TT):
                        pool.wait_ge(r_ld[t], 16)
                        pool.tensor_tensor(tok[:, t, :], tok[:, t, :], bout[:], ALU.add).then_inc(res_ok, 1)
                        if after is not None and t == POWER_AT:
                            pool.wait_ge(res_ok, t + 1)
                            pool.wait_ge(var_ok, 1)
                            pool.tensor_tensor(small[:, 32:36], small[:, 28:32], neg_half[:], ALU.pow)\
                                .then_inc(rstd_ok, 1)
                            pool.wait_ge(rstd_ok, 1)

        if n_images > 1:
            with nc.Fori(0, n_images - 1) as i:
                image(i, x[1:])
                nc.all_engine_barrier(sems_to_clear=range(min(nums), max(nums) + 1))
        image(n_images - 1)
        first_nums = [s.num for s in (*wq_ld, wo_ld, wql_ok, ld, cst, spl, pe_s, chn)]
        assert max(first_nums) + 1 == min(nums) and len(first_nums) == min(nums) - min(first_nums)
        nc.all_engine_barrier(sems_to_clear=range(min(first_nums), max(nums) + 1))


def layer1(nc, x2, ln_g, ln_b, wq, bq, wv, bv, dw_w, dw_b, pw_w, mq_w, mq_b, mk_w, mk_b, mv_w, mv_b,
           mo_w, mo_b, mlp_w, mlp_b, out, n_images=B):
    NK = NS
    KT = NK // P
    QG = 4
    GR = TT // QG
    U = NH * GR
    SLOTS = 4
    DIAGS = 16
    DVE_TAPS = [29, 29, 28, 28]
    SOLO = 20
    left = [[(c, n) for n in range(DVE_TAPS[c])] + [(c, None)] for c in range(CT)]
    taps = [left[0].pop(0) for _ in range(SOLO)]
    while any(left):
        for l in [l for l in left if l][:4]:
            taps.append(l.pop(0))
    tap_before = [max([m + 1 for m in range(k) if taps[m][0] == taps[k][0]], default=0) for k in range(len(taps))]
    taps_upto = [taps.index((c, None)) + 1 for c in range(CT)]
    pe_taps = [(c, n) for c in range(CT) for n in range(DVE_TAPS[c], KS * KS)]
    pe_upto = [sum(e[0] <= c for e in pe_taps) for c in range(CT)]

    with ExitStack() as ctx:
        def sem(name):
            return ctx.enter_context(nc.semaphore("b_" + name))

        ps = ctx.enter_context(nc.psum_tensor("b_ps", [P, 8, 512], F32))
        R = Region(nc, SB_START, SB_END)
        names = ("wq", "wqm", "wvk", "wvv", "mo", "mlp")
        wh = {n: R.take(f"b_{n}_hi", [P, CT, C], F32R) for n in names}
        wl = {n: R.take(f"b_{n}_lo", [P, CT, C], F32R) for n in names}
        ident = R.take("b_ident", [P, P])
        lng = R.take("b_lng", [P, C])
        lnb = R.take("b_lnb", [P, C])
        bqw = R.take("b_bqw", [P, C])
        bmo = R.take("b_bmo", [P, C])
        bmlp = R.take("b_bmlp", [P, C])
        refs = R.take("b_refs", [P, 2, NS])
        vec = R.take("b_vec", [P, 40])
        dww = R.take("b_dww", [P, CT, KS * KS])
        bqm = R.take("b_bqm", [P, CT])
        bkm = R.take("b_bkm", [P, CT])
        bvm = R.take("b_bvm", [P, CT])
        neg_x = R.take("b_neg_x", [P, 1])
        neg_y = R.take("b_neg_y", [P, TT])
        neg_half = R.take("b_neg_half", [P, CT])
        bn = R.take("b_bn", [P, TT, 6])
        mv = R.take("b_mv", [P, TT, 2])
        rstd = R.take("b_rstd", [P, TT])
        nbn = R.take("b_nbn", [P, TT, 6])
        zmv = R.take("b_zmv", [P, TT, 2])
        zrs = R.take("b_zrs", [P, TT])
        neg_max = R.take("b_neg_max", [P, U * QG])
        row_sum = R.take("b_row_sum", [P, U * QG])
        row_inv = R.take("b_row_inv", [P, U * QG])
        x_at = R.at
        xs = R.take("b_xs", [P, TT, C])
        q_at = R.at
        qh = R.take("b_qh", [P, CT, TOK], F32R)
        ql = R.take("b_ql", [P, CT, TOK], F32R)
        l_at = R.at
        xh, xl, ln = [], [], []
        for s in range(2):
            xh.append(R.take(f"b_xh{s}", [P, CT, C], F32R))
            ln.append(Region(nc, R.at, SB_END).take(f"b_ln{s}", [P, CT, C]))
            xl.append(R.take(f"b_xl{s}", [P, CT, C], F32R))
        t_at = R.at
        assert t_at + 16384 <= SB_END
        qpad = Region(nc, q_at, l_at).take("b_qpad", [P, CT, PADW * PADW])
        E = Region(nc, t_at, SB_END)
        acc = E.take("b_acc", [P, CT, NS])
        o = E.take("b_o", [P, CT, NS])
        diag = E.take("b_diag", [P, DIAGS, P])
        E = Region(nc, t_at, SB_END)
        ith = E.take("b_it_hi", [P, KT, 2, NK], F32R)
        itl = E.take("b_it_lo", [P, KT, 2, NK], F32R)
        hat = E.take("b_hat", [P, TT, NS])
        E = Region(nc, t_at, SB_END)
        xy = E.take("b_xy", [P, 2, NS])
        hx = E.take("b_hx", [P, NS])
        E = Region(nc, x_at, q_at)
        kch = E.take("b_kc_hi", [P, CT, NK], F32R)
        kcl = E.take("b_kc_lo", [P, CT, NK], F32R)
        vh = E.take("b_v_hi", [P, KT, C], F32R)
        vl = E.take("b_v_lo", [P, KT, C], F32R)
        E = Region(nc, l_at, t_at)
        kh = E.take("b_kh", [P, SLOTS, NK], F32R)
        kl = E.take("b_kl", [P, SLOTS, NK], F32R)
        prob = E.take("b_prob", [P, 2, QG, NK])
        qs = E.take("b_qs", [P, SLOTS, TOK], F32R)
        E = Region(nc, t_at, SB_END)
        ph = E.take("b_ph", [P, 2, KT, 512], F32R)
        pl = E.take("b_pl", [P, 2, KT, 512], F32R)
        z = Region(nc, l_at + 16384, t_at).take("b_z", [P, TT, C])
        E = Region(nc, t_at, SB_END)
        zn = E.take("b_zn", [P, 2, C])
        zh = E.take("b_zh", [P, 2, CT, P], F32R)
        zl = E.take("b_zl", [P, 2, CT, P], F32R)
        ot = E.take("b_ot", [P, 2, C])
        W = Region(nc, q_at, SB_END)
        raws = {n: W.take(f"b_{n}_raw", [P, CT, C]) for n in ("mq", "mk", "mv", "mo", "wq", "wv", "mlp")}
        wqt = W.take("b_wq_t", [P, CT, C])
        wvt = W.take("b_wv_t", [P, CT, C])
        rows = W.take("b_rows", [40, P])
        wide = W.take("b_wide", [P, 2, CT, P])
        bo_raw = W.take("b_bo_raw", [P, C])
        bm_raw = W.take("b_bm_raw", [P, C])
        assert W.at <= SB_END

        x_ld = [sem(f"x_ld{t}") for t in range(TT)]
        z_ld = [sem(f"z_ld{t}") for t in range(TT)]
        s_ld = [sem(f"s_ld{j}") for j in range(SLOTS)]
        o_st = [sem(f"o_st{j}") for j in range(2)]
        (bn_ok, bn_ag, var_ok, rstd_ok, ln1, ln_ok, xh_ok, xl_ok, pad_ok, q_ps, q_sb, dg_ok, dg_used, tap,
         gelu_ok, qh_ps, qh_sb, ql_sb, off_ps, tanh_ok, xy_ok, hx_ok, hy_ok, hat_ok, it_ps, ih_ok, il_ok, k_ps, k_sb,
         kl_sb, v_ps, vh_ok, vl_ok, score, max_ok, exp_ok, inv_ok, sc_ok, tr_ps, ph_ok, pl_ok, av_ps, ah_ok, al_ok,
         mo_ps, z1_ok, z_ok, zvar, zrstd, zn_ok, zt_ps, zh_ok, zl_ok, ml_ps, y_ok, ge_ok, out_ok, chain) = singles = [
            sem(n) for n in (
                "bn_ok bn_ag var_ok rstd_ok ln1 ln_ok xh_ok xl_ok pad_ok q_ps q_sb dg_ok dg_used tap "
                "gelu_ok qh_ps qh_sb ql_sb off_ps tanh_ok xy_ok hx_ok hy_ok hat_ok it_ps ih_ok il_ok k_ps k_sb "
                "kl_sb v_ps vh_ok vl_ok score max_ok exp_ok inv_ok sc_ok tr_ps ph_ok pl_ok av_ps ah_ok al_ok "
                "mo_ps z1_ok z_ok zvar zrstd zn_ok zt_ps zh_ok zl_ok ml_ps y_ok ge_ok out_ok chain").split()]
        nums = [s.num for s in [*x_ld, *z_ld, *s_ld, *o_st, *singles]]
        assert sorted(nums) == list(range(min(nums), max(nums) + 1))

        ld, cst, hi_ok, lo_ok, pe_s, chn = (sem("s_" + n) for n in ("ld", "cst", "hi", "lo", "pe", "chn"))
        wt_sb, mlp_hi = sem("s_wt"), sem("s_mlp_hi")
        mo_hi, w_ld = sem("s_mo_hi"), {n: sem("s_" + n) for n in raws}
        N_LD = 15

        def centre(dve, t):
            return dve.scalar_tensor_tensor(ln[t // 4][:, t % 4, :], xs[:, t, :], mv[:, t, 0:1], lng[:],
                                            ALU.subtract, ALU.mult)

        def scale(dve, t):
            here = ln[t // 4][:, t % 4, :]
            return dve.scalar_tensor_tensor(here, here, rstd[:, t:t + 1], lnb[:], ALU.mult, ALU.add)

        def high(act, t):
            return act.activation(xh[t // 4][:, t % 4, :], ln[t // 4][:, t % 4, :], ACT.Copy)

        def low(dve, t):
            return dve.tensor_tensor(xl[t // 4][:, t % 4, :], ln[t // 4][:, t % 4, :], raw(xh[t // 4][:, t % 4, :]),
                                     ALU.subtract)

        def three(pe, bank, left, right, first, last):
            (lh, ll), (rh, rl) = left, right
            for e, (a, b) in enumerate(((lh, rh), (lh, rl), (ll, rh))):
                mm = pe.matmul(bank, a, b, start=first and e == 0, stop=last and e == 2)
            return mm

        def project(pe, s, c, k):
            n = slice(c * P, (c + 1) * P)
            return three(pe, ps[:, 4 * s + c, :], (xh[s][:, k, n], xl[s][:, k, n]),
                         (wh["wq"][:, k, :], wl["wq"][:, k, :]), k == 0, k == CT - 1)

        EARLY = 2

        with nc.Block() as block:
            @block.sync
            def _(sp):
                for n, w in (("wq", wq), ("wv", wv)):
                    sp.dma_start(raws[n][:], w.rearrange("(t p) n -> p t n", p=P)).then_inc(w_ld[n], 16)
                for n, vv in enumerate((bq, bv, mq_b, mk_b, mv_b)):
                    sp.dma_start(rows[4 * n:4 * n + 4, :], vv.rearrange("(t p) -> t p", p=P)).then_inc(ld, 16)
                sp.dma_start(rows[20:28, :], pw_w.rearrange("k (t p) -> (k t) p", p=P)).then_inc(ld, 16)
                sp.dma_start(rows[28:32, :], dw_b.rearrange("(t p) -> t p", p=P)).then_inc(ld, 16)
                sp.dma_start(rows[32:36, :], ln_g.rearrange("(t p) -> t p", p=P)).then_inc(ld, 16)
                sp.dma_start(rows[36:40, :], ln_b.rearrange("(t p) -> t p", p=P)).then_inc(ld, 16)
                sp.dma_start(dww[:], dw_w.rearrange("(t p) k -> p t k", p=P)).then_inc(ld, 16)
                for d, s in ((lng, ln_g), (lnb, ln_b), (bqw, bq), (bo_raw, mo_b), (bm_raw, mlp_b)):
                    sp.dma_start(d[:], s.partition_broadcast(P)).then_inc(ld, 16)
                for n, w in (("mq", mq_w), ("mk", mk_w), ("mv", mv_w)):
                    sp.dma_start(raws[n][:], w.rearrange("(t p) n -> p t n", p=P)).then_inc(w_ld[n], 16)
                for t in range(TT):
                    sp.dma_start(xs[:, t, :], x2[0, t * P:(t + 1) * P, :]).then_inc(x_ld[t], 16)
                for n, w in (("mo", mo_w), ("mlp", mlp_w)):
                    sp.dma_start(raws[n][:], w.rearrange("(t p) n -> p t n", p=P)).then_inc(w_ld[n], 16)
                sp.wait_ge(ld, N_LD * 16)

            @block.gpsimd
            def _(pool):
                make_identity(pool, ident, cst)
                pool.memset(neg_half[:], -0.5).then_inc(cst, 1)
                for g in range(4):
                    here = slice(32 * g, 32 * g + 32)
                    pool.wait_ge(cst, 3 + 2 * g)
                    pool.iota(neg_x[here, :], [[0, 1]], base=0, channel_multiplier=-1,
                              allow_small_or_imprecise_dtypes=True).then_inc(cst, 1)
                    pool.iota(neg_y[here, :], [[-4, TT]], base=-g, channel_multiplier=0,
                              allow_small_or_imprecise_dtypes=True).then_inc(cst, 1)
                pool.wait_ge(cst, 11)
                pool.iota(refs[:, 0, :], [[1, GRID], [0, GRID]], base=0, channel_multiplier=0,
                          allow_small_or_imprecise_dtypes=True).then_inc(cst, 1)
                pool.wait_ge(cst, 12)
                pool.iota(refs[:, 1, :], [[0, GRID], [1, GRID]], base=0, channel_multiplier=0,
                          allow_small_or_imprecise_dtypes=True).then_inc(cst, 1)
                pool.wait_ge(cst, 13)
                for s in range(2):
                    here = slice(4 * s, 4 * s + 4)
                    pool.wait_ge(var_ok, s + 1)
                    pool.tensor_tensor(rstd[:, here], rstd[:, here], neg_half[:], ALU.pow).then_inc(rstd_ok, 1)
                    pool.wait_ge(rstd_ok, s + 1)

            products = (("wqm", wqt, "mq"), ("wvk", wvt, "mk"), ("wvv", wvt, "mv"))

            @block.scalar
            def _(act):
                act.wait_ge(w_ld["wq"], 16)
                act.activation(wh["wq"][:], raws["wq"][:], ACT.Copy).then_inc(hi_ok, 1)
                for t in range(4):
                    act.wait_ge(ln_ok, t + 1)
                    high(act, t).then_inc(xh_ok, 1)
                for g in range(12):
                    n, j = products[g // 4][0], g % 4
                    act.wait_ge(pe_s, 9 + g + 1)
                    act.activation(wh[n][:, j, :], ps[:, g % 8, :], ACT.Copy).then_inc(hi_ok, 1)
                    if g == 3:
                        act.wait_ge(w_ld["mo"], 16)
                        act.activation(wh["mo"][:], raws["mo"][:], ACT.Copy).then_inc(mo_hi, 1)
                        act.wait_ge(w_ld["mlp"], 16)
                        act.wait_ge(chn, 1)
                        for k in range(CT):
                            act.activation(wh["mlp"][:, k, :], raws["mlp"][:, k, :], ACT.Copy,
                                           scale=vec[:, 32 + k:33 + k]).then_inc(mlp_hi, 1)

            @block.tensor
            def _(pe):
                pe.wait_ge(cst, 2)
                for w, n in enumerate(("wq", "wv")):
                    pe.wait_ge(w_ld[n], 16)
                    for k in range(CT):
                        for j in range(CT):
                            mm = pe.transpose(ps[:, 4 * w + k, j * P:(j + 1) * P],
                                              raws[n][:, j, k * P:(k + 1) * P], ident[:])
                        mm.then_inc(pe_s, 1)
                pe.wait_ge(wt_sb, 8)
                pe.wait_ge(ld, N_LD * 16)
                pe.transpose(ps[:, 0, 0:40], rows[:], ident[0:40, 0:40]).then_inc(pe_s, 1)
                for g in range(12):
                    n, wt, m = products[g // 4]
                    j = g % 4
                    pe.wait_ge(chn, 1)
                    pe.wait_ge(w_ld[m], 16)
                    if g >= 8:
                        pe.wait_ge(lo_ok, g - 7)
                    for k in range(CT):
                        mm = pe.matmul(ps[:, g % 8, :], wt[:, k, j * P:(j + 1) * P], raws[m][:, k, :],
                                       start=k == 0, stop=k == CT - 1)
                    mm.then_inc(pe_s, 1)
                pe.wait_ge(lo_ok, 10)
                pe.wait_ge(wt_sb, 9)
                pe.wait_ge(xh_ok, 4)
                pe.wait_ge(xl_ok, 4)
                for c in range(EARLY):
                    for k in range(CT):
                        project(pe, 0, c, k)
                pe.wait_ge(lo_ok, 12)
                for g, (at, m) in enumerate(((0, "mq"), (4, "mk"), (4, "mv"))):
                    for j in range(CT):
                        for k in range(CT):
                            mm = pe.matmul(ps[:, 5, 4 * g + j:4 * g + j + 1], raws[m][:, k, j * P:(j + 1) * P],
                                           vec[:, at + k:at + k + 1], start=k == 0, stop=k == CT - 1)
                mm.then_inc(pe_s, 1)
                pe.wait_ge(chn, 8)
                pe.wait_ge(w_ld["mo"], 16)
                pe.wait_ge(w_ld["mlp"], 16)
                for g, m in enumerate(("mo", "mlp")):
                    for k in range(CT):
                        mm = pe.matmul(ps[:, 6 + g, :], wide[:, g, k, :], raws[m][:, k, :], start=k == 0,
                                       stop=k == CT - 1)
                mm.then_inc(pe_s, 1)

            @block.vector
            def _(dve):
                for g in range(8):
                    dve.wait_ge(pe_s, g + 1)
                    dve.tensor_copy((wqt if g < 4 else wvt)[:, g % 4, :], ps[:, g, :]).then_inc(wt_sb, 1)
                dve.wait_ge(pe_s, 9)
                dve.tensor_copy(vec[:], ps[:, 0, 0:40]).then_inc(chn, 1)
                dve.wait_ge(hi_ok, 1)
                dve.tensor_tensor(wl["wq"][:], raws["wq"][:], raw(wh["wq"][:]), ALU.subtract).then_inc(wt_sb, 1)
                for s in range(2):
                    for t in range(4 * s, 4 * s + 4):
                        dve.wait_ge(x_ld[t], 16)
                        dve.bn_stats(bn[:, t, :], xs[:, t, :]).then_inc(bn_ok, 1)
                    for t in range(4 * s, 4 * s + 4):
                        dve.wait_ge(bn_ok, t + 1)
                        dve.bn_aggr(mv[:, t, :], bn[:, t, :]).then_inc(bn_ag, 1)
                    dve.wait_ge(bn_ag, 4 * s + 4)
                    dve.tensor_scalar(rstd[:, 4 * s:4 * s + 4], mv[:, 4 * s:4 * s + 4, 1], 1e-5, None, ALU.add)\
                       .then_inc(var_ok, 1)
                dve.wait_ge(wt_sb, 9)
                for t in range(4):
                    centre(dve, t).then_inc(ln1, 1)
                dve.wait_ge(rstd_ok, 1)
                for t in range(4):
                    dve.wait_ge(ln1, t + 1)
                    scale(dve, t).then_inc(ln_ok, 1)
                for t in range(4):
                    dve.wait_ge(xh_ok, t + 1)
                    low(dve, t).then_inc(xl_ok, 1)
                for g in range(12):
                    n, j = products[g // 4][0], g % 4
                    dve.wait_ge(hi_ok, 1 + g + 1)
                    dve.tensor_tensor(wl[n][:, j, :], ps[:, g % 8, :], raw(wh[n][:, j, :]), ALU.subtract)\
                       .then_inc(lo_ok, 1)
                    if g == 3:
                        dve.wait_ge(mo_hi, 1)
                        dve.tensor_tensor(wl["mo"][:], raws["mo"][:], raw(wh["mo"][:]), ALU.subtract).then_inc(wt_sb, 1)
                        for k in range(CT):
                            dve.wait_ge(mlp_hi, k + 1)
                            dve.scalar_tensor_tensor(wl["mlp"][:, k, :], raws["mlp"][:, k, :], vec[:, 32 + k:33 + k],
                                                     raw(wh["mlp"][:, k, :]), ALU.mult, ALU.subtract).then_inc(wt_sb, 1)
                dve.wait_ge(cst, 13)
                dve.tensor_scalar(refs[:], refs[:], 0.5, 2.0 / GRID, ALU.add, ALU.mult).then_inc(chn, 1)
                dve.wait_ge(chn, 2)
                dve.tensor_scalar(refs[:], refs[:], -1.0, None, ALU.add).then_inc(chn, 1)
                dve.wait_ge(pe_s, 22)
                for g, (dst, at) in enumerate(((bqm, 8), (bkm, 12), (bvm, 16))):
                    dve.tensor_tensor(dst[:], ps[:, 5, 4 * g:4 * g + 4], vec[:, at:at + 4], ALU.add).then_inc(chn, 1)
                dve.wait_ge(chn, 6)
                dve.tensor_copy(wide[:, 0], bvm[:].unsqueeze(2).to_broadcast([P, CT, P])).then_inc(chn, 1)
                dve.tensor_copy(wide[:, 1], vec[:, 36:40].unsqueeze(2).to_broadcast([P, CT, P])).then_inc(chn, 1)
                dve.wait_ge(pe_s, 23)
                dve.tensor_tensor(bmo[:], ps[:, 6, :], bo_raw[:], ALU.add).then_inc(chn, 1)
                dve.tensor_tensor(bmlp[:], ps[:, 7, :], bm_raw[:], ALU.add).then_inc(chn, 1)

        nc.all_engine_barrier(sems_to_clear=range(min(nums), max(nums) + 1))

        QH_BANK = (4, 5, 6, 0, 1, 2, 4, 5)
        IT_BANK = (7, 3)
        K_BANK = (6, 0, 1, 2)
        V_BANK = (7, 6)

        STATS_AT = {0: (0,), 1: (1, 2), 2: (3, 4), 7: (5,), 8: (6, 7)}
        POWER_AT = (2, 9)
        NORM_AT = 3

        def image(i, after=None):
            with nc.Block() as block:
                @block.sync
                def _(sp):
                    def q_copies(h):
                        j = h % SLOTS
                        sp.dma_start(raw(qs[0:HD, j, :]), raw(qh[own_half(h), h // 2, :])).then_inc(s_ld[j], 16)
                        sp.dma_start(raw(qs[HD:P, j, :]), raw(ql[own_half(h), h // 2, :])).then_inc(s_ld[j], 16)

                    def k_copies(h):
                        j = h % SLOTS
                        for half in range(2):
                            rows_ = slice(HD * half, HD * half + HD)
                            sp.dma_start(raw(kh[rows_, j, :]), raw(kch[own_half(h), h // 2, :])).then_inc(s_ld[j], 16)
                            sp.dma_start(raw(kl[rows_, j, :]), raw(kcl[own_half(h), h // 2, :])).then_inc(s_ld[j], 16)

                    sp.wait_ge(qh_ps, 2 * CT)
                    for h in range(SLOTS):
                        sp.wait_ge(qh_sb, 2 * (h // 2) + 2)
                        sp.wait_ge(ql_sb, 2 * (h // 2) + 2)
                        q_copies(h)
                    for h in range(SLOTS):
                        sp.wait_ge(k_sb, h // 2 + 1)
                        sp.wait_ge(kl_sb, h // 2 + 1)
                        k_copies(h)
                    sp.wait_ge(qh_sb, 2 * CT)
                    sp.wait_ge(ql_sb, 2 * CT)
                    sp.wait_ge(k_sb, CT)
                    sp.wait_ge(kl_sb, CT)
                    for h in range(SLOTS, NH):
                        sp.wait_ge(score, GR * (h - SLOTS + 1))
                        q_copies(h)
                        k_copies(h)
                    for t in range(TT):
                        sp.wait_ge(score, GR * (NH - SLOTS + t // 2 + 1))
                        sp.dma_start(z[:, t, :], x2[i, t * P:(t + 1) * P, :]).then_inc(z_ld[t], 16)
                    if after is not None:
                        sp.wait_ge(av_ps, U)
                        for t in range(TT):
                            sp.dma_start(xs[:, t, :], after[i, t * P:(t + 1) * P, :]).then_inc(x_ld[t], 16)
                    for t in range(TT):
                        sp.wait_ge(out_ok, t + 1)
                        sp.dma_start(out[i, t * P:(t + 1) * P, :], ot[:, t % 2, :]).then_inc(o_st[t % 2], 16)
                    for t in range(2):
                        sp.wait_ge(o_st[t], 16 * (TT // 2))

                @block.tensor
                def _(pe):
                    for s in range(2):
                        for c in range(EARLY if s == 0 else 0, CT):
                            for k in range(CT):
                                if s == 1 and c == 0:
                                    pe.wait_ge(xh_ok, k + 1)
                                    pe.wait_ge(xl_ok, k + 1)
                                mm = project(pe, s, c, k)
                            mm.then_inc(q_ps, 1)
                    for e, (c, n) in enumerate(pe_taps):
                        first, last = n == DVE_TAPS[c], n == KS * KS - 1
                        if first:
                            pe.wait_ge(q_sb, CT + c + 1)
                        pe.wait_ge(dg_ok, e + 1)
                        dy, dx = n // KS, n % KS
                        src = qpad[:, c, :].rearrange("p (y x) -> p y x", x=PADW)[
                            :, dy:dy + 2 * GRID - 1:2, dx:dx + 2 * GRID - 1:2]
                        mm = pe.matmul(ps[:, c, 0:NS], diag[:, e % DIAGS, :], src, start=first, stop=last)
                        mm.then_inc(dg_used, 1)

                    def queries(groups):
                        for g in groups:
                            if g >= 6:
                                pe.wait_ge(qh_sb, g - 5)
                                pe.wait_ge(ql_sb, g - 5)
                            m, s = g // 2, g % 2
                            n = slice(m * P, (m + 1) * P)
                            for k in range(CT):
                                mm = three(pe, ps[:, QH_BANK[g], :], (wh["wqm"][:, k, n], wl["wqm"][:, k, n]),
                                           (xh[s][:, k, :], xl[s][:, k, :]), k == 0, k == CT - 1)
                            mm.then_inc(qh_ps, 1)

                    pe.wait_ge(q_sb, 2 * CT)
                    queries(range(3))
                    for c in range(2):
                        for k in range(CT):
                            if c == 0:
                                pe.wait_ge(gelu_ok, k + 1)
                            mm = pe.matmul(ps[:, 7, c * NS:(c + 1) * NS],
                                           vec[:, 20 + 4 * c + k:21 + 4 * c + k].to_broadcast([P, P]), o[:, k, :],
                                           start=k == 0, stop=k == CT - 1)
                    mm.then_inc(off_ps, 1)
                    queries(range(3, 6))
                    pe.wait_ge(tanh_ok, 1)
                    for st in range(KT):
                        n = slice(st * P, (st + 1) * P)
                        for t in range(TT):
                            pe.wait_ge(hat_ok, t // 4 + 1)
                            mm = pe.matmul(ps[:, IT_BANK[st], :], hat[:, t, n], xs[:, t, :], start=t == 0, stop=t == TT - 1)
                        mm.then_inc(it_ps, 1)
                    queries(range(6, 8))
                    pe.wait_ge(ih_ok, KT)
                    pe.wait_ge(il_ok, KT)
                    for m in range(CT):
                        pe.wait_ge(qh_sb, m + 3)
                        pe.wait_ge(ql_sb, m + 3)
                        n = slice(m * P, (m + 1) * P)
                        for f in range(4):
                            e, st = f // 2, f % 2
                            mm = three(pe, ps[:, K_BANK[m], 0:NK], (wh["wvk"][:, f, n], wl["wvk"][:, f, n]),
                                       (ith[:, st, e, :], itl[:, st, e, :]), f == 0, f == 3)
                        mm.then_inc(k_ps, 1)
                    for r in range(KT):
                        if r == 1:
                            pe.wait_ge(k_sb, 1)
                            pe.wait_ge(kl_sb, 1)
                        n = slice(r * P, (r + 1) * P)
                        for f in range(4):
                            e, st = f // 2, f % 2
                            mm = three(pe, ps[:, V_BANK[r], :], (ith[:, st, e, n], itl[:, st, e, n]),
                                       (wh["wvv"][:, f, :], wl["wvv"][:, f, :]), f == 0, f == 3)
                        mm.then_inc(v_ps, 1)

                    pe.wait_ge(k_sb, CT)
                    pe.wait_ge(kl_sb, CT)
                    pe.wait_ge(qh_sb, 2 * CT)
                    pe.wait_ge(ql_sb, 2 * CT)

                    def output(u):
                        h = u // GR
                        if u == 0:
                            pe.wait_ge(vh_ok, KT)
                            pe.wait_ge(vl_ok, KT)
                        if u >= 2:
                            pe.wait_ge(ah_ok, u - 1)
                            pe.wait_ge(al_ok, u - 1)
                        pe.wait_ge(pl_ok, 2 * u + 2)
                        n = slice(h // 2 * P, h // 2 * P + P)
                        for kt in range(KT):
                            mm = three(pe, ps[:, 6 + u % 2, :], (vh[:, kt, n], vl[:, kt, n]),
                                       (ph[:, u % 2, kt, :], pl[:, u % 2, kt, :]), kt == 0, kt == KT - 1)
                        mm.then_inc(av_ps, 1)

                    def scores(u):
                        h, g = u // GR, u % GR
                        j = h % SLOTS
                        if g == 0:
                            pe.wait_ge(s_ld[j], 96 * (h // SLOTS + 1))
                        if u >= 2:
                            pe.wait_ge(exp_ok, QG * (u - 1))
                        for t in range(QG):
                            dst = ps[:, 2 * (u % 2) + t // 2, (t % 2) * NK:(t % 2 + 1) * NK]
                            q_ = qs[:, j, (QG * g + t) * P:(QG * g + t + 1) * P]
                            pe.matmul(dst, q_, kh[:, j, :], start=True, stop=False)
                            mm = pe.matmul(dst, q_, kl[:, j, :], start=False, stop=True)
                        mm.then_inc(score, 1)

                    def transposes(u):
                        pe.wait_ge(sc_ok, QG * (u + 1))
                        for kt in range(KT):
                            if u >= 1:
                                pe.wait_ge(pl_ok, 2 * u - 1 + kt)
                            for t in range(QG):
                                mm = pe.transpose(ps[:, 4 + kt, t * P:(t + 1) * P],
                                                  prob[:, u % 2, t, kt * P:(kt + 1) * P], ident[:])
                            mm.then_inc(tr_ps, 1)

                    for n in range(U + 4):
                        if n < U:
                            scores(n)
                        if n >= 4:
                            output(n - 4)
                        if 2 <= n < U + 2:
                            transposes(n - 2)

                    for t in range(TT + 2):
                        if t < TT:
                            if t >= 2:
                                pe.wait_ge(z1_ok, t - 1)
                            n = slice(t * P, (t + 1) * P)
                            for k in range(CT):
                                if t == 0:
                                    pe.wait_ge(ah_ok, 2 * GR * (k + 1))
                                    pe.wait_ge(al_ok, 2 * GR * (k + 1))
                                mm = three(pe, ps[:, t % 2, :], (qh[:, k, n], ql[:, k, n]),
                                           (wh["mo"][:, k, :], wl["mo"][:, k, :]), k == 0, k == CT - 1)
                            mm.then_inc(mo_ps, 1)
                        if 1 <= t <= TT:
                            u = t - 1
                            pe.wait_ge(zn_ok, u + 1)
                            if u >= 2:
                                pe.wait_ge(zl_ok, u - 1)
                            for k in range(CT):
                                mm = pe.transpose(ps[:, 2 + u % 2, k * P:(k + 1) * P], zn[:, u % 2, k * P:(k + 1) * P],
                                                  ident[:])
                            mm.then_inc(zt_ps, 1)
                        if t >= 2:
                            u = t - 2
                            pe.wait_ge(zl_ok, u + 1)
                            if u >= 2:
                                pe.wait_ge(y_ok, u - 1)
                            for k in range(CT):
                                mm = three(pe, ps[:, 4 + u % 2, :], (zh[:, u % 2, k, :], zl[:, u % 2, k, :]),
                                           (wh["mlp"][:, k, :], wl["mlp"][:, k, :]), k == 0, k == CT - 1)
                            mm.then_inc(ml_ps, 1)
                    if after is not None:
                        pe.wait_ge(z1_ok, TT)
                        pe.wait_ge(xh_ok, 8)
                        pe.wait_ge(xl_ok, 8)
                        for c in range(EARLY):
                            for k in range(CT):
                                project(pe, 0, c, k)

                @block.scalar
                def _(act):
                    def diagonal(e):
                        c, n = pe_taps[e]
                        act.activation(diag[:, e % DIAGS, :], ident[:], ACT.Copy, scale=dww[:, c, n:n + 1])\
                           .then_inc(dg_ok, 1)

                    for e in range(DIAGS):
                        diagonal(e)
                    for t in range(4):
                        act.wait_ge(ln_ok, t + 1)
                        high(act, 4 + t).then_inc(xh_ok, 1)
                    for e in range(DIAGS, len(pe_taps)):
                        act.wait_ge(dg_used, e - DIAGS + 1)
                        diagonal(e)
                    for c in range(CT):
                        act.wait_ge(tap, taps_upto[c])
                        act.activation(o[:, c, :], acc[:, c, :], ACT.Gelu).then_inc(gelu_ok, 1)

                    def query(g):
                        m, s = g // 2, g % 2
                        act.wait_ge(qh_ps, g + 1)
                        act.activation(qh[:, m, :].rearrange("p (c s) -> p s c", s=2)[:, s, :], ps[:, QH_BANK[g], :],
                                       ACT.Identity, bias=bqm[:, m:m + 1]).then_inc(qh_sb, 1)

                    act.wait_ge(tap, len(taps))
                    query(0)
                    act.wait_ge(off_ps, 1)
                    act.activation(xy[:].rearrange("p k n -> p (k n)"), ps[:, 7, :], ACT.Tanh).then_inc(tanh_ok, 1)
                    query(1)
                    act.wait_ge(xy_ok, 3)
                    act.activation(hx[:], xy[:, 1, :], ACT.Abs, bias=neg_x[:, 0:1]).then_inc(hx_ok, 1)
                    for t in range(TT):
                        act.activation(hat[:, t, :], xy[:, 0, :], ACT.Abs, bias=neg_y[:, t:t + 1]).then_inc(hy_ok, 1)
                        if t == 0:
                            act.wait_ge(hx_ok, 1)
                            act.activation(hx[:], hx[:], ACT.Relu, bias=1.0, scale=-1.0).then_inc(hx_ok, 1)
                        if t % 4 == 3:
                            half = hat[:, t - 3:t + 1, :]
                            act.wait_ge(hy_ok, t + 1 + t // 4)
                            act.activation(half, half, ACT.Relu, bias=1.0, scale=-1.0).then_inc(hy_ok, 1)
                    for g in range(2, 6):
                        query(g)
                    for st in range(KT):
                        act.wait_ge(it_ps, st + 1)
                        act.activation(ith[:, st, :, :], ps[:, IT_BANK[st], :].rearrange("p (r e) -> p e r", e=2),
                                       ACT.Copy).then_inc(ih_ok, 1)
                    for g in range(6, 8):
                        query(g)
                    for m in range(CT):
                        act.wait_ge(k_ps, m + 1)
                        act.activation(kch[:, m, :], ps[:, K_BANK[m], 0:NK], ACT.Identity, bias=bkm[:, m:m + 1])\
                            .then_inc(k_sb, 1)
                    for r in range(KT):
                        act.wait_ge(v_ps, r + 1)
                        act.activation(vh[:, r, :], ps[:, V_BANK[r], :], ACT.Copy).then_inc(vh_ok, 1)
                    def output(u):
                        h, g = u // GR, u % GR
                        act.wait_ge(av_ps, u + 1)
                        act.activation(qh[own_half(h), h // 2, g * 512:(g + 1) * 512],
                                       ps[own_half(h), 6 + u % 2, :], ACT.Copy).then_inc(ah_ok, 1)

                    def transposes(u):
                        for kt in range(KT):
                            n = KT * u + kt
                            act.wait_ge(tr_ps, n + 1)
                            if u >= 2:
                                act.wait_ge(av_ps, u - 1)
                            act.activation(ph[:, u % 2, kt, :], ps[:, 4 + kt, :], ACT.Copy).then_inc(ph_ok, 1)

                    def exponents(u):
                        act.wait_ge(max_ok, u + 1)
                        if u >= 2:
                            act.wait_ge(tr_ps, KT * (u - 1))
                        for t in range(QG):
                            c = QG * u + t
                            act.activation(prob[:, u % 2, t, :],
                                           ps[:, 2 * (u % 2) + t // 2, (t % 2) * NK:(t % 2 + 1) * NK], ACT.Exp,
                                           bias=neg_max[:, c:c + 1], accum_out=row_sum[:, c:c + 1]).then_inc(exp_ok, 1)

                    for n in range(U + 4):
                        if n >= 4:
                            output(n - 4)
                        if 2 <= n < U + 2:
                            transposes(n - 2)
                        if n < U:
                            exponents(n)
                    for t in range(1, TT + 2):
                        if t <= TT:
                            u = t - 1
                            act.wait_ge(zt_ps, u + 1)
                            if u >= 2:
                                act.wait_ge(ml_ps, u - 1)
                            act.activation(zh[:, u % 2, :, :], ps[:, 2 + u % 2, :].rearrange("p (k q) -> p k q", k=CT),
                                           ACT.Copy).then_inc(zh_ok, 1)
                        w = t - NORM_AT - 1
                        if after is not None and 0 <= w < 4:
                            act.wait_ge(ln_ok, w + 5)
                            high(act, w).then_inc(xh_ok, 1)
                        if t >= 2:
                            u = t - 2
                            act.wait_ge(y_ok, u + 1)
                            act.activation(ot[:, u % 2, :], ot[:, u % 2, :], ACT.Gelu).then_inc(ge_ok, 1)

                @block.vector
                def _(dve):
                    steps = [0]

                    def link(ins):
                        steps[0] += 1
                        ins.then_inc(chain, 1)
                        dve.wait_ge(chain, steps[0])

                    for t in range(4):
                        centre(dve, 4 + t).then_inc(ln1, 1)
                    for t in range(4):
                        dve.wait_ge(ln1, t + 1)
                        scale(dve, 4 + t).then_inc(ln_ok, 1)
                    for t in range(4):
                        dve.wait_ge(xh_ok, t + 1)
                        low(dve, 4 + t).then_inc(xl_ok, 1)
                    done = 0

                    def convolve(upto):
                        nonlocal done
                        while done < upto:
                            c, n = taps[done]
                            if tap_before[done]:
                                dve.wait_ge(tap, tap_before[done])
                            if n is None:
                                dve.wait_ge(dg_used, pe_upto[c])
                                dve.tensor_tensor(acc[:, c, :], ps[:, c, 0:NS], acc[:, c, :], ALU.add).then_inc(tap, 1)
                                done += 1
                                continue
                            if n == 0:
                                dve.wait_ge(q_sb, CT + c + 1)
                            dy, dx = n // KS, n % KS
                            src = qpad[:, c, :].rearrange("p (y x) -> p y x", x=PADW)[
                                :, dy:dy + 2 * GRID - 1:2, dx:dx + 2 * GRID - 1:2]
                            dst = acc[:, c, :].rearrange("p (y x) -> p y x", x=GRID)
                            if n == 0:
                                dve.tensor_scalar(dst, src, dww[:, c, n:n + 1], vec[:, 28 + c:29 + c], ALU.mult,
                                                  ALU.add).then_inc(tap, 1)
                            else:
                                dve.scalar_tensor_tensor(dst, src, dww[:, c, n:n + 1], dst, ALU.mult, ALU.add)\
                                   .then_inc(tap, 1)
                            done += 1

                    for g in range(2 * CT):
                        s, c = g // 4, g % 4
                        dve.wait_ge(pad_ok, c + 1)
                        if g >= EARLY:
                            dve.wait_ge(q_ps, g + 1 - EARLY)
                        inside = qpad[:, c, :].rearrange("p (y x) -> p y x", x=PADW)[
                            :, KS // 2 + 16 * s:KS // 2 + 16 * s + 16, KS // 2:KS // 2 + HW]
                        dve.tensor_tensor(inside, ps[:, g, :].rearrange("p (y x) -> p y x", x=HW),
                                          bqw[:].rearrange("p (y x) -> p y x", x=HW), ALU.add).then_inc(q_sb, 1)
                        if s == 1 and c < CT - 1:
                            convolve(SOLO * (c + 1) // (CT - 1))
                    convolve(len(taps))

                    def query(g):
                        m, s = g // 2, g % 2
                        here = (slice(None), m)
                        dve.wait_ge(qh_sb, g + 1)
                        dve.scalar_tensor_tensor(ql[here].rearrange("p (c s) -> p s c", s=2)[:, s, :],
                                                 ps[:, QH_BANK[g], :], bqm[:, m:m + 1],
                                                 raw(qh[here]).rearrange("p (c s) -> p s c", s=2)[:, s, :],
                                                 ALU.add, ALU.subtract).then_inc(ql_sb, 1)

                    query(0)
                    dve.wait_ge(tanh_ok, 1)
                    dve.tensor_tensor(xy[:], xy[:], refs[:], ALU.add).then_inc(xy_ok, 1)
                    dve.wait_ge(xy_ok, 1)
                    dve.tensor_scalar(xy[:], xy[:], 1.0, HW / 2 / 2.0, ALU.add, ALU.mult).then_inc(xy_ok, 1)
                    dve.wait_ge(xy_ok, 2)
                    dve.tensor_scalar(xy[:], xy[:], 1.0, 0.5 * (HW - 1), ALU.add, ALU.mult).then_inc(xy_ok, 1)
                    query(1)
                    for s in range(2):
                        dve.wait_ge(hx_ok, 2)
                        dve.wait_ge(hy_ok, 5 * s + 5)
                        half = hat[:, 4 * s:4 * s + 4, :]
                        dve.tensor_tensor(half, half, hx[:].unsqueeze(1).to_broadcast([P, 4, NS]), ALU.mult)\
                           .then_inc(hat_ok, 1)
                    for g in range(2, 6):
                        query(g)
                    for st in range(KT):
                        dve.wait_ge(ih_ok, st + 1)
                        dve.tensor_tensor(itl[:, st, :, :], ps[:, IT_BANK[st], :].rearrange("p (r e) -> p e r", e=2),
                                          raw(ith[:, st, :, :]), ALU.subtract).then_inc(il_ok, 1)
                    for g in range(6, 8):
                        query(g)
                    for m in range(CT):
                        dve.wait_ge(k_sb, m + 1)
                        dve.scalar_tensor_tensor(kcl[:, m, :], ps[:, K_BANK[m], 0:NK], bkm[:, m:m + 1],
                                                 raw(kch[:, m, :]), ALU.add, ALU.subtract).then_inc(kl_sb, 1)
                    for r in range(KT):
                        dve.wait_ge(vh_ok, r + 1)
                        dve.tensor_tensor(vl[:, r, :], ps[:, V_BANK[r], :], raw(vh[:, r, :]), ALU.subtract)\
                           .then_inc(vl_ok, 1)
                    def output(u):
                        h, g = u // GR, u % GR
                        here = (own_half(h), h // 2, slice(g * 512, (g + 1) * 512))
                        dve.wait_ge(ah_ok, u + 1)
                        dve.tensor_tensor(ql[here], ps[own_half(h), 6 + u % 2, :], raw(qh[here]), ALU.subtract)\
                           .then_inc(al_ok, 1)

                    def inverses(u):
                        dve.wait_ge(exp_ok, QG * (u + 1))
                        dve.reciprocal(row_inv[:, QG * u:QG * u + QG], row_sum[:, QG * u:QG * u + QG])\
                           .then_inc(inv_ok, 1)

                    def maxima(u):
                        dve.wait_ge(score, u + 1)
                        dve.tensor_reduce(neg_max[:, QG * u:QG * u + QG],
                                          ps[:, 2 * (u % 2):2 * (u % 2) + 2, :].rearrange("p a (b k) -> p (a b) k", b=2),
                                          AX, ALU.max, negate=True).then_inc(max_ok, 1)

                    def transposes(u):
                        for kt in range(KT):
                            dve.wait_ge(ph_ok, KT * u + kt + 1)
                            dve.tensor_tensor(pl[:, u % 2, kt, :], ps[:, 4 + kt, :], raw(ph[:, u % 2, kt, :]),
                                              ALU.subtract).then_inc(pl_ok, 1)

                    for n in range(U + 4):
                        if 1 <= n < U + 1:
                            inverses(n - 1)
                        if n < U:
                            maxima(n)
                        if n >= 4:
                            output(n - 4)
                        if 2 <= n < U + 2:
                            transposes(n - 2)
                    for t in range(TT + 2):
                        if t < TT:
                            dve.wait_ge(mo_ps, t + 1)
                            dve.wait_ge(z_ok, t + 1)
                            dve.tensor_tensor(z[:, t, :], ps[:, t % 2, :], z[:, t, :], ALU.add).then_inc(z1_ok, 1)
                            dve.wait_ge(z1_ok, t + 1)
                            link(dve.bn_stats(nbn[:, t, :], z[:, t, :]))
                            link(dve.bn_aggr(zmv[:, t, :], nbn[:, t, :]))
                            dve.tensor_scalar(zrs[:, t:t + 1], zmv[:, t, 1:2], 1e-5, None, ALU.add).then_inc(zvar, 1)
                        if 1 <= t <= TT:
                            u = t - 1
                            dve.wait_ge(zh_ok, u + 1)
                            dve.tensor_tensor(zl[:, u % 2, :, :], ps[:, 2 + u % 2, :].rearrange("p (k q) -> p k q", k=CT),
                                              raw(zh[:, u % 2, :, :]), ALU.subtract).then_inc(zl_ok, 1)
                        if t < TT:
                            if t >= 2:
                                dve.wait_ge(zt_ps, t - 1)
                            dve.wait_ge(zrstd, t + 1)
                            dve.tensor_scalar(zn[:, t % 2, :], z[:, t, :], zmv[:, t, 0:1], zrs[:, t:t + 1],
                                              ALU.subtract, ALU.mult).then_inc(zn_ok, 1)
                        if after is not None:
                            for w in STATS_AT.get(t, ()):
                                dve.wait_ge(x_ld[w], 16)
                                dve.bn_stats(bn[:, w, :], xs[:, w, :]).then_inc(bn_ok, 1)
                                dve.wait_ge(bn_ok, w + 1)
                                dve.bn_aggr(mv[:, w, :], bn[:, w, :]).then_inc(bn_ag, 1)
                                if w % 4 == 3:
                                    dve.wait_ge(bn_ag, w + 1)
                                    dve.tensor_scalar(rstd[:, w - 3:w + 1], mv[:, w - 3:w + 1, 1], 1e-5, None, ALU.add)\
                                       .then_inc(var_ok, 1)
                            w = t - NORM_AT - 1
                            if 0 <= w < 4:
                                dve.wait_ge(xh_ok, w + 5)
                                low(dve, w).then_inc(xl_ok, 1)
                            w = t - NORM_AT
                            if 0 <= w < 4:
                                centre(dve, w).then_inc(ln1, 1)
                                dve.wait_ge(ln1, w + 5)
                                dve.wait_ge(rstd_ok, 1)
                                scale(dve, w).then_inc(ln_ok, 1)
                        if t >= 2:
                            u = t - 2
                            dve.wait_ge(ml_ps, u + 1)
                            if u >= 2:
                                dve.wait_ge(o_st[u % 2], 16 * (u // 2))
                            dve.tensor_tensor(ot[:, u % 2, :], ps[:, 4 + u % 2, :], bmlp[:], ALU.add).then_inc(y_ok, 1)

                @block.gpsimd
                def _(pool):
                    for c in range(CT):
                        pool.memset(qpad[:, c, :], 0.0).then_inc(pad_ok, 1)
                        pool.wait_ge(pad_ok, c + 1)
                    for c in range(U * QG):
                        u, t = c // QG, c % QG
                        pool.wait_ge(inv_ok, u + 1)
                        pool.tensor_scalar(prob[:, u % 2, t, :], prob[:, u % 2, t, :], row_inv[:, c:c + 1], 0.0,
                                           ALU.mult, ALU.add).then_inc(sc_ok, 1)
                        pool.wait_ge(sc_ok, c + 1)
                    def residual(t):
                        pool.wait_ge(z_ld[t], 16)
                        pool.tensor_tensor(z[:, t, :], z[:, t, :], bmo[:], ALU.add).then_inc(z_ok, 1)
                        pool.wait_ge(z_ok, t + 1)

                    for t in range(4):
                        residual(t)
                    for t in range(TT + 2):
                        if t < TT:
                            pool.wait_ge(zvar, t + 1)
                            pool.tensor_tensor(zrs[:, t:t + 1], zrs[:, t:t + 1], neg_half[:, 0:1], ALU.pow)\
                                .then_inc(zrstd, 1)
                            pool.wait_ge(zrstd, t + 1)
                            if t + 4 < TT:
                                residual(t + 4)
                        if after is not None and t in POWER_AT:
                            s = POWER_AT.index(t)
                            here = slice(4 * s, 4 * s + 4)
                            pool.wait_ge(var_ok, s + 1)
                            pool.tensor_tensor(rstd[:, here], rstd[:, here], neg_half[:], ALU.pow).then_inc(rstd_ok, 1)
                            pool.wait_ge(rstd_ok, s + 1)
                        if t >= 2:
                            u = t - 2
                            pool.wait_ge(ge_ok, u + 1)
                            pool.tensor_tensor(ot[:, u % 2, :], ot[:, u % 2, :], z[:, u, :], ALU.add).then_inc(out_ok, 1)
                            pool.wait_ge(out_ok, u + 1)

        if n_images > 1:
            with nc.Fori(0, n_images - 1) as i:
                image(i, x2[1:])
                nc.all_engine_barrier(sems_to_clear=range(min(nums), max(nums) + 1))
        image(n_images - 1)


_INS = ["x", "L0_conv_gn_scale", "L0_conv_gn_bias", "L0_conv_w_qkv", "L0_conv_b_qkv", "L0_conv_w_out", "L0_conv_b_out",
        "L1_conv_ln_g", "L1_conv_ln_b", "L1_conv_wq", "L1_conv_bq", "L1_conv_wv", "L1_conv_bv", "L1_conv_dw_w",
        "L1_conv_dw_b", "L1_conv_pw_w", "L1_conv_mq_w", "L1_conv_mq_b", "L1_conv_mk_w", "L1_conv_mk_b",
        "L1_conv_mv_w", "L1_conv_mv_b", "L1_conv_mo_w", "L1_conv_mo_b", "L1_conv_mlp_w", "L1_conv_mlp_b"]


def build(nc, a, out, n_images=B):
    x2 = nc.dram_tensor("x2", [B, TOK, C], F32, kind="Internal").ap()
    l0 = [a["L0_conv_" + n] for n in ("gn_scale", "gn_bias", "w_qkv", "b_qkv", "w_out", "b_out")]
    layer0(nc, a["x"].rearrange("b h w c -> b (h w) c"), *l0, x2, n_images)
    l1 = {n: a["L1_conv_" + n] for n in ("ln_g", "ln_b", "wq", "bq", "wv", "bv", "dw_w", "dw_b", "pw_w", "mq_w", "mq_b",
                                         "mk_w", "mk_b", "mv_w", "mv_b", "mo_w", "mo_b", "mlp_w", "mlp_b")}
    l1["dw_w"] = l1["dw_w"].rearrange("c o y x -> c (o y x)")
    l1["pw_w"] = l1["pw_w"].rearrange("k c y x -> k (c y x)")
    layer1(nc, x2, *l1.values(), out.rearrange("b h w c -> b (h w) c"), n_images)


def kernel(**inputs):
    import numpy as _np
    import concourse.bacc as _bacc
    from concourse.bass_utils import run_bass_kernel_spmd as _run

    nc = _bacc.Bacc("TRN2", target_bir_lowering=False, num_devices=1)
    arrays, args = {}, {}
    for name in _INS:
        arr = _np.ascontiguousarray(inputs[name])
        arrays[f"in_{name}"] = arr
        args[name] = nc.dram_tensor(f"in_{name}", arr.shape, mybir.dt.from_np(arr.dtype), kind="ExternalInput").ap()
    out = nc.dram_tensor("out_0", (B, HW, HW, C), F32, kind="ExternalOutput").ap()
    build(nc, args, out)
    r = _run(nc, [arrays], core_ids=[0])
    return r.results[0]["out_0"]
```
